# Optimizing a Trainium2 kernel written in Bass

```python
import numpy as np
import jax
import jax.numpy as jnp

def _softmax(x, axis=-1):
    return jax.nn.softmax(x, axis=axis)

def _gelu(x):
    return jax.nn.gelu(x, approximate=True)

def _silu(x):
    return jax.nn.silu(x)

def _sigmoid(x):
    return jax.nn.sigmoid(x)

def _layernorm(x, axis=-1, eps=1e-05):
    m = jnp.mean(x, axis=axis, keepdims=True)
    v = jnp.var(x, axis=axis, keepdims=True)
    return (x - m) / jnp.sqrt(v + eps)

def _scatter_add(tgt, idx, src, axis=0):
    return tgt.at[idx].add(src)

def _segment_sum(src, seg, n):
    return jax.ops.segment_sum(src, seg, n)
kernel_name = 'mk_decoder_postln_d1_seqx_r2_c225e8'

def setup_inputs(seed: int=0):
    np.random.seed(seed)
    _w = jnp.asarray

    def _rec_inputs():
        import jax
        import jax.numpy as jnp
        _rk = jax.random.key(seed)
        x = -0.0002928 + 1 * jax.random.normal(jax.random.fold_in(_rk, 1), (2, 2048, 512), jnp.float32)
        _lenS = 2048 - jax.random.randint(jax.random.fold_in(_rk, 7), (2,), 0, max(1, 2048 // 4) + 1, jnp.int32)
        _lenS2 = 77 - jax.random.randint(jax.random.fold_in(_rk, 8), (2,), 0, max(1, 77 // 4) + 1, jnp.int32)
        _ctx_1024P = jax.random.normal(jax.random.fold_in(_rk, 11), (2, 16, 512), jnp.float32)
        _ctx_1024c = jax.random.dirichlet(jax.random.fold_in(_rk, 511), 0.3 * jnp.ones((16,), jnp.float32), (2, 77))
        _ctx_1024t = jnp.einsum('bsk,bkd->bsd', _ctx_1024c, _ctx_1024P)
        _ctx_1024t = _ctx_1024t * jax.lax.rsqrt(jnp.mean(jnp.square(_ctx_1024t)) + 1e-12) * 0.953939
        ctx_1024 = -1.39393e-06 + 0.999914 * (_ctx_1024t + 0.3 * jax.random.normal(jax.random.fold_in(_rk, 611), (2, 77, 512), jnp.float32))
        return (x, ctx_1024)
    x, ctx_1024 = _rec_inputs()

    def _L0_attn_setup():
        import jax, jax.numpy as jnp
        import numpy as np
        B, T, C = (8, 1024, 512)
        EPS_LN = 1e-05
        EPS_WKV = 1e-08

        def layer_norm(x, g, b):
            mu = jnp.mean(x, axis=-1, keepdims=True)
            var = jnp.var(x, axis=-1, keepdims=True)
            return (x - mu) * jax.lax.rsqrt(var + EPS_LN) * g + b

        def time_shift(x, ratio):
            x_prev = jnp.pad(x[:, :-1, :], ((0, 0), (1, 0), (0, 0)))
            return x * ratio + x_prev * (1.0 - ratio)

        def wkv(w, u, k, v):
            kT = jnp.swapaxes(k, 0, 1)
            vT = jnp.swapaxes(v, 0, 1)
            aa0 = jnp.zeros((k.shape[0], k.shape[2]), k.dtype)
            ninf = jnp.full_like(aa0, -jnp.inf)

            def step(carry, kv):
                aa, bb, pp = carry
                kk, vv = kv
                ww = u + kk
                p = jnp.maximum(pp, ww)
                e1 = jnp.exp(pp - p)
                e2 = jnp.exp(ww - p)
                out = (e1 * aa + e2 * vv) / (e1 + e2 + EPS_WKV)
                bb_new = w + pp
                p2 = jnp.maximum(pp, kk)
                e1b = jnp.exp(pp - p2)
                e2b = jnp.exp(kk - p2)
                aa_new = e1b * aa + e2b * vv
                pp_new = p2 + jnp.log(e1b + e2b + EPS_WKV)
                return ((aa_new, bb_new, pp_new), out)
            (aa, bb, pp), outT = jax.lax.scan(step, (aa0, ninf, ninf), (kT, vT))
            output = jnp.swapaxes(outT, 0, 1)
            final_state = jnp.stack([aa, bb, pp], axis=2)
            return (output, final_state)

        def _reference_tuple_inner(x, time_decay, time_first, Wk_t, Wv_t, Wr_t, Wk_c, Wv_c, Wr_c, ln1_g, ln1_b, ln2_g, ln2_b, mix_k, mix_v, mix_r, cmix_k, cmix_r):
            h = layer_norm(x, ln1_g, ln1_b)
            k = time_shift(h, mix_k) @ Wk_t.T
            v = time_shift(h, mix_v) @ Wv_t.T
            r = jax.nn.sigmoid(time_shift(h, mix_r) @ Wr_t.T)
            w = -jnp.exp(time_decay)
            wkv_out, new_state = wkv(w, time_first, k, v)
            x = x + r * wkv_out
            h2 = layer_norm(x, ln2_g, ln2_b)
            kc = time_shift(h2, cmix_k) @ Wk_c.T
            rc = jax.nn.sigmoid(time_shift(h2, cmix_r) @ Wr_c.T)
            vv = jnp.square(jax.nn.relu(kc)) @ Wv_c.T
            x = x + rc * vv
            return (x, new_state)
        key = jax.random.key(seed)
        ks = jax.random.split(key, 16)
        s = 1.0 / np.sqrt(C)
        inp = {'x': jax.random.normal(ks[0], (B, T, C), jnp.float32), 'time_decay': jax.random.normal(ks[1], (C,), jnp.float32), 'time_first': jax.random.normal(ks[2], (C,), jnp.float32), 'Wk_t': jax.random.normal(ks[3], (C, C), jnp.float32) * s, 'Wv_t': jax.random.normal(ks[4], (C, C), jnp.float32) * s, 'Wr_t': jax.random.normal(ks[5], (C, C), jnp.float32) * s, 'Wk_c': jax.random.normal(ks[6], (4 * C, C), jnp.float32) * s, 'Wv_c': jax.random.normal(ks[7], (C, 4 * C), jnp.float32) * (0.5 * s), 'Wr_c': jax.random.normal(ks[8], (C, C), jnp.float32) * s, 'ln1_g': jnp.ones((C,), jnp.float32), 'ln1_b': jnp.zeros((C,), jnp.float32), 'ln2_g': jnp.ones((C,), jnp.float32), 'ln2_b': jnp.zeros((C,), jnp.float32), 'mix_k': jnp.ones((C,), jnp.float32), 'mix_v': jnp.ones((C,), jnp.float32), 'mix_r': jnp.ones((C,), jnp.float32), 'cmix_k': jnp.ones((C,), jnp.float32), 'cmix_r': jnp.ones((C,), jnp.float32)}
        return inp
    _L0_attn_all = _L0_attn_setup()
    _L0_attn_in = {k: v for k, v in _L0_attn_all.items() if k in ('time_decay', 'time_first', 'Wk_t', 'Wv_t', 'Wr_t', 'Wk_c', 'Wv_c', 'Wr_c', 'ln1_g', 'ln1_b', 'ln2_g', 'ln2_b', 'mix_k', 'mix_v', 'mix_r', 'cmix_k', 'cmix_r')}
    del _L0_attn_all

    def _L0_xattn_setup():
        import jax, jax.numpy as jnp
        import numpy as np
        D_MODEL = 512
        NUM_HEADS = 16
        HEAD_DIM = D_MODEL // NUM_HEADS

        def _split_heads(x):
            B, N, _ = x.shape
            return x.reshape(B, N, NUM_HEADS, HEAD_DIM).transpose(0, 2, 1, 3)
        key = jax.random.key(seed)
        ks = jax.random.split(key, 11)
        B, N = (2, 1024)
        s = 1.0 / np.sqrt(D_MODEL)
        return {'query': jax.random.normal(ks[0], (B, N, D_MODEL), jnp.float32), 'key': jax.random.normal(ks[1], (B, N, D_MODEL), jnp.float32), 'value': jax.random.normal(ks[2], (B, N, D_MODEL), jnp.float32), 'Wq': jax.random.normal(ks[3], (D_MODEL, D_MODEL), jnp.float32) * s, 'bq': jax.random.normal(ks[4], (D_MODEL,), jnp.float32) * 0.01, 'Wk': jax.random.normal(ks[5], (D_MODEL, D_MODEL), jnp.float32) * s, 'bk': jax.random.normal(ks[6], (D_MODEL,), jnp.float32) * 0.01, 'Wv': jax.random.normal(ks[7], (D_MODEL, D_MODEL), jnp.float32) * s, 'bv': jax.random.normal(ks[8], (D_MODEL,), jnp.float32) * 0.01, 'Wo': jax.random.normal(ks[9], (D_MODEL, D_MODEL), jnp.float32) * s, 'bo': jax.random.normal(ks[10], (D_MODEL,), jnp.float32) * 0.01}
    _L0_xattn_all = _L0_xattn_setup()
    _L0_xattn_in = {k: v for k, v in _L0_xattn_all.items() if k in ('Wq', 'bq', 'Wk', 'bk', 'Wv', 'bv', 'Wo', 'bo')}
    del _L0_xattn_all

    def _L0_ffn_setup():
        import jax, jax.numpy as jnp
        import numpy as np
        NUM_GEMMS = 8
        HIDDEN = 512
        INTER = 2048
        key = jax.random.key(seed)
        k_x, k_w1, k_b1, k_w2, k_b2 = jax.random.split(key, 5)
        x = jax.random.normal(k_x, (8, 1024, HIDDEN), dtype=jnp.float32)
        s1 = 1.0 / np.sqrt(HIDDEN)
        s2 = 1.0 / np.sqrt(INTER)
        W1 = jax.random.uniform(k_w1, (NUM_GEMMS, INTER, HIDDEN), jnp.float32, -s1, s1)
        b1 = jax.random.uniform(k_b1, (NUM_GEMMS, INTER), jnp.float32, -s1, s1)
        W2 = jax.random.uniform(k_w2, (NUM_GEMMS, HIDDEN, INTER), jnp.float32, -s2, s2)
        b2 = jax.random.uniform(k_b2, (NUM_GEMMS, HIDDEN), jnp.float32, -s2, s2)
        return {'x': x, 'W1': W1, 'b1': b1, 'W2': W2, 'b2': b2}
    _L0_ffn_all = _L0_ffn_setup()
    _L0_ffn_in = {k: v for k, v in _L0_ffn_all.items() if k in ('W1', 'b1', 'W2', 'b2')}
    del _L0_ffn_all
    return {'x': x, 'ctx_1024': ctx_1024, 'L0_attn_time_decay': _L0_attn_in['time_decay'], 'L0_attn_time_first': _L0_attn_in['time_first'], 'L0_attn_Wk_t': _L0_attn_in['Wk_t'], 'L0_attn_Wv_t': _L0_attn_in['Wv_t'], 'L0_attn_Wr_t': _L0_attn_in['Wr_t'], 'L0_attn_Wk_c': _L0_attn_in['Wk_c'], 'L0_attn_Wv_c': _L0_attn_in['Wv_c'], 'L0_attn_Wr_c': _L0_attn_in['Wr_c'], 'L0_attn_ln1_g': _L0_attn_in['ln1_g'], 'L0_attn_ln1_b': _L0_attn_in['ln1_b'], 'L0_attn_ln2_g': _L0_attn_in['ln2_g'], 'L0_attn_ln2_b': _L0_attn_in['ln2_b'], 'L0_attn_mix_k': _L0_attn_in['mix_k'], 'L0_attn_mix_v': _L0_attn_in['mix_v'], 'L0_attn_mix_r': _L0_attn_in['mix_r'], 'L0_attn_cmix_k': _L0_attn_in['cmix_k'], 'L0_attn_cmix_r': _L0_attn_in['cmix_r'], 'L0_xattn_Wq': _L0_xattn_in['Wq'], 'L0_xattn_bq': _L0_xattn_in['bq'], 'L0_xattn_Wk': _L0_xattn_in['Wk'], 'L0_xattn_bk': _L0_xattn_in['bk'], 'L0_xattn_Wv': _L0_xattn_in['Wv'], 'L0_xattn_bv': _L0_xattn_in['bv'], 'L0_xattn_Wo': _L0_xattn_in['Wo'], 'L0_xattn_bo': _L0_xattn_in['bo'], 'L0_ffn_W1': _L0_ffn_in['W1'], 'L0_ffn_b1': _L0_ffn_in['b1'], 'L0_ffn_W2': _L0_ffn_in['W2'], 'L0_ffn_b2': _L0_ffn_in['b2']}

def reference(x, ctx_1024, L0_attn_time_decay, L0_attn_time_first, L0_attn_Wk_t, L0_attn_Wv_t, L0_attn_Wr_t, L0_attn_Wk_c, L0_attn_Wv_c, L0_attn_Wr_c, L0_attn_ln1_g, L0_attn_ln1_b, L0_attn_ln2_g, L0_attn_ln2_b, L0_attn_mix_k, L0_attn_mix_v, L0_attn_mix_r, L0_attn_cmix_k, L0_attn_cmix_r, L0_xattn_Wq, L0_xattn_bq, L0_xattn_Wk, L0_xattn_bk, L0_xattn_Wv, L0_xattn_bv, L0_xattn_Wo, L0_xattn_bo, L0_ffn_W1, L0_ffn_b1, L0_ffn_W2, L0_ffn_b2):
    import jax
    import jax.numpy as jnp

    def _L0_attn_ref(x, time_decay, time_first, Wk_t, Wv_t, Wr_t, Wk_c, Wv_c, Wr_c, ln1_g, ln1_b, ln2_g, ln2_b, mix_k, mix_v, mix_r, cmix_k, cmix_r):
        import jax, jax.numpy as jnp
        import numpy as np
        B, T, C = (8, 1024, 512)
        EPS_LN = 1e-05
        EPS_WKV = 1e-08

        def layer_norm(x, g, b):
            mu = jnp.mean(x, axis=-1, keepdims=True)
            var = jnp.var(x, axis=-1, keepdims=True)
            return (x - mu) * jax.lax.rsqrt(var + EPS_LN) * g + b

        def time_shift(x, ratio):
            x_prev = jnp.pad(x[:, :-1, :], ((0, 0), (1, 0), (0, 0)))
            return x * ratio + x_prev * (1.0 - ratio)

        def wkv(w, u, k, v):
            kT = jnp.swapaxes(k, 0, 1)
            vT = jnp.swapaxes(v, 0, 1)
            aa0 = jnp.zeros((k.shape[0], k.shape[2]), k.dtype)
            ninf = jnp.full_like(aa0, -jnp.inf)

            def step(carry, kv):
                aa, bb, pp = carry
                kk, vv = kv
                ww = u + kk
                p = jnp.maximum(pp, ww)
                e1 = jnp.exp(pp - p)
                e2 = jnp.exp(ww - p)
                out = (e1 * aa + e2 * vv) / (e1 + e2 + EPS_WKV)
                bb_new = w + pp
                p2 = jnp.maximum(pp, kk)
                e1b = jnp.exp(pp - p2)
                e2b = jnp.exp(kk - p2)
                aa_new = e1b * aa + e2b * vv
                pp_new = p2 + jnp.log(e1b + e2b + EPS_WKV)
                return ((aa_new, bb_new, pp_new), out)
            (aa, bb, pp), outT = jax.lax.scan(step, (aa0, ninf, ninf), (kT, vT))
            output = jnp.swapaxes(outT, 0, 1)
            final_state = jnp.stack([aa, bb, pp], axis=2)
            return (output, final_state)

        def _reference_tuple_inner(x, time_decay, time_first, Wk_t, Wv_t, Wr_t, Wk_c, Wv_c, Wr_c, ln1_g, ln1_b, ln2_g, ln2_b, mix_k, mix_v, mix_r, cmix_k, cmix_r):
            h = layer_norm(x, ln1_g, ln1_b)
            k = time_shift(h, mix_k) @ Wk_t.T
            v = time_shift(h, mix_v) @ Wv_t.T
            r = jax.nn.sigmoid(time_shift(h, mix_r) @ Wr_t.T)
            w = -jnp.exp(time_decay)
            wkv_out, new_state = wkv(w, time_first, k, v)
            x = x + r * wkv_out
            h2 = layer_norm(x, ln2_g, ln2_b)
            kc = time_shift(h2, cmix_k) @ Wk_c.T
            rc = jax.nn.sigmoid(time_shift(h2, cmix_r) @ Wr_c.T)
            vv = jnp.square(jax.nn.relu(kc)) @ Wv_c.T
            x = x + rc * vv
            return (x, new_state)
        return _reference_tuple_inner(x, time_decay, time_first, Wk_t, Wv_t, Wr_t, Wk_c, Wv_c, Wr_c, ln1_g, ln1_b, ln2_g, ln2_b, mix_k, mix_v, mix_r, cmix_k, cmix_r)[0]

    def _L0_xattn_ref(query, key, value, Wq, bq, Wk, bk, Wv, bv, Wo, bo):
        import jax, jax.numpy as jnp
        import numpy as np
        D_MODEL = 512
        NUM_HEADS = 16
        HEAD_DIM = D_MODEL // NUM_HEADS

        def _split_heads(x):
            B, N, _ = x.shape
            return x.reshape(B, N, NUM_HEADS, HEAD_DIM).transpose(0, 2, 1, 3)
        B, N, _ = query.shape
        q = _split_heads(query @ Wq.T + bq)
        k = _split_heads(key @ Wk.T + bk)
        v = _split_heads(value @ Wv.T + bv)
        scores = jnp.einsum('bhnd,bhmd->bhnm', q, k)
        attn = jax.nn.softmax(scores, axis=-1)
        out = jnp.einsum('bhnm,bhmd->bhnd', attn, v)
        out = out.transpose(0, 2, 1, 3).reshape(B, N, D_MODEL)
        return out @ Wo.T + bo

    def _L0_ffn_ref(x, W1, b1, W2, b2):
        import jax, jax.numpy as jnp
        import numpy as np
        NUM_GEMMS = 8
        HIDDEN = 512
        INTER = 2048
        orig_shape = x.shape
        token_num = int(np.prod(orig_shape[:-1]))
        m = token_num // NUM_GEMMS
        xg = x.reshape(NUM_GEMMS, m, HIDDEN)
        h1 = jnp.einsum('gmh,goh->gmo', xg, W1) + b1[:, None, :]
        h2 = jnp.einsum('gmo,gho->gmh', h1, W2) + b2[:, None, :]
        return h2.reshape(orig_shape)
    x = _layernorm(x + _L0_attn_ref(x, L0_attn_time_decay, L0_attn_time_first, L0_attn_Wk_t, L0_attn_Wv_t, L0_attn_Wr_t, L0_attn_Wk_c, L0_attn_Wv_c, L0_attn_Wr_c, L0_attn_ln1_g, L0_attn_ln1_b, L0_attn_ln2_g, L0_attn_ln2_b, L0_attn_mix_k, L0_attn_mix_v, L0_attn_mix_r, L0_attn_cmix_k, L0_attn_cmix_r), axis=-1)
    x = _layernorm(x + _L0_xattn_ref(x, ctx_1024, ctx_1024, L0_xattn_Wq, L0_xattn_bq, L0_xattn_Wk, L0_xattn_bk, L0_xattn_Wv, L0_xattn_bv, L0_xattn_Wo, L0_xattn_bo), axis=-1)
    x = _layernorm(x + _L0_ffn_ref(x, L0_ffn_W1, L0_ffn_b1, L0_ffn_W2, L0_ffn_b2), axis=-1)
    return x

_drawn_inputs = setup_inputs


def setup_inputs(seed=0):
    import zlib

    import numpy as np

    out = dict(_drawn_inputs(seed))
    spreads = {'L0_attn_ln1_g': (1.0, 0.2),
     'L0_attn_ln1_b': (0.0, 0.1),
     'L0_attn_ln2_g': (1.0, 0.2),
     'L0_attn_ln2_b': (0.0, 0.1),
     'L0_attn_mix_k': (1.0, 0.2),
     'L0_attn_mix_v': (1.0, 0.2),
     'L0_attn_mix_r': (1.0, 0.2),
     'L0_attn_cmix_k': (1.0, 0.2),
     'L0_attn_cmix_r': (1.0, 0.2)}
    factors = {'L0_attn_time_first': 4.284,
     'L0_xattn_bq': 4.908,
     'L0_xattn_bk': 8.0,
     'L0_xattn_bv': 8.0,
     'L0_xattn_bo': 7.654,
     'L0_ffn_b1': 4.066,
     'L0_ffn_b2': 4.685}
    for name, (base, spread) in spreads.items():
        noise = np.random.default_rng([zlib.crc32(name.encode()), seed]).standard_normal(out[name].shape)
        drawn = base * np.exp(spread * noise) if base else spread * noise
        out[name] = jnp.asarray(drawn.astype(out[name].dtype))
    for name, factor in factors.items():
        out[name] = (out[name] * factor).astype(out[name].dtype)
    return out
```

```python
from contextlib import ExitStack

import concourse.bass as bass
from concourse import mybir

F32 = mybir.dt.float32
F32R = mybir.dt.float32r
ALU = mybir.AluOpType
ACT = mybir.ActivationFunctionType
AX_X = mybir.AxisListType.X

P = 128
B = 2
C = 512
M = C // P
N = 512
T = N // P
Q = 4
HID = 2048
O = HID // P
HB = M // 2
HEADS, KEYS = 16, 77
HD = C // HEADS
HG = P // HD
GK = HG * KEYS
KC = -(-GK // P)
LN_EPS = 1e-5
LEAST = -1e30

COLS = ("ln1_g", "ln1_b", "ln2_g", "ln2_b", "mix_k", "mix_v", "mix_r", "cmix_k", "cmix_r", "first", "bq", "bk")


class Signal:

    def __init__(self, sem, per=0, places=0, unit=1, batches=B):
        self.sem, self.per, self.places, self.unit, self.batches = sem, per, places, unit, batches

    def _until(self, eng, q, b, n):
        eng.wait_ge(self.sem, q * (self.batches * self.per * self.unit) + self.unit * (b * self.per + n))

    def item(self, eng, q, b, n):
        self._until(eng, q, b, self.places + n)

    def place(self, eng, q, b, n):
        self._until(eng, q, b, n)

    def give_places(self, eng):
        eng.sem_inc(self.sem, self.places * self.unit)


def split_product(nc, out, stationary, moving, start, stop):
    (s_hi, s_lo), (m_hi, m_lo) = stationary, moving
    nc.tensor.matmul(out, s_hi, m_hi, start=start, stop=False)
    nc.tensor.matmul(out, s_hi, m_lo, start=False, stop=False)
    return nc.tensor.matmul(out, s_lo, m_hi, start=False, stop=stop)

A_STEPS = 20


def phase_a(nc, io, scratch):
    with ExitStack() as ctx:
        def sb(name, shape, dt=F32):
            return ctx.enter_context(nc.sbuf_tensor("a_" + name, shape, dt))

        def sig(name, *args, **kw):
            return Signal(ctx.enter_context(nc.semaphore("a_" + name)), *args, **kw)

        WK, WV, WR, WRC = range(4)
        w_hi = sb("w_hi", [P, 4, M, C], F32R)
        w_lo = sb("w_lo", [P, 4, M, C], F32R)
        cols = sb("cols", [P, len(COLS) * M])
        ident = sb("ident", [P, P])
        half_neg = sb("half_neg", [P, T])

        def col(name, m):
            i = COLS.index(name) * M + m
            return cols[:, i:i + 1]

        x = sb("x", [P, B, T, C])
        xn = sb("xn", [P, T, C])
        gate = sb("gate", [P, T, C])
        stats = sb("stats", [P, T, 6])
        mv = sb("mv", [P, T, 2])
        rstd = sb("rstd", [P, T])
        veps = sb("veps", [P, T])
        h = sb("h", [P, M, N + 1])
        d = sb("d", [P, M, N])
        mixf = sb("mixf", [P, 2, HB, N])
        mix_hi = sb("mix_hi", [P, 2, HB, N], F32R)
        mix_lo = sb("mix_lo", [P, 2, HB, N], F32R)
        k = sb("k", [P, M, N])
        v = sb("v", [P, M, N])
        mx = sb("mx", [P, HB, N + 1])
        ee = sb("ee", [P, 2, HB, N])
        pp = sb("pp", [P, HB, N + 1])
        dl = sb("dl", [P, HB, N])
        aa = sb("aa", [P, HB, N + 1])
        h_last = sb("h_last", [P, 2, B, M])
        m_last = sb("m_last", [P, B, M])
        s_last = sb("s_last", [P, B, M])
        p_last = sb("p_last", [P, B, M])
        a_last = sb("a_last", [P, B, M])
        wt = sb("wt", [P, 2, 2, C])
        wt_hi = sb("wt_hi", [P, 2, 2, C], F32R)
        wt_lo = sb("wt_lo", [P, 2, 2, C], F32R)
        going = sb("going", [P, 2, C])

        ring = [ctx.enter_context(nc.psum_tensor(f"a_ring{i}", [P, 512], F32)) for i in range(4)]
        joint = [ctx.enter_context(nc.psum_tensor(f"a_joint{i}", [P, 512], F32)) for i in range(4)]

        consts_in = sig("consts_in")
        raw_in = [sig(f"raw_in{i}") for i in range(4)]
        w_hi_ready = sig("w_hi_ready")
        w_lo_ready = sig("w_lo_ready")
        state_ready = sig("state_ready")
        half_ready = sig("half_ready")

        x_in = [sig(f"x_in{b}", 1, unit=16, batches=1) for b in range(B)]
        wt_in = [sig(f"wt_in{s}", O // 2, unit=16) for s in range(2)]
        wt_hi_ready = sig("wt_hi_ready", O)
        wt_lo_ready = sig("wt_lo_ready", O, places=2)
        wt_used = sig("wt_used", O, places=2)
        joint_ready = sig("joint_ready", M)
        joint_taken = sig("joint_taken", M, places=M)
        gone = [sig(f"gone{s}", (M + T) // 2, places=1, unit=16) for s in range(2)]
        step = sig("step", A_STEPS)
        var_ready = sig("var_ready", 2)
        rstd_ready = sig("rstd_ready", 2)
        xn_ready = sig("xn_ready", 2)
        xt_ready = sig("xt_ready", M)
        xt_taken = sig("xt_taken", M)
        h_read = sig("h_read", 2, places=1)
        full_ready = sig("full_ready", 10)
        hi_ready = sig("hi_ready", 8)
        lo_ready = sig("lo_ready", 8)
        mix_used = sig("mix_used", 8, places=2)
        k_ready = sig("k_ready", M)
        k_taken = sig("k_taken", M)
        k_read = sig("k_read", 2, places=2)
        v_ready = sig("v_ready", M)
        v_taken = sig("v_taken", M)
        r_ready = sig("r_ready", T)
        r_taken = sig("r_taken", T)
        ex_ready = sig("ex_ready", 2)
        ex_done = sig("ex_done", 2)
        s_ready = sig("s_ready", 2)
        ln_done = sig("ln_done", 2)
        z_ready = sig("z_ready", 2)
        z_done = sig("z_done", 2)
        share_done = sig("share_done", 2)
        wkv_ready = sig("wkv_ready", 2)
        ot_ready = sig("ot_ready", T, places=T)
        ot_taken = sig("ot_taken", T)
        x1_ready = sig("x1_ready", 1)
        xs_ready = sig("xs_ready", 1, places=1)
        xs_stored = [sig(f"xs_stored{b}", 1, places=1, unit=16, batches=1) for b in range(B)]
        h2_ready = sig("h2_ready", M, places=M)
        h2_taken = sig("h2_taken", M)
        rc_ready = sig("rc_ready", T)
        rc_taken = sig("rc_taken", T, places=T)
        kc_stored = [sig(f"kc_stored{s}", 1, unit=16) for s in range(2)]

        block = ctx.enter_context(nc.Block())

        @block.sync
        def _(sp):
            sp.dma_start(cols[:], io["cols"]).then_inc(consts_in.sem, 16)
            sp.dma_start(ident[:], io["ident"]).then_inc(consts_in.sem, 16)
            for i, (name, to) in enumerate((("wk", d), ("wv", k), ("wr", v), ("wrc", xn))):
                sp.dma_start(to[:], io[name].rearrange("(m p) n -> p m n", p=P)).then_inc(raw_in[i].sem, 16)
            with sp.Fori(0, Q) as q:
                for b in range(B):
                    xs_stored[b].place(sp, q, 0, 1)
                    sp.dma_start(x[:, b], io["x"][b, q].rearrange("(t p) c -> p t c", p=P)
                                 ).then_inc(x_in[b].sem, 16)
                    for o in range(O):
                        wt_lo_ready.place(sp, q, b, o + 1)
                        sp.dma_start(wt[:, o % 2], io["w12"][b, q, o].rearrange("w p c -> p w c")
                                     ).then_inc(wt_in[o % 2].sem, 16)

        @block.tensor
        def _(pe):
            def transposes(banks, source, ready, free):
                for m in range(4):
                    free(m)
                    for t in range(4):
                        last = nc.tensor.transpose(banks[m][:, t * P:(t + 1) * P],
                                                   source[:, t, m * P:(m + 1) * P], ident[:])
                    last.then_inc(ready.sem, 1)

            pe.wait_ge(consts_in.sem, 32)
            pe.wait_ge(w_lo_ready.sem, 4)
            for s in (mix_used, wt_used, ot_ready, h2_ready):
                s.give_places(pe)
            with pe.Fori(0, Q) as q:
                for b in range(B):
                    def joint_part(first, count):
                        for o in range(first, first + count):
                            s = o % 2
                            wt_lo_ready.item(pe, q, b, o + 1)
                            for m in range(M):
                                if o == 0:
                                    joint_taken.place(pe, q, b, m + 1)
                                last = split_product(
                                    nc, joint[m][:],
                                    (wt_hi[:, s, 0, m * P:(m + 1) * P], wt_lo[:, s, 0, m * P:(m + 1) * P]),
                                    (wt_hi[:, s, 1], wt_lo[:, s, 1]), o == 0, o == O - 1)
                                if o == O - 1:
                                    last.then_inc(joint_ready.sem, 1)
                            if o == O - 1:
                                pe.drain().then_inc(wt_used.sem, 1)
                            else:
                                last.then_inc(wt_used.sem, 1)

                    def mix_half(w, first, hf, rows, free, ready):
                        slot = (first + hf) % 2
                        lo_ready.item(pe, q, b, first + hf + 1)
                        for n in range(4):
                            if hf == 0:
                                free(n)
                            for i in range(HB):
                                kb = hf * HB + i
                                part = slice(n * P, (n + 1) * P)
                                act_parts = (mix_hi[:, slot, i], mix_lo[:, slot, i])
                                w_parts = (w_hi[:, w, kb], w_lo[:, w, kb])
                                if rows:
                                    st, mvg = tuple(a[:, part] for a in act_parts), w_parts
                                else:
                                    st, mvg = tuple(a[:, part] for a in w_parts), act_parts
                                last = split_product(nc, ring[n][:], st, mvg, kb == 0, kb == M - 1)
                            if hf == 1:
                                last.then_inc(ready.sem, 1)
                        if hf == 0:
                            last.then_inc(mix_used.sem, 1)
                        else:
                            pe.drain().then_inc(mix_used.sem, 1)

                    def mixed(w, first, rows, free, ready):
                        for hf in range(2):
                            mix_half(w, first, hf, rows, free, ready)

                    xn_ready.item(pe, q, b, 1)
                    transposes(ring, xn, xt_ready, lambda m: rc_taken.place(pe, q, b, m + 1))
                    joint_part(0, 4)
                    mixed(WK, 0, False, lambda m: xt_taken.item(pe, q, b, m + 1), k_ready)
                    mixed(WV, 2, False, lambda m: k_taken.item(pe, q, b, m + 1), v_ready)
                    joint_part(4, 4)
                    mixed(WR, 4, True, lambda t: v_taken.item(pe, q, b, t + 1), r_ready)
                    joint_part(8, 8)
                    wkv_ready.item(pe, q, b, 2)
                    transposes(ring, v, ot_ready, lambda t: r_taken.item(pe, q, b, t + 1))
                    xn_ready.item(pe, q, b, 2)
                    transposes(ring, xn, h2_ready, lambda m: ot_taken.item(pe, q, b, m + 1))
                    mixed(WRC, 6, True, lambda t: h2_taken.item(pe, q, b, t + 1), rc_ready)

        @block.scalar
        def _(act):
            act.wait_ge(consts_in.sem, 32)
            for i, raw in enumerate((d, k, v, xn)):
                act.wait_ge(raw_in[i].sem, 16)
                nc.scalar.copy(w_hi[:, i], raw[:]).then_inc(w_hi_ready.sem, 1)
            for s in (joint_taken, rc_taken, *gone, *xs_stored):
                s.give_places(act)
            act.wait_ge(w_lo_ready.sem, 4)
            with act.Fori(0, Q) as q:
                for b in range(B):
                    def wt_high(first, count):
                        for o in range(first, first + count):
                            wt_in[o % 2].item(act, q, b, o // 2 + 1)
                            wt_used.place(act, q, b, o + 1)
                            nc.scalar.copy(wt_hi[:, o % 2], wt[:, o % 2]).then_inc(wt_hi_ready.sem, 1)

                    def high(full, i):
                        full_ready.item(act, q, b, full + 1)
                        mix_used.place(act, q, b, i + 1)
                        nc.scalar.copy(mix_hi[:, i % 2], mixf[:, full % 2]).then_inc(hi_ready.sem, 1)

                    def to_h(ready, taken, which, g, beta):
                        for m in range(M):
                            ready.item(act, q, b, m + 1)
                            if m == 0:
                                h_read.place(act, q, b, which + 1)
                            nc.scalar.activation(h[:, m, 1:], ring[m][:], ACT.Identity, scale=col(g, m),
                                                 bias=col(beta, m)).then_inc(taken.sem, 1)

                    to_h(xt_ready, xt_taken, 0, "ln1_g", "ln1_b")
                    wt_high(0, 4)
                    high(0, 0)
                    high(1, 1)
                    high(2, 2)
                    for m in range(M):
                        k_ready.item(act, q, b, m + 1)
                        k_read.place(act, q, b, m // HB + 1)
                        nc.scalar.copy(k[:, m], ring[m][:]).then_inc(k_taken.sem, 1)
                    high(3, 3)
                    high(4, 4)
                    for m in range(M):
                        v_ready.item(act, q, b, m + 1)
                        if m == 0:
                            ot_ready.place(act, q, b, T)
                        nc.scalar.copy(v[:, m], ring[m][:]).then_inc(v_taken.sem, 1)
                    high(5, 5)
                    wt_high(4, 4)
                    for hf in range(2):
                        ex_ready.item(act, q, b, hf + 1)
                        nc.scalar.activation(ee[:], ee[:], ACT.Exp).then_inc(ex_done.sem, 1)
                        wt_high(8 + 4 * hf, 2)
                        s_ready.item(act, q, b, hf + 1)
                        nc.scalar.activation(pp[:, :, 1:], ee[:, 1], ACT.Ln).then_inc(ln_done.sem, 1)
                        wt_high(10 + 4 * hf, 2)
                        z_ready.item(act, q, b, hf + 1)
                        nc.scalar.activation(ee[:], ee[:], ACT.Exp).then_inc(z_done.sem, 1)
                        for i in range(HB):
                            ins = nc.scalar.activation(dl[:, i], dl[:, i], ACT.Sigmoid, scale=-1.0,
                                                       bias=col("first", hf * HB + i))
                        ins.then_inc(share_done.sem, 1)
                    for t in range(T):
                        r_ready.item(act, q, b, t + 1)
                        if t == 0:
                            xs_ready.place(act, q, b, 1)
                        nc.scalar.activation(gate[:, t], ring[t][:], ACT.Sigmoid).then_inc(r_taken.sem, 1)
                    for m in range(M):
                        joint_ready.item(act, q, b, m + 1)
                        gone[m % 2].place(act, q, b, m // 2 + 1)
                        nc.scalar.copy(going[:, m % 2], joint[m][:]).then_inc(joint_taken.sem, 1)
                        joint_taken.item(act, q, b, m + 1)
                        act.dma_start(scratch["wc"][b * Q + q, m], going[:, m % 2]).then_inc(gone[m % 2].sem, 16)
                    to_h(h2_ready, h2_taken, 1, "ln2_g", "ln2_b")
                    xs_ready.item(act, q, b, 1)
                    act.dma_start(scratch["xs"][b * Q + q], x[:, b]).then_inc(xs_stored[b].sem, 16)
                    for hf in range(2):
                        full_ready.item(act, q, b, 7 + hf)
                        act.dma_start(scratch["kc"][b * Q + q, hf], mixf[:, hf]).then_inc(kc_stored[hf].sem, 16)
                    high(8, 6)
                    high(9, 7)
                    for t in range(T):
                        rc_ready.item(act, q, b, t + 1)
                        gone[t % 2].place(act, q, b, (M + t) // 2 + 1)
                        nc.scalar.activation(going[:, t % 2], ring[t][:], ACT.Sigmoid).then_inc(rc_taken.sem, 1)
                        rc_taken.item(act, q, b, t + 1)
                        act.dma_start(scratch["rc"][b * Q + q, t], going[:, t % 2]).then_inc(gone[t % 2].sem, 16)
            for s in gone:
                act.wait_ge(s.sem, 16 * (1 + B * Q * (M + T) // 2))
            for s in xs_stored:
                act.wait_ge(s.sem, 16 * (1 + Q))
            for s in kc_stored:
                act.wait_ge(s.sem, 16 * B * Q)

        @block.gpsimd
        def _(pool):
            xs_ready.give_places(pool)
            nc.gpsimd.memset(half_neg[:], -0.5).then_inc(half_ready.sem, 1)
            pool.wait_ge(half_ready.sem, 1)
            with pool.Fori(0, Q) as q:
                for b in range(B):
                    def root(which):
                        var_ready.item(pool, q, b, which + 1)
                        nc.gpsimd.tensor_tensor(rstd[:], veps[:], half_neg[:], ALU.pow
                                                ).then_inc(rstd_ready.sem, 1)

                    root(0)
                    root(1)
                    x1_ready.item(pool, q, b, 1)
                    nc.gpsimd.tensor_tensor(x[:, b], x[:, b], gate[:], ALU.add).then_inc(xs_ready.sem, 1)

        @block.vector
        def _(dve):
            for i, raw in enumerate((d, k, v, xn)):
                dve.wait_ge(raw_in[i].sem, 16)
                dve.wait_ge(w_hi_ready.sem, i + 1)
                nc.vector.tensor_tensor(w_lo[:, i], raw[:], w_hi[:, i].bitcast(F32), ALU.subtract
                                        ).then_inc(w_lo_ready.sem, 1)
            for s in (wt_lo_ready, h_read, k_read):
                s.give_places(dve)
            for tile, value in ((h_last, 0.0), (m_last, LEAST), (s_last, 0.0), (p_last, LEAST), (a_last, 0.0)):
                nc.vector.memset(tile[:], value).then_inc(state_ready.sem, 1)
            dve.wait_ge(state_ready.sem, 5)
            dve.wait_ge(consts_in.sem, 32)
            dve.wait_ge(w_lo_ready.sem, 4)
            with dve.Fori(0, Q) as q:
                for b in range(B):
                    done = [0]

                    def then(ins):
                        ins.then_inc(step.sem, 1)
                        done[0] += 1
                        step.item(dve, q, b, done[0])

                    def wt_low(first, count):
                        for o in range(first, first + count):
                            wt_hi_ready.item(dve, q, b, o + 1)
                            nc.vector.tensor_tensor(wt_lo[:, o % 2], wt[:, o % 2], wt_hi[:, o % 2].bitcast(F32),
                                                    ALU.subtract).then_inc(wt_lo_ready.sem, 1)

                    def layer_norm(source, which):
                        for t in range(T):
                            ins = nc.vector.bn_stats(stats[:, t], source[:, t])
                        then(ins)
                        nc.vector.tensor_copy(h[:, :, 0], h_last[:, which, b])
                        for t in range(T):
                            ins = nc.vector.bn_aggr(mv[:, t], stats[:, t])
                        then(ins)
                        nc.vector.tensor_scalar(veps[:], mv[:, :, 1], LN_EPS, None, ALU.add
                                                ).then_inc(var_ready.sem, 1)
                        if which == 0:
                            h2_ready.place(dve, q, b, M)
                        else:
                            xt_ready.item(dve, q, b, M)
                        rstd_ready.item(dve, q, b, which + 1)
                        for t in range(T):
                            ins = nc.vector.tensor_scalar(xn[:, t], source[:, t], mv[:, t, 0:1], rstd[:, t:t + 1],
                                                          ALU.subtract, ALU.mult)
                        ins.then_inc(xn_ready.sem, 1)

                    def shifted_difference(which, taken):
                        taken.item(dve, q, b, M)
                        nc.vector.tensor_copy(h_last[:, which, b], h[:, :, N])
                        then(nc.vector.tensor_tensor(d[:], h[:, :, 1:], h[:, :, 0:N], ALU.subtract))

                    def mix(full, name):
                        hf = full % 2
                        for i in range(HB):
                            m = hf * HB + i
                            ins = nc.vector.scalar_tensor_tensor(mixf[:, hf, i], d[:, m], col(name, m), h[:, m, 0:N],
                                                                 ALU.mult, ALU.add)
                        ins.then_inc(full_ready.sem, 1)

                    def low(full, i):
                        hi_ready.item(dve, q, b, i + 1)
                        nc.vector.tensor_tensor(mix_lo[:, i % 2], mixf[:, full % 2], mix_hi[:, i % 2].bitcast(F32),
                                                ALU.subtract).then_inc(lo_ready.sem, 1)
                        lo_ready.item(dve, q, b, i + 1)

                    x_in[b].item(dve, q, 0, 1)
                    layer_norm(x[:, b], 0)
                    wt_low(0, 4)
                    shifted_difference(0, xt_taken)
                    mix(0, "mix_k")
                    mix(1, "mix_k")
                    low(0, 0)
                    mix(2, "mix_v")
                    low(1, 1)
                    mix(3, "mix_v")
                    low(2, 2)
                    mix(4, "mix_r")
                    low(3, 3)
                    mix(5, "mix_r")
                    low(4, 4)
                    low(5, 5)
                    dve.sem_inc(h_read.sem, 1)
                    wt_low(4, 4)
                    for hf in range(2):
                        mine = slice(hf * HB, (hf + 1) * HB)
                        k_taken.item(dve, q, b, (hf + 1) * HB)
                        nc.vector.tensor_copy(mx[:, :, 0], m_last[:, b, mine])
                        for i in range(HB):
                            ins = nc.vector.tensor_tensor_scan(mx[:, i, 1:], k[:, hf * HB + i], k[:, hf * HB + i],
                                                               m_last[:, b, hf * HB + i:hf * HB + i + 1],
                                                               ALU.max, ALU.max)
                        then(ins)
                        nc.vector.tensor_tensor(ee[:, 0], mx[:, :, 0:N], mx[:, :, 1:], ALU.subtract)
                        nc.vector.tensor_tensor(ee[:, 1], k[:, mine], mx[:, :, 1:], ALU.subtract
                                                ).then_inc(ex_ready.sem, 1)
                        nc.vector.tensor_copy(m_last[:, b, mine], mx[:, :, N])
                        wt_low(8 + 4 * hf, 2)
                        ex_done.item(dve, q, b, hf + 1)
                        for i in range(HB):
                            ins = nc.vector.tensor_tensor_scan(ee[:, 1, i], ee[:, 0, i], ee[:, 1, i],
                                                               s_last[:, b, hf * HB + i:hf * HB + i + 1],
                                                               ALU.mult, ALU.add)
                        ins.then_inc(s_ready.sem, 1)
                        s_ready.item(dve, q, b, hf + 1)
                        nc.vector.tensor_copy(s_last[:, b, mine], ee[:, 1, :, N - 1])
                        then(nc.vector.tensor_copy(pp[:, :, 0], p_last[:, b, mine]))
                        wt_low(10 + 4 * hf, 2)
                        ln_done.item(dve, q, b, hf + 1)
                        then(nc.vector.tensor_tensor(pp[:, :, 1:], pp[:, :, 1:], mx[:, :, 1:], ALU.add))
                        nc.vector.tensor_copy(p_last[:, b, mine], pp[:, :, N])
                        ins = nc.vector.tensor_tensor(dl[:], pp[:, :, 0:N], k[:, mine], ALU.subtract)
                        ins.then_inc(k_read.sem, 1)
                        k_read.item(dve, q, b, hf + 1)
                        nc.vector.tensor_scalar(ee[:, 0], dl[:], 0.0, None, ALU.min)
                        nc.vector.tensor_scalar(ee[:, 1], dl[:], -1.0, 0.0, ALU.mult, ALU.min
                                                ).then_inc(z_ready.sem, 1)
                        nc.vector.tensor_copy(aa[:, :, 0], a_last[:, b, mine])
                        z_done.item(dve, q, b, hf + 1)
                        v_taken.item(dve, q, b, (hf + 1) * HB)
                        then(nc.vector.tensor_tensor(ee[:, 1], ee[:, 1], v[:, mine], ALU.mult))
                        for i in range(HB):
                            ins = nc.vector.tensor_tensor_scan(aa[:, i, 1:], ee[:, 0, i], ee[:, 1, i],
                                                               a_last[:, b, hf * HB + i:hf * HB + i + 1],
                                                               ALU.mult, ALU.add)
                        then(ins)
                        nc.vector.tensor_copy(a_last[:, b, mine], aa[:, :, N])
                        then(nc.vector.tensor_tensor(v[:, mine], v[:, mine], aa[:, :, 0:N], ALU.subtract))
                        share_done.item(dve, q, b, hf + 1)
                        then(nc.vector.tensor_tensor(v[:, mine], v[:, mine], dl[:], ALU.mult))
                        nc.vector.tensor_tensor(v[:, mine], v[:, mine], aa[:, :, 0:N], ALU.add
                                                ).then_inc(wkv_ready.sem, 1)
                        wkv_ready.item(dve, q, b, hf + 1)
                    for t in range(T):
                        ot_ready.item(dve, q, b, t + 1)
                        r_taken.item(dve, q, b, t + 1)
                        nc.vector.tensor_tensor(gate[:, t], gate[:, t], ring[t][:], ALU.mult
                                                ).then_inc(ot_taken.sem, 1)
                    ot_taken.item(dve, q, b, T)
                    nc.vector.tensor_tensor(gate[:], gate[:], x[:, b], ALU.add).then_inc(x1_ready.sem, 1)
                    x1_ready.item(dve, q, b, 1)
                    layer_norm(gate, 1)
                    shifted_difference(1, h2_taken)
                    mix(6, "cmix_k")
                    mix(7, "cmix_k")
                    for hf in range(2):
                        kc_stored[hf].item(dve, q, b, 1)
                        mix(8 + hf, "cmix_r")
                    low(8, 6)
                    low(9, 7)
                    dve.sem_inc(h_read.sem, 1)
                    assert done[0] == A_STEPS, done[0]


def phase_b(nc, io, scratch):
    with ExitStack() as ctx:
        def sb(name, shape, dt=F32):
            return ctx.enter_context(nc.sbuf_tensor("b_" + name, shape, dt))

        def sig(name, *args, **kw):
            return Signal(ctx.enter_context(nc.semaphore("b_" + name)), *args, **kw)

        wk_hi = sb("wk_hi", [P, O // M, M, C], F32R)
        wk_lo = sb("wk_lo", [P, O // M, M, C], F32R)
        wv_hi = sb("wv_hi", [P, O, C], F32R)
        wv_lo = sb("wv_lo", [P, O, C], F32R)
        ones = sb("ones", [P, P])
        half_neg = sb("half_neg", [P, T])
        raw = sb("raw", [P, M, N])
        in_hi = sb("in_hi", [P, M, N], F32R)
        in_lo = sb("in_lo", [P, M, N], F32R)
        relu = sb("relu", [P, 2, N])
        sq = sb("sq", [P, 2, N])
        sq_hi = sb("sq_hi", [P, 4, N], F32R)
        sq_lo = sb("sq_lo", [P, 4, N], F32R)
        rc = sb("rc", [P, 2, C])
        xs = sb("xs", [P, 2, C])
        y = sb("y", [P, T, C])
        stats = sb("stats", [P, T, 6])
        mv = sb("mv", [P, T, 2])
        veps = sb("veps", [P, T])
        rstd = sb("rstd", [P, T])
        w2 = sb("w2", [P, 2, C])
        b1 = sb("b1", [P, B, O])
        b2 = sb("b2", [1, B, C])
        acc = sb("acc", [P, C])
        bias_row = sb("bias_row", [1, C])

        wide = [ctx.enter_context(nc.psum_tensor(f"b_wide{i}", [P, 512], F32)) for i in range(2)]
        back = [ctx.enter_context(nc.psum_tensor(f"b_back{i}", [P, 512], F32)) for i in range(T)]
        bias_sum = ctx.enter_context(nc.psum_tensor("b_bias_sum", [P, 512], F32))

        PIECES = 2 * O // M
        piece_in = [sig(f"piece_in{i}") for i in range(2)]
        piece_hi = sig("piece_hi")
        piece_lo = sig("piece_lo")
        ones_ready = sig("ones_ready")
        half_ready = sig("half_ready")

        raw_in = [sig(f"raw_in{i}", 1, unit=16) for i in range(2)]
        in_hi_ready = sig("in_hi_ready", 2)
        in_lo_ready = sig("in_lo_ready", 2, places=2)
        wide_ready = sig("wide_ready", O, places=O)
        relu_done = sig("relu_done", O, places=2)
        sq_done = sig("sq_done", O, places=2)
        sq_hi_ready = sig("sq_hi_ready", O)
        sq_lo_ready = sig("sq_lo_ready", O)
        sq_used = sig("sq_used", O, places=4)
        back_ready = sig("back_ready", T)
        back_taken = sig("back_taken", T, places=T)
        rc_in = [sig(f"rc_in{i}", T // 2, unit=16) for i in range(2)]
        xs_in = [sig(f"xs_in{i}", T // 2, unit=16) for i in range(2)]
        tile_done = sig("tile_done", T, places=2)
        step = sig("step", 2)
        var_ready = sig("var_ready", 1)
        rstd_ready = sig("rstd_ready", 1)
        x2_ready = sig("x2_ready", 1)
        x2_stored = sig("x2_stored", 1, places=1, unit=16)
        b_in = [sig(f"b_in{b}", 2, unit=16, batches=1) for b in range(B)]
        w2_in = [sig(f"w2_in{i}", O // 2, unit=16) for i in range(2)]
        acc_step = sig("acc_step", O, places=2)
        bias_summed = sig("bias_summed", 1, places=1)
        bias_out = sig("bias_out", 1, places=1)
        bias_stored = sig("bias_stored", 1, places=1, unit=16)

        def w2_at(o):
            return 4 + o // 2

        block = ctx.enter_context(nc.Block())

        @block.sync
        def _(sp):
            for i in range(PIECES):
                stage = (raw, y)[i % 2]
                if i >= 2:
                    sp.wait_ge(piece_lo.sem, i - 1)
                j = i // 2
                if i % 2 == 0:
                    src = io["wkc"][:, j * C:(j + 1) * C].rearrange("(m p) n -> p m n", p=P)
                else:
                    src = io["wvc"][j * M * P:(j + 1) * M * P].rearrange("(m p) n -> p m n", p=P)
                sp.dma_start(stage[:], src).then_inc(piece_in[i % 2].sem, 16)
            sp.wait_ge(piece_lo.sem, PIECES)
            for hf in range(2):
                sp.dma_start(raw[:, hf * HB:(hf + 1) * HB], scratch["kc"][0, hf]).then_inc(raw_in[hf].sem, 16)
            with sp.Fori(0, Q) as q:
                for b in range(B):
                    g = q + b * Q
                    acc_step.place(sp, q, b, 2)
                    sp.dma_start(b1[:, b], io["b1"][b, q]).then_inc(b_in[b].sem, 16)
                    bias_summed.place(sp, q, b, 1)
                    sp.dma_start(b2[:, b], io["b2"][b, q]).then_inc(b_in[b].sem, 16)
                    for hf in range(2):
                        in_lo_ready.item(sp, q, b, hf + 1)
                        nxt = q + Q if b == 0 else q + 1
                        sp.dma_start(raw[:, hf * HB:(hf + 1) * HB], scratch["kc"][nxt, hf]
                                     ).then_inc(raw_in[hf].sem, 16)
                    for o in range(O):
                        acc_step.place(sp, q, b, o + 1)
                        sp.dma_start(w2[:, o % 2], io["w12"][b, q, o, 1]).then_inc(w2_in[o % 2].sem, 16)
                    for t in range(T):
                        tile_done.place(sp, q, b, t + 1)
                        sp.dma_start(rc[:, t % 2], scratch["rc"][g, t]).then_inc(rc_in[t % 2].sem, 16)
                        sp.dma_start(xs[:, t % 2], scratch["xs"][g, :, t]).then_inc(xs_in[t % 2].sem, 16)
                    x2_ready.item(sp, q, b, 1)
                    sp.dma_start(scratch["x2"][g], y[:]).then_inc(x2_stored.sem, 16)
            sp.wait_ge(x2_stored.sem, 16 * (1 + B * Q))
            for hf in range(2):
                sp.wait_ge(raw_in[hf].sem, 16 * (1 + B * Q))

        @block.tensor
        def _(pe):
            for s in (wide_ready, sq_used, bias_summed):
                s.give_places(pe)
            pe.wait_ge(piece_lo.sem, PIECES)
            pe.wait_ge(ones_ready.sem, 1)
            with pe.Fori(0, Q) as q:
                for b in range(B):
                    def widen(o):
                        relu_done.place(pe, q, b, o + 1)
                        for m in range(M):
                            if o == 0 and m % HB == 0:
                                in_lo_ready.item(pe, q, b, m // HB + 1)
                            part = slice((o % M) * P, (o % M + 1) * P)
                            last = split_product(nc, wide[o % 2][:],
                                                 (wk_hi[:, o // M, m, part], wk_lo[:, o // M, m, part]),
                                                 (in_hi[:, m], in_lo[:, m]), m == 0, m == M - 1)
                        last.then_inc(wide_ready.sem, 1)

                    def narrow(o):
                        sq_lo_ready.item(pe, q, b, o + 1)
                        for t in range(T):
                            if o == 0:
                                back_taken.place(pe, q, b, t + 1)
                            part = slice(t * P, (t + 1) * P)
                            last = split_product(nc, back[t][:],
                                                 (sq_hi[:, o % 4, part], sq_lo[:, o % 4, part]),
                                                 (wv_hi[:, o], wv_lo[:, o]), o == 0, o == O - 1)
                            if o == O - 1:
                                last.then_inc(back_ready.sem, 1)
                        if o == O - 1:
                            pe.drain().then_inc(sq_used.sem, 1)
                        else:
                            last.then_inc(sq_used.sem, 1)

                    for o in range(O):
                        widen(o)
                        if o >= 2:
                            narrow(o - 2)
                        if o == 14:
                            acc_step.item(pe, q, b, O)
                            b_in[b].item(pe, q, 0, 2)
                            bias_out.place(pe, q, b, 1)
                            nc.tensor.matmul(bias_sum[:], ones[:], acc[:], start=True, stop=False)
                            nc.tensor.matmul(bias_sum[:], ones[0:1, :], b2[:, b], start=False, stop=True
                                             ).then_inc(bias_summed.sem, 1)
                    narrow(O - 2)
                    narrow(O - 1)

        @block.scalar
        def _(act):
            for i in range(PIECES):
                act.wait_ge(piece_in[i % 2].sem, 16 * (i // 2 + 1))
                stage, to = ((raw, wk_hi[:, i // 2]), (y, wv_hi[:, i // 2 * M:(i // 2 + 1) * M]))[i % 2]
                nc.scalar.copy(to, stage[:]).then_inc(piece_hi.sem, 1)
            for s in (relu_done, bias_out, bias_stored):
                s.give_places(act)
            with act.Fori(0, Q) as q:
                for b in range(B):
                    for hf in range(2):
                        mine = slice(hf * HB, (hf + 1) * HB)
                        raw_in[hf].item(act, q, b, 1)
                        if hf == 0:
                            wide_ready.place(act, q, b, O)
                        nc.scalar.copy(in_hi[:, mine], raw[:, mine]).then_inc(in_hi_ready.sem, 1)
                    for o in range(O):
                        wide_ready.item(act, q, b, o + 1)
                        sq_done.place(act, q, b, o + 1)
                        nc.scalar.activation(relu[:, o % 2], wide[o % 2][:], ACT.Relu).then_inc(relu_done.sem, 1)
                        relu_done.item(act, q, b, o + 1)
                        sq_used.place(act, q, b, o + 1)
                        nc.scalar.activation(sq_hi[:, o % 4], relu[:, o % 2], ACT.Square
                                             ).then_inc(sq_hi_ready.sem, 1)
                    bias_summed.item(act, q, b, 1)
                    bias_stored.place(act, q, b, 1)
                    nc.scalar.copy(bias_row[:], bias_sum[0:1, :]).then_inc(bias_out.sem, 1)
                    bias_out.item(act, q, b, 1)
                    act.dma_start(scratch["bias"][q + b * Q], bias_row[:]).then_inc(bias_stored.sem, 16)
            act.wait_ge(bias_stored.sem, 16 * (1 + B * Q))

        @block.gpsimd
        def _(pool):
            in_lo_ready.give_places(pool)
            nc.gpsimd.memset(half_neg[:], -0.5).then_inc(half_ready.sem, 1)
            pool.wait_ge(half_ready.sem, 1)
            with pool.Fori(0, Q) as q:
                for b in range(B):
                    for hf in range(2):
                        mine = slice(hf * HB, (hf + 1) * HB)
                        in_hi_ready.item(pool, q, b, hf + 1)
                        nc.gpsimd.tensor_tensor(in_lo[:, mine], raw[:, mine], in_hi[:, mine].bitcast(F32),
                                                ALU.subtract).then_inc(in_lo_ready.sem, 1)
                    var_ready.item(pool, q, b, 1)
                    nc.gpsimd.tensor_tensor(rstd[:], veps[:], half_neg[:], ALU.pow).then_inc(rstd_ready.sem, 1)

        @block.vector
        def _(dve):
            for i in range(PIECES):
                stage, hi, lo = ((raw, wk_hi[:, i // 2], wk_lo[:, i // 2]),
                                 (y, wv_hi[:, i // 2 * M:(i // 2 + 1) * M],
                                  wv_lo[:, i // 2 * M:(i // 2 + 1) * M]))[i % 2]
                dve.wait_ge(piece_hi.sem, i + 1)
                dve.wait_ge(piece_in[i % 2].sem, 16 * (i // 2 + 1))
                nc.vector.tensor_tensor(lo, stage[:], hi.bitcast(F32), ALU.subtract).then_inc(piece_lo.sem, 1)
            nc.vector.memset(ones[:], 1.0).then_inc(ones_ready.sem, 1)
            for s in (sq_done, back_taken, tile_done, acc_step):
                s.give_places(dve)
            dve.wait_ge(piece_lo.sem, PIECES)
            x2_stored.give_places(dve)
            with dve.Fori(0, Q) as q:
                for b in range(B):
                    for o in range(O):
                        relu_done.item(dve, q, b, o + 1)
                        if o >= 2:
                            sq_lo_ready.item(dve, q, b, o - 1)
                        nc.vector.tensor_tensor(sq[:, o % 2], relu[:, o % 2], relu[:, o % 2], ALU.mult
                                                ).then_inc(sq_done.sem, 1)
                        for w in range(O):
                            if w2_at(w) != o:
                                continue
                            w2_in[w % 2].item(dve, q, b, w // 2 + 1)
                            column = b1[:, b, w:w + 1]
                            if w == 0:
                                b_in[b].item(dve, q, 0, 2)
                                bias_summed.place(dve, q, b, 1)
                                nc.vector.tensor_scalar(acc[:], w2[:, 0], column, None, ALU.mult
                                                        ).then_inc(acc_step.sem, 1)
                            else:
                                acc_step.item(dve, q, b, w)
                                nc.vector.scalar_tensor_tensor(acc[:], w2[:, w % 2], column, acc[:],
                                                               ALU.mult, ALU.add).then_inc(acc_step.sem, 1)
                        sq_done.item(dve, q, b, o + 1)
                        sq_hi_ready.item(dve, q, b, o + 1)
                        nc.vector.tensor_tensor(sq_lo[:, o % 4], sq[:, o % 2], sq_hi[:, o % 4].bitcast(F32),
                                                ALU.subtract).then_inc(sq_lo_ready.sem, 1)
                    x2_stored.place(dve, q, b, 1)
                    for t in range(T + 1):
                        if t < T:
                            back_ready.item(dve, q, b, t + 1)
                            rc_in[t % 2].item(dve, q, b, t // 2 + 1)
                            nc.vector.tensor_tensor(y[:, t], rc[:, t % 2], back[t][:], ALU.mult
                                                    ).then_inc(back_taken.sem, 1)
                        if t >= 1:
                            back_taken.item(dve, q, b, t)
                            xs_in[(t - 1) % 2].item(dve, q, b, (t - 1) // 2 + 1)
                            nc.vector.tensor_tensor(y[:, t - 1], y[:, t - 1], xs[:, (t - 1) % 2], ALU.add
                                                    ).then_inc(tile_done.sem, 1)
                    for t in range(T):
                        tile_done.item(dve, q, b, t + 1)
                        ins = nc.vector.bn_stats(stats[:, t], y[:, t])
                    ins.then_inc(step.sem, 1)
                    step.item(dve, q, b, 1)
                    nc.vector.memset(veps[:], LN_EPS)
                    for t in range(T):
                        ins = nc.vector.bn_aggr(mv[:, t], stats[:, t])
                    ins.then_inc(step.sem, 1)
                    step.item(dve, q, b, 2)
                    nc.vector.tensor_tensor(veps[:], mv[:, :, 1], veps[:], ALU.add).then_inc(var_ready.sem, 1)
                    rstd_ready.item(dve, q, b, 1)
                    for t in range(T):
                        ins = nc.vector.tensor_scalar(y[:, t], y[:, t], mv[:, t, 0:1], rstd[:, t:t + 1],
                                                      ALU.subtract, ALU.mult)
                    ins.then_inc(x2_ready.sem, 1)


def phase_c(nc, io, scratch, out):
    with ExitStack() as ctx:
        def sb(name, shape, dt=F32):
            return ctx.enter_context(nc.sbuf_tensor("c_" + name, shape, dt))

        def sig(name, *args, **kw):
            return Signal(ctx.enter_context(nc.semaphore("c_" + name)), *args, **kw)

        G = M
        PG = 2
        STEPS = T * G // PG
        PH = PG * HG
        ROWS = [min(P, GK - j * P) for j in range(KC)]

        wq_hi, wq_lo = sb("wq_hi", [P, M, C], F32R), sb("wq_lo", [P, M, C], F32R)
        wo_hi, wo_lo = sb("wo_hi", [P, M, C], F32R), sb("wo_lo", [P, M, C], F32R)
        kd_hi, kd_lo = sb("kd_hi", [P, B, G, GK], F32R), sb("kd_lo", [P, B, G, GK], F32R)
        vd_hi, vd_lo = sb("vd_hi", [P, B, G, KC, P], F32R), sb("vd_lo", [P, B, G, KC, P], F32R)
        cols = sb("cols", [P, len(COLS) * M])
        ident = sb("ident", [P, P])
        half_neg = sb("half_neg", [P, T])
        bo = sb("bo", [P, C])
        bv = sb("bv", [P, C])
        values = sb("values", [KEYS, B, C])
        context = sb("context", [P, M, B * KEYS])

        def col(name, m):
            i = COLS.index(name) * M + m
            return cols[:, i:i + 1]

        x2 = sb("x2", [P, B, T, C])
        xt_hi, xt_lo = sb("xt_hi", [P, M, N], F32R), sb("xt_lo", [P, M, N], F32R)
        qt_hi, qt_lo = sb("qt_hi", [P, M, N], F32R), sb("qt_lo", [P, M, N], F32R)
        pr = sb("pr", [P, T, HEADS * KEYS])
        pt_hi, pt_lo = sb("pt_hi", [P, 3, N], F32R), sb("pt_lo", [P, 3, N], F32R)
        most = sb("most", [P, 2, PG, HG])
        total = sb("total", [P, 2, PH])
        share = sb("share", [P, 2, PH])
        x3 = sb("x3", [P, T, C])
        wc = sb("wc", [P, 2, C])
        wc_hi, wc_lo = sb("wc_hi", [P, M, C], F32R), sb("wc_lo", [P, M, C], F32R)
        bias = sb("bias", [P, C])
        stats = sb("stats", [P, T, 6])
        mv = sb("mv", [P, T, 2])
        veps = sb("veps", [P, T])
        rstd = sb("rstd", [P, T])

        ring = [ctx.enter_context(nc.psum_tensor(f"c_ring{i}", [P, 512], F32)) for i in range(4)]
        sc = [ctx.enter_context(nc.psum_tensor(f"c_sc{i}", [P, PG, 512], F32)) for i in range(2)]

        pr_flat = pr[:].rearrange("p t k -> p (t k)")
        x2_flat = x2[:].rearrange("p b t c -> p (b t c)")
        wk_raw, wv_raw = x2[:, 0], x2[:, 1]
        wq_raw = x3[:]
        wo_raw = pr_flat[:, 0:M * C].rearrange("p (m c) -> p m c", m=M)
        kd_raw = pr_flat[:, M * C:M * C + B * G * GK].rearrange("p (b g k) -> p b g k", b=B, g=G)
        vd_raw = x2_flat[:, 0:B * G * KC * P].rearrange("p (b g j e) -> p b g j e", b=B, g=G, j=KC)

        s_consts = sig("s_consts")
        s_kv_raw = sig("s_kv_raw")
        s_q_raw = sig("s_q_raw")
        s_o_raw = sig("s_o_raw")
        s_kd_zero = sig("s_kd_zero")
        s_vd_zero = sig("s_vd_zero")
        s_keys = sig("s_keys")
        s_keys_taken = sig("s_keys_taken")
        s_values = sig("s_values")
        s_values_taken = sig("s_values_taken")
        s_values_out = sig("s_values_out")
        s_vd_in = sig("s_vd_in")
        s_hi = sig("s_hi")
        s_lo = sig("s_lo")
        s_half = sig("s_half")

        x2_in = [sig(f"x2_in{b}", 1, unit=16, batches=1) for b in range(B)]
        wc_in = [sig(f"wc_in{i}", M // 2, unit=16) for i in range(2)]
        bias_in = sig("bias_in", 1, unit=16)
        wc_hi_ready = sig("wc_hi_ready", M)
        wc_lo_ready = sig("wc_lo_ready", M, places=2)
        xt_ready = sig("xt_ready", M)
        xt_hi_ready = sig("xt_hi_ready", M)
        xt_taken = sig("xt_taken", M)
        q_ready = sig("q_ready", M)
        q_hi_ready = sig("q_hi_ready", M)
        q_taken = sig("q_taken", M)
        sc_ready = sig("sc_ready", STEPS)
        sc_taken = sig("sc_taken", STEPS, places=2)
        most_ready = sig("most_ready", STEPS)
        exp_done = sig("exp_done", STEPS)
        total_ready = sig("total_ready", STEPS)
        share_ready = sig("share_ready", STEPS)
        pr_ready = sig("pr_ready", STEPS)
        pt_ready = sig("pt_ready", G * KC)
        pt_hi_ready = sig("pt_hi_ready", G * KC)
        pt_taken = sig("pt_taken", G * KC)
        pt_used = sig("pt_used", G * KC, places=3)
        o_ready = sig("o_ready", G)
        o_hi_ready = sig("o_hi_ready", G)
        o_taken = sig("o_taken", G)
        x2_read = sig("x2_read", 1, places=1)
        bo_added = sig("bo_added", 1)
        proj_ready = sig("proj_ready", T)
        proj_taken = sig("proj_taken", T)
        step = sig("step", 4)
        var_ready = sig("var_ready", 2)
        rstd_ready = sig("rstd_ready", 2)
        x3_ready = sig("x3_ready", 1)
        x3t_ready = sig("x3t_ready", M)
        x3t_hi_ready = sig("x3t_hi_ready", M)
        x3t_taken = sig("x3t_taken", M)
        bias_added = sig("bias_added", 1, places=1)
        ffn_ready = sig("ffn_ready", T, places=T)
        ffn_taken = sig("ffn_taken", T, places=T)
        y_ready = sig("y_ready", 1)
        y_stored = sig("y_stored", 1, places=1, unit=16)

        def segments():
            for head in range(HG):
                key = 0
                while key < KEYS:
                    chunk, row = divmod(head * KEYS + key, P)
                    count = min(KEYS - key, P - row)
                    yield head, key, chunk, row, count
                    key += count

        block = ctx.enter_context(nc.Block())

        @block.sync
        def _(sp):
            for to, src in ((cols[:], io["cols"]), (ident[:], io["ident"]),
                            (context[:], io["ctx"].rearrange("(m p) k -> p m k", p=P)),
                            (bv[:], io["bv"].to_broadcast([P, C])), (bo[:], io["bo"].to_broadcast([P, C]))):
                sp.dma_start(to, src).then_inc(s_consts.sem, 16)
            for to, name in ((wk_raw, "xwk"), (wv_raw, "xwv")):
                sp.dma_start(to, io[name].rearrange("(m p) n -> p m n", p=P)).then_inc(s_kv_raw.sem, 16)
            sp.dma_start(wq_raw, io["xwq"].rearrange("(m p) n -> p m n", p=P)).then_inc(s_q_raw.sem, 16)
            sp.dma_start(wo_raw, io["xwo"].rearrange("(m p) n -> p m n", p=P)).then_inc(s_o_raw.sem, 16)
            sp.wait_ge(s_values_taken.sem, B)
            sp.dma_start(scratch["v"].rearrange("b k c -> k b c"), values[:]).then_inc(s_values_out.sem, 16)
            sp.wait_ge(s_values_out.sem, 16)
            sp.wait_ge(s_vd_zero.sem, 1)
            for b in range(B):
                src = scratch["v"][b].rearrange("k (g h d) -> h k g d", g=G, h=HG)
                for head, key, chunk, row, count in segments():
                    sp.dma_start(vd_raw[row:row + count, b, :, chunk, head * HD:(head + 1) * HD],
                                 src[head, key:key + count]).then_inc(s_vd_in.sem, 16)
            sp.wait_ge(s_lo.sem, 4)
            sp.dma_start(x2[:, 0], scratch["x2"][0]).then_inc(x2_in[0].sem, 16)
            with sp.Fori(0, Q) as q:
                for b in range(B):
                    x2_read.place(sp, q, b, 1)
                    nxt = q + Q if b == 0 else q + 1
                    sp.dma_start(x2[:, 1 - b], scratch["x2"][nxt]).then_inc(x2_in[1 - b].sem, 16)
                    for m in range(M):
                        wc_lo_ready.place(sp, q, b, m + 1)
                        sp.dma_start(wc[:, m % 2], scratch["wc"][q + b * Q, m]).then_inc(wc_in[m % 2].sem, 16)
                    bias_added.place(sp, q, b, 1)
                    sp.dma_start(bias[:], scratch["bias"][q + b * Q].to_broadcast([P, C])
                                 ).then_inc(bias_in.sem, 16)
                    y_ready.item(sp, q, b, 1)
                    sp.dma_start(out[b, q].rearrange("(t p) c -> p t c", p=P), x3[:]).then_inc(y_stored.sem, 16)
            sp.wait_ge(y_stored.sem, 16 * (1 + B * Q))
            sp.wait_ge(x2_in[0].sem, 16 * (1 + Q))

        @block.tensor
        def _(pe):
            pe.wait_ge(s_consts.sem, 16 * 5)
            pe.wait_ge(s_kv_raw.sem, 32)
            for g in range(G):
                for m in range(M):
                    last = nc.tensor.matmul(ring[g][:, 0:B * KEYS], wk_raw[:, m, g * P:(g + 1) * P],
                                            context[:, m], start=m == 0, stop=m == M - 1)
                last.then_inc(s_keys.sem, 1)
            for b in range(B):
                for m in range(M):
                    last = nc.tensor.matmul(sc[0][0:KEYS, b], context[:, m, b * KEYS:(b + 1) * KEYS],
                                            wv_raw[:, m], start=m == 0, stop=m == M - 1)
                last.then_inc(s_values.sem, 1)
            for s in (pt_used, ffn_ready):
                s.give_places(pe)
            pe.wait_ge(s_lo.sem, 4)
            with pe.Fori(0, Q) as q:
                for b in range(B):
                    def transposes(source, ready, free):
                        for m in range(M):
                            free(m)
                            for t in range(T):
                                last = nc.tensor.transpose(ring[m][:, t * P:(t + 1) * P],
                                                           source[:, t, m * P:(m + 1) * P], ident[:])
                            last.then_inc(ready.sem, 1)

                    def by_tokens(source, weight, ready, free):
                        (s_hi, s_lo), (w_hi, w_lo) = source, weight
                        for t in range(T):
                            free(t)
                            part = slice(t * P, (t + 1) * P)
                            for m in range(M):
                                last = split_product(nc, ring[t][:], (s_hi[:, m, part], s_lo[:, m, part]),
                                                     (w_hi[:, m], w_lo[:, m]), m == 0, m == M - 1)
                            last.then_inc(ready.sem, 1)

                    def attend(i):
                        g, j = divmod(i, KC)
                        pt_taken.item(pe, q, b, i + 1)
                        if j == 0:
                            if g == 0:
                                q_taken.item(pe, q, b, M)
                            else:
                                o_taken.item(pe, q, b, g)
                        rows, s = ROWS[j], i % 3
                        last = split_product(nc, ring[3][:], (vd_hi[0:rows, b, g, j], vd_lo[0:rows, b, g, j]),
                                             (pt_hi[0:rows, s], pt_lo[0:rows, s]), j == 0, j == KC - 1)
                        if j == KC - 1:
                            last.then_inc(o_ready.sem, 1)
                            pe.drain().then_inc(pt_used.sem, 1)
                        else:
                            last.then_inc(pt_used.sem, 1)

                    x2_in[b].item(pe, q, 0, 1)
                    transposes(x2[:, b], xt_ready, lambda m: ffn_taken.place(pe, q, b, m + 1))
                    for g in range(M):
                        xt_taken.item(pe, q, b, M if g == 0 else g + 1)
                        part = slice(g * P, (g + 1) * P)
                        for m in range(M):
                            last = split_product(nc, ring[g][:], (wq_hi[:, m, part], wq_lo[:, m, part]),
                                                 (xt_hi[:, m], xt_lo[:, m]), m == 0, m == M - 1)
                        last.then_inc(q_ready.sem, 1)
                    for i in range(STEPS):
                        t, pair = divmod(i, G // PG)
                        sc_taken.place(pe, q, b, i + 1)
                        for gg in range(PG):
                            g = pair * PG + gg
                            if t == 0:
                                q_taken.item(pe, q, b, g + 1)
                            part = slice(t * P, (t + 1) * P)
                            last = split_product(nc, sc[i % 2][:, gg, 0:GK], (qt_hi[:, g, part], qt_lo[:, g, part]),
                                                 (kd_hi[:, b, g], kd_lo[:, b, g]), True, True)
                        last.then_inc(sc_ready.sem, 1)
                    pr_ready.item(pe, q, b, STEPS)
                    for i in range(G * KC + 2):
                        if i < G * KC:
                            g, j = divmod(i, KC)
                            if g == 0:
                                q_taken.item(pe, q, b, j + 1)
                            else:
                                pt_taken.item(pe, q, b, i - KC + 1)
                        if i >= 2:
                            attend(i - 2)
                        if i < G * KC:
                            for t in range(T):
                                last = nc.tensor.transpose(
                                    ring[j][0:ROWS[j], t * P:(t + 1) * P],
                                    pr[:, t, g * GK + j * P:g * GK + j * P + ROWS[j]], ident[:])
                            last.then_inc(pt_ready.sem, 1)
                    o_taken.item(pe, q, b, G)
                    by_tokens((qt_hi, qt_lo), (wo_hi, wo_lo), proj_ready, lambda t: None)
                    x3_ready.item(pe, q, b, 1)
                    transposes(x3, x3t_ready, lambda m: proj_taken.item(pe, q, b, m + 1))
                    x3t_taken.item(pe, q, b, M)
                    wc_lo_ready.item(pe, q, b, M)
                    by_tokens((xt_hi, xt_lo), (wc_hi, wc_lo), ffn_ready, lambda t: None)

        @block.scalar
        def _(act):
            act.wait_ge(s_consts.sem, 16 * 5)
            act.wait_ge(s_kd_zero.sem, 1)
            for g in range(G):
                act.wait_ge(s_keys.sem, g + 1)
                for head in range(HG):
                    mine = slice(head * HD, (head + 1) * HD)
                    ins = nc.scalar.activation(
                        kd_raw[mine, :, g, head * KEYS:(head + 1) * KEYS],
                        ring[g][mine, 0:B * KEYS].rearrange("p (b k) -> p b k", b=B), ACT.Identity,
                        bias=col("bk", g)[mine])
            ins.then_inc(s_keys_taken.sem, 1)
            act.wait_ge(s_q_raw.sem, 16)
            nc.scalar.copy(wq_hi[:], wq_raw).then_inc(s_hi.sem, 1)
            act.wait_ge(s_o_raw.sem, 16)
            nc.scalar.copy(wo_hi[:], wo_raw).then_inc(s_hi.sem, 1)
            act.wait_ge(s_keys_taken.sem, 1)
            nc.scalar.copy(kd_hi[:], kd_raw).then_inc(s_hi.sem, 1)
            act.wait_ge(s_vd_in.sem, 16 * B * len(list(segments())))
            nc.scalar.copy(vd_hi[:], vd_raw).then_inc(s_hi.sem, 1)
            with act.Fori(0, Q) as q:
                for b in range(B):
                    def high(ready, done, to, count=M):
                        for m in range(count):
                            ready.item(act, q, b, m + 1)
                            nc.scalar.copy(to[:, m], ring[m][:]).then_inc(done.sem, 1)

                    ffn_ready.place(act, q, b, T)
                    high(xt_ready, xt_hi_ready, xt_hi)
                    for g in range(M):
                        q_ready.item(act, q, b, g + 1)
                        nc.scalar.activation(qt_hi[:, g], ring[g][:], ACT.Identity, bias=col("bq", g)
                                             ).then_inc(q_hi_ready.sem, 1)
                    for i in range(STEPS):
                        t, pair = divmod(i, G // PG)
                        sc_taken.item(act, q, b, i + 1)
                        span = pr[:, t, pair * PH * KEYS:(pair + 1) * PH * KEYS]
                        nc.scalar.activation(span, span, ACT.Exp).then_inc(exp_done.sem, 1)
                    for m in range(M):
                        wc_in[m % 2].item(act, q, b, m // 2 + 1)
                        nc.scalar.copy(wc_hi[:, m], wc[:, m % 2]).then_inc(wc_hi_ready.sem, 1)
                    for i in range(G * KC):
                        g, j = divmod(i, KC)
                        pt_ready.item(act, q, b, i + 1)
                        pt_used.place(act, q, b, i + 1)
                        rows = slice(0, ROWS[j])
                        nc.scalar.copy(pt_hi[rows, i % 3], ring[j][rows, :]).then_inc(pt_hi_ready.sem, 1)
                        if j == KC - 2 and g >= 1:
                            o_ready.item(act, q, b, g)
                            nc.scalar.copy(qt_hi[:, g - 1], ring[3][:]).then_inc(o_hi_ready.sem, 1)
                    o_ready.item(act, q, b, G)
                    nc.scalar.copy(qt_hi[:, G - 1], ring[3][:]).then_inc(o_hi_ready.sem, 1)
                    high(x3t_ready, x3t_hi_ready, xt_hi)

        @block.gpsimd
        def _(pool):
            nc.gpsimd.memset(kd_raw, 0.0).then_inc(s_kd_zero.sem, 1)
            nc.gpsimd.memset(half_neg[:], -0.5).then_inc(s_half.sem, 1)
            pool.wait_ge(s_values.sem, B)
            nc.gpsimd.memset(vd_raw, 0.0).then_inc(s_vd_zero.sem, 1)
            wc_lo_ready.give_places(pool)
            bias_added.give_places(pool)
            pool.wait_ge(s_half.sem, 1)
            pool.wait_ge(s_consts.sem, 16 * 5)
            with pool.Fori(0, Q) as q:
                for b in range(B):
                    xt_ready.item(pool, q, b, M)
                    nc.gpsimd.tensor_tensor(x2[:, b], x2[:, b], bo[:].unsqueeze(1).to_broadcast([P, T, C]),
                                            ALU.add).then_inc(bo_added.sem, 1)
                    for m in range(M):
                        wc_hi_ready.item(pool, q, b, m + 1)
                        nc.gpsimd.tensor_tensor(wc_lo[:, m], wc[:, m % 2], wc_hi[:, m].bitcast(F32), ALU.subtract
                                                ).then_inc(wc_lo_ready.sem, 1)
                    var_ready.item(pool, q, b, 1)
                    nc.gpsimd.tensor_tensor(rstd[:], veps[:], half_neg[:], ALU.pow).then_inc(rstd_ready.sem, 1)
                    bias_in.item(pool, q, b, 1)
                    x3t_ready.item(pool, q, b, M)
                    nc.gpsimd.tensor_tensor(x3[:], x3[:], bias[:].unsqueeze(1).to_broadcast([P, T, C]),
                                            ALU.add).then_inc(bias_added.sem, 1)
                    var_ready.item(pool, q, b, 2)
                    nc.gpsimd.tensor_tensor(rstd[:], veps[:], half_neg[:], ALU.pow).then_inc(rstd_ready.sem, 1)

        @block.vector
        def _(dve):
            dve.wait_ge(s_consts.sem, 16 * 5)
            for b in range(B):
                dve.wait_ge(s_values.sem, b + 1)
                nc.vector.tensor_tensor(values[:, b], sc[0][0:KEYS, b], bv[0:KEYS, :], ALU.add
                                        ).then_inc(s_values_taken.sem, 1)
            for i, (raw, hi, lo) in enumerate(((wq_raw, wq_hi, wq_lo), (wo_raw, wo_hi, wo_lo),
                                               (kd_raw, kd_hi, kd_lo), (vd_raw, vd_hi, vd_lo))):
                dve.wait_ge(s_hi.sem, i + 1)
                nc.vector.tensor_tensor(lo[:], raw, hi[:].bitcast(F32), ALU.subtract).then_inc(s_lo.sem, 1)
            for s in (sc_taken, ffn_taken, x2_read, y_stored):
                s.give_places(dve)
            dve.wait_ge(s_lo.sem, 4)
            dve.wait_ge(s_values_taken.sem, B)
            with dve.Fori(0, Q) as q:
                for b in range(B):
                    def low(hi_ready, taken, hi, lo):
                        for m in range(M):
                            hi_ready.item(dve, q, b, m + 1)
                            nc.vector.tensor_tensor(lo[:, m], ring[m][:], hi[:, m].bitcast(F32), ALU.subtract
                                                    ).then_inc(taken.sem, 1)

                    def layer_norm(tile, taken, which, ready):
                        for t in range(T):
                            taken.item(dve, q, b, t + 1)
                            ins = nc.vector.bn_stats(stats[:, t], tile[:, t])
                        ins.then_inc(step.sem, 1)
                        step.item(dve, q, b, 2 * which + 1)
                        nc.vector.memset(veps[:], LN_EPS)
                        for t in range(T):
                            ins = nc.vector.bn_aggr(mv[:, t], stats[:, t])
                        ins.then_inc(step.sem, 1)
                        step.item(dve, q, b, 2 * which + 2)
                        nc.vector.tensor_tensor(veps[:], mv[:, :, 1], veps[:], ALU.add).then_inc(var_ready.sem, 1)
                        rstd_ready.item(dve, q, b, which + 1)
                        for t in range(T):
                            ins = nc.vector.tensor_scalar(tile[:, t], tile[:, t], mv[:, t, 0:1], rstd[:, t:t + 1],
                                                          ALU.subtract, ALU.mult)
                        ins.then_inc(ready.sem, 1)

                    def heads(ap):
                        return ap.rearrange("p g (h k) -> p g h k", k=KEYS)

                    def softmax_front(i):
                        t, pair = divmod(i, G // PG)
                        s = i % 2
                        sc_ready.item(dve, q, b, i + 1)
                        scores = heads(sc[s][:, :, 0:GK])
                        nc.vector.tensor_reduce(most[:, s], scores, AX_X, ALU.max).then_inc(most_ready.sem, 1)
                        most_ready.item(dve, q, b, i + 1)
                        span = pr[:, t, pair * PH * KEYS:(pair + 1) * PH * KEYS]
                        nc.vector.tensor_tensor(span.rearrange("p (g h k) -> p g h k", g=PG, k=KEYS), scores,
                                                most[:, s].unsqueeze(3).to_broadcast([P, PG, HG, KEYS]),
                                                ALU.subtract).then_inc(sc_taken.sem, 1)

                    def softmax_back(i):
                        t, pair = divmod(i, G // PG)
                        s = i % 2
                        span = pr[:, t, pair * PH * KEYS:(pair + 1) * PH * KEYS].rearrange("p (h k) -> p h k", k=KEYS)
                        exp_done.item(dve, q, b, i + 1)
                        nc.vector.tensor_reduce(total[:, s], span, AX_X, ALU.add).then_inc(total_ready.sem, 1)
                        total_ready.item(dve, q, b, i + 1)
                        nc.vector.reciprocal(share[:, s], total[:, s]).then_inc(share_ready.sem, 1)
                        share_ready.item(dve, q, b, i + 1)
                        nc.vector.tensor_tensor(span, span, share[:, s].unsqueeze(2).to_broadcast([P, PH, KEYS]),
                                                ALU.mult).then_inc(pr_ready.sem, 1)

                    low(xt_hi_ready, xt_taken, xt_hi, xt_lo)
                    for g in range(M):
                        q_hi_ready.item(dve, q, b, g + 1)
                        nc.vector.scalar_tensor_tensor(qt_lo[:, g], ring[g][:], col("bq", g),
                                                       qt_hi[:, g].bitcast(F32), ALU.add, ALU.subtract
                                                       ).then_inc(q_taken.sem, 1)
                    for i in range(STEPS + 1):
                        if i < STEPS:
                            softmax_front(i)
                        if i >= 1:
                            softmax_back(i - 1)

                    def o_low(g):
                        o_hi_ready.item(dve, q, b, g + 1)
                        nc.vector.tensor_tensor(qt_lo[:, g], ring[3][:], qt_hi[:, g].bitcast(F32), ALU.subtract
                                                ).then_inc(o_taken.sem, 1)

                    for i in range(G * KC):
                        g, j = divmod(i, KC)
                        rows = slice(0, ROWS[j])
                        pt_hi_ready.item(dve, q, b, i + 1)
                        nc.vector.tensor_tensor(pt_lo[rows, i % 3], ring[j][rows, :],
                                                pt_hi[rows, i % 3].bitcast(F32), ALU.subtract
                                                ).then_inc(pt_taken.sem, 1)
                        if j == KC - 2 and g >= 1:
                            o_low(g - 1)
                    o_low(G - 1)
                    y_stored.place(dve, q, b, 1)
                    bo_added.item(dve, q, b, 1)
                    for t in range(T):
                        proj_ready.item(dve, q, b, t + 1)
                        nc.vector.tensor_tensor(x3[:, t], x2[:, b, t], ring[t][:], ALU.add
                                                ).then_inc(proj_taken.sem, 1)
                    layer_norm(x3, proj_taken, 0, x3_ready)
                    dve.sem_inc(x2_read.sem, 1)
                    low(x3t_hi_ready, x3t_taken, xt_hi, xt_lo)
                    bias_added.item(dve, q, b, 1)
                    for t in range(T):
                        ffn_ready.item(dve, q, b, t + 1)
                        nc.vector.tensor_tensor(x3[:, t], x3[:, t], ring[t][:], ALU.add
                                                ).then_inc(ffn_taken.sem, 1)
                    layer_norm(x3, ffn_taken, 1, y_ready)


def build(nc, io, out):
    scratch = {
        "xs": nc.dram_tensor("xs_scratch", (B * Q, P, T, C), F32).ap(),
        "kc": nc.dram_tensor("kc_scratch", (B * Q, 2, P, HB, N), F32).ap(),
        "rc": nc.dram_tensor("rc_scratch", (B * Q, T, P, C), F32).ap(),
        "wc": nc.dram_tensor("wc_scratch", (B * Q, M, P, C), F32).ap(),
        "bias": nc.dram_tensor("bias_scratch", (B * Q, 1, C), F32).ap(),
        "x2": nc.dram_tensor("x2_scratch", (B * Q, P, T, C), F32).ap(),
        "v": nc.dram_tensor("v_scratch", (B, KEYS, C), F32).ap(),
    }
    phase_a(nc, io, scratch)
    phase_b(nc, io, scratch)
    phase_c(nc, io, scratch, out)


def kernel(**inputs):
    import numpy as np
    import concourse.bacc as bacc
    from concourse.bass_utils import run_bass_kernel_spmd

    a = {n: np.asarray(v) for n, v in inputs.items()}

    def turned(w):
        return np.ascontiguousarray(np.swapaxes(w, -1, -2))

    w1 = a["L0_ffn_W1"].reshape(B, Q, O, 1, P, C)
    w2t = turned(a["L0_ffn_W2"]).reshape(B, Q, O, 1, P, C)
    per_channel = [a["L0_attn_" + n] for n in ("ln1_g", "ln1_b", "ln2_g", "ln2_b", "mix_k", "mix_v", "mix_r",
                                               "cmix_k", "cmix_r", "time_first")]
    per_channel += [a["L0_xattn_bq"], a["L0_xattn_bk"]]
    arrays = {
        "x": a["x"].reshape(B, Q, N, C),
        "ctx": turned(a["ctx_1024"].reshape(B * KEYS, C)),
        "cols": np.concatenate([v.reshape(M, P).T for v in per_channel], axis=1),
        "ident": np.eye(P, dtype=np.float32),
        "wk": turned(a["L0_attn_Wk_t"]), "wv": turned(a["L0_attn_Wv_t"]), "wr": turned(a["L0_attn_Wr_t"]),
        "wrc": turned(a["L0_attn_Wr_c"]), "wkc": turned(a["L0_attn_Wk_c"]), "wvc": turned(a["L0_attn_Wv_c"]),
        "xwq": turned(a["L0_xattn_Wq"]), "xwk": turned(a["L0_xattn_Wk"]), "xwv": turned(a["L0_xattn_Wv"]),
        "xwo": turned(a["L0_xattn_Wo"]), "bv": a["L0_xattn_bv"].reshape(1, C), "bo": a["L0_xattn_bo"].reshape(1, C),
        "w12": np.concatenate([w1, w2t], axis=3),
        "b1": turned(a["L0_ffn_b1"].reshape(B, Q, O, P)), "b2": a["L0_ffn_b2"].reshape(B, Q, 1, C),
    }
    arrays = {n: np.ascontiguousarray(v) for n, v in arrays.items()}
    nc = bacc.Bacc("TRN2", target_bir_lowering=False, num_devices=1)
    io = {n: nc.dram_tensor(n + "_dram", v.shape, F32, kind="ExternalInput").ap() for n, v in arrays.items()}
    out = nc.dram_tensor("out_dram", (B, Q, N, C), F32, kind="ExternalOutput").ap()
    build(nc, io, out)
    got = run_bass_kernel_spmd(nc, [{n + "_dram": v for n, v in arrays.items()}], core_ids=[0])
    return got.results[0]["out_dram"].reshape(B, Q * N, C)
```

```python
import math
from contextlib import ExitStack

import concourse.bass as bass
from concourse import mybir

F32 = mybir.dt.float32
F32R = mybir.dt.float32r
ALU = mybir.AluOpType
ACT = mybir.ActivationFunctionType
AX_X = mybir.AxisListType.X

P = 128
B = 2
C = 512
M = C // P
N = 512
T = N // P
Q = 4
HID = 2048
O = HID // P
HB = M // 2
HEADS, KEYS = 16, 77
HD = C // HEADS
HG = P // HD
GK = HG * KEYS
KC = -(-GK // P)
LN_EPS = 1e-5
LEAST = -1e30

COLS = ("ln1_g", "ln1_b", "ln2_g", "ln2_b", "mix_k", "mix_v", "mix_r", "cmix_k", "cmix_r", "first", "bq", "bk")


class Signal:

    def __init__(self, sem, per=0, places=0, unit=1, batches=B):
        self.sem, self.per, self.places, self.unit, self.batches = sem, per, places, unit, batches

    def _until(self, eng, q, b, n):
        eng.wait_ge(self.sem, q * (self.batches * self.per * self.unit) + self.unit * (b * self.per + n))

    def item(self, eng, q, b, n):
        self._until(eng, q, b, self.places + n)

    def place(self, eng, q, b, n):
        self._until(eng, q, b, n)

    def give_places(self, eng):
        eng.sem_inc(self.sem, self.places * self.unit)


def split_product(nc, out, stationary, moving, start, stop):
    (s_hi, s_lo), (m_hi, m_lo) = stationary, moving
    nc.tensor.matmul(out, s_hi, m_hi, start=start, stop=False)
    nc.tensor.matmul(out, s_hi, m_lo, start=False, stop=False)
    return nc.tensor.matmul(out, s_lo, m_hi, start=False, stop=stop)


def clear(nc, semaphores):
    nc.clear_and_free_semaphores(semaphores)
    nc.all_engine_barrier()

A_STEPS = 14
OPENING_LINKS = 3


def phase_a(nc, io, scratch):
    semaphores = []
    with ExitStack() as ctx:
        def sb(name, shape, dt=F32):
            return ctx.enter_context(nc.sbuf_tensor("a_" + name, shape, dt))

        def sig(name, *args, **kw):
            semaphores.append(nc.alloc_semaphore(name="a_" + name))
            return Signal(semaphores[-1], *args, **kw)

        def in_place(name, shape):
            low = sb(name + "_lo", shape, F32R)
            size = 4 * math.prod(shape[1:])
            return low, nc.alloc_sbuf_tensor_at("a_" + name, shape, F32, offset=nc.sbuf_base - size)

        WK, WV, WR, WRC = range(4)
        w_hi = sb("w_hi", [P, 4, M, C], F32R)
        w_lo = sb("w_lo", [P, 4, M, C], F32R)
        cols = sb("cols", [P, len(COLS) * M])
        rest = sb("rest", [P, 5, M])
        ident = sb("ident", [P, P])
        half_neg = sb("half_neg", [P, T])

        def col(name, m):
            i = COLS.index(name) * M + m
            return cols[:, i:i + 1]

        x = sb("x", [P, B, T, C])
        xn = sb("xn", [P, T, C])
        gate = sb("gate", [P, T, C])
        stats = sb("stats", [P, T, 6])
        mv = sb("mv", [P, T, 2])
        rstd = sb("rstd", [P, T])
        veps = sb("veps", [P, T])
        h = sb("h", [P, 2, M, N + 1])
        mix_lo, mixf = in_place("mixf", [P, 2, M, N])
        mix_hi = sb("mix_hi", [P, 2, HB, N], F32R)
        k = sb("k", [P, B, M, N])
        v = sb("v", [P, M, N])
        mx = sb("mx", [P, HB, N + 1])
        ee = sb("ee", [P, 2, HB, N])
        pp = sb("pp", [P, HB, N + 1])
        dl = sb("dl", [P, HB, N])
        aa = sb("aa", [P, HB, N + 1])
        h_last = sb("h_last", [P, 2, B, M])
        m_last = sb("m_last", [P, B, M])
        s_last = sb("s_last", [P, B, M])
        p_last = sb("p_last", [P, B, M])
        a_last = sb("a_last", [P, B, M])
        SLOTS = 4
        wt_lo, wt = in_place("wt", [P, SLOTS, 2, C])
        wt_hi = sb("wt_hi", [P, SLOTS, 2, C], F32R)
        going = sb("going", [P, 2, C])

        ring = [ctx.enter_context(nc.psum_tensor(f"a_ring{i}", [P, 512], F32)) for i in range(4)]
        joint = [ctx.enter_context(nc.psum_tensor(f"a_joint{i}", [P, 512], F32)) for i in range(4)]

        MIX = {"k": (0, "mix_k", 0), "v": (0, "mix_v", 1), "r": (0, "mix_r", 0),
               "kc": (1, "cmix_k", 1), "rc": (1, "cmix_r", 0)}
        REST = {n: i for i, n in enumerate(MIX)}

        consts_in = sig("consts_in")
        raw_in = [sig(f"raw_in{i}") for i in range(4)]
        w_hi_ready = sig("w_hi_ready")
        w_lo_ready = sig("w_lo_ready")
        state_ready = sig("state_ready")
        half_ready = sig("half_ready")

        x_in = [sig(f"x_in{b}", 1, unit=16, batches=1) for b in range(B)]
        wt_in = [sig(f"wt_in{s}", O // SLOTS, unit=16) for s in range(SLOTS)]
        wt_hi_ready = sig("wt_hi_ready", O)
        wt_lo_ready = sig("wt_lo_ready", O)
        wt_used = sig("wt_used", O, places=SLOTS)
        joint_ready = sig("joint_ready", M)
        joint_taken = sig("joint_taken", M, places=M)
        wc_stored = [sig(f"wc_stored{m}", 1, places=1, unit=16) for m in range(M)]
        rc_stored = [sig(f"rc_stored{s}", T // 2, places=1, unit=16) for s in range(2)]
        ln_step = [sig(f"ln_step{w}", 2) for w in range(2)]
        var_ready = [sig(f"var_ready{w}", 1) for w in range(2)]
        rstd_ready = [sig(f"rstd_ready{w}", 1) for w in range(2)]
        xn_ready = [sig(f"xn_ready{w}", 1) for w in range(2)]
        halo_step = [sig(f"halo_step{w}", 2) for w in range(2)]
        xt_ready = sig("xt_ready", M)
        xt_taken = sig("xt_taken", M)
        pre_ready = {n: sig(f"pre_{n}", 2) for n in MIX}
        full_ready = {n: sig(f"full_{n}", 2) for n in MIX}
        hi_ready = {n: sig(f"hi_{n}", 2) for n in MIX if n != "kc"}
        lo_ready = {n: sig(f"lo_{n}", 2) for n in MIX if n != "kc"}
        used = {n: sig(f"used_{n}", 2, places=2 if n == "rc" else 0) for n in MIX if n != "kc"}
        k_ready = sig("k_ready", M)
        k_taken = sig("k_taken", M)
        v_ready = sig("v_ready", M)
        v_taken = sig("v_taken", M)
        r_ready = sig("r_ready", T)
        r_taken = sig("r_taken", T)
        step = sig("step", A_STEPS)
        ex_ready = sig("ex_ready", 2)
        ex_done = sig("ex_done", 2)
        s_ready = sig("s_ready", 2)
        ln_done = sig("ln_done", 2)
        dl_ready = sig("dl_ready", 2)
        z_ready = sig("z_ready", 2)
        z_done = sig("z_done", 2)
        share_done = sig("share_done", 2)
        wkv_ready = sig("wkv_ready", 2)
        ot_ready = sig("ot_ready", T)
        ot_taken = sig("ot_taken", T)
        x1_ready = sig("x1_ready", 1)
        xs_ready = sig("xs_ready", 1)
        xs_stored = [sig(f"xs_stored{b}", 1, places=1, unit=16, batches=1) for b in range(B)]
        h2_ready = sig("h2_ready", M, places=M)
        h2_taken = sig("h2_taken", M)
        rc_ready = sig("rc_ready", T)
        rc_taken = sig("rc_taken", T, places=T)
        kc_stored = [sig(f"kc_stored{s}", 1, places=1, unit=16) for s in range(2)]

        block = ctx.enter_context(nc.Block())

        LEAD = 3

        @block.sync
        def _(sp):
            def load_x(q, b):
                if not (isinstance(q, int) and q == 0 and b == 0):
                    xs_stored[b % B].place(sp, q, 0, 1 + b // B)
                sp.dma_start(x[:, b % B], io["x"][b % B, q + b // B].rearrange("(t p) c -> p t c", p=P)
                             ).then_inc(x_in[b % B].sem, 16)

            load_x(0, 0)
            sp.dma_start(ident[:], io["ident"]).then_inc(consts_in.sem, 16)
            sp.dma_start(cols[:], io["cols"]).then_inc(consts_in.sem, 16)
            for i, (name, to) in enumerate((("wk", k[:, 0]), ("wv", k[:, 1]), ("wr", v[:]), ("wrc", gate[:]))):
                sp.dma_start(to, io[name].rearrange("(m p) n -> p m n", p=P)).then_inc(raw_in[i].sem, 16)

            def period(q, b, more):
                if more:
                    load_x(q, b + 1)
                for o in range(O):
                    wt_used.place(sp, q, b, o + 1)
                    sp.dma_start(wt[:, o % SLOTS], io["w12"][b, q, o].rearrange("w p c -> p w c")
                                 ).then_inc(wt_in[o % SLOTS].sem, 16)

            with sp.Fori(0, Q - 1) as q:
                for b in range(B):
                    period(q, b, True)
            for b in range(B):
                period(Q - 1, b, b + 1 < B)

        @block.tensor
        def _(pe):
            def transposes(source, ready, free):
                for m in range(4):
                    free(m + 1)
                    for t in range(4):
                        last = nc.tensor.transpose(ring[m][:, t * P:(t + 1) * P],
                                                   source[:, t, m * P:(m + 1) * P], ident[:])
                    last.then_inc(ready.sem, 1)

            def joint_part(q, b, first, count):
                for o in range(first, first + count):
                    s = o % SLOTS
                    wt_lo_ready.item(pe, q, b, o + 1)
                    for m in range(M):
                        if o == 0:
                            joint_taken.place(pe, q, b, m + 1)
                        last = split_product(
                            nc, joint[m][:],
                            (wt_hi[:, s, 0, m * P:(m + 1) * P], wt_lo[:, s, 0, m * P:(m + 1) * P]),
                            (wt_hi[:, s, 1], wt_lo[:, s, 1]), o == 0, o == O - 1)
                        if o == O - 1:
                            last.then_inc(joint_ready.sem, 1)
                    if o == O - 1:
                        pe.drain().then_inc(wt_used.sem, 1)
                    else:
                        last.then_inc(wt_used.sem, 1)

            def mixed(q, b, name, w, rows, free, ready):
                for hf in range(2):
                    lo_ready[name].item(pe, q, b, hf + 1)
                    for n in range(4):
                        if hf == 0:
                            free(n + 1)
                        for i in range(HB):
                            kb = hf * HB + i
                            part = slice(n * P, (n + 1) * P)
                            act_parts = (mix_hi[:, hf, i], mix_lo[:, MIX[name][2], kb])
                            w_parts = (w_hi[:, w, kb], w_lo[:, w, kb])
                            if rows:
                                st, mvg = tuple(a[:, part] for a in act_parts), w_parts
                            else:
                                st, mvg = tuple(a[:, part] for a in w_parts), act_parts
                            last = split_product(nc, ring[n][:], st, mvg, kb == 0, kb == M - 1)
                        if hf == 1:
                            last.then_inc(ready.sem, 1)
                    if hf == 0:
                        last.then_inc(used[name].sem, 1)
                    else:
                        pe.drain().then_inc(used[name].sem, 1)

            for s in (used["rc"], wt_used, h2_ready):
                s.give_places(pe)
            pe.wait_ge(consts_in.sem, 32)
            xn_ready[0].item(pe, 0, 0, 1)
            transposes(xn, xt_ready, lambda n: None)
            pe.wait_ge(w_lo_ready.sem, 4)
            mixed(0, 0, "k", WK, False, lambda n: xt_taken.item(pe, 0, 0, n), k_ready)
            mixed(0, 0, "v", WV, False, lambda n: k_taken.item(pe, 0, 0, n), v_ready)
            mixed(0, 0, "r", WR, True, lambda n: v_taken.item(pe, 0, 0, n), r_ready)

            def period(q, b, more):
                nxt = b + 1

                def behind_products(n):
                    rc_taken.place(pe, q, b, n)
                    r_taken.item(pe, q, b, n)

                joint_part(q, b, 0, 3)
                if more:
                    xn_ready[0].item(pe, q, nxt, 1)
                    transposes(xn, xt_ready, behind_products)
                joint_part(q, b, 3, 2)
                if more:
                    mixed(q, nxt, "k", WK, False, lambda n: xt_taken.item(pe, q, nxt, n), k_ready)
                joint_part(q, b, 5, 2)
                wkv_ready.item(pe, q, b, 2)
                transposes(v, ot_ready, (lambda n: k_taken.item(pe, q, nxt, n)) if more else behind_products)
                joint_part(q, b, 7, 2)
                if more:
                    mixed(q, nxt, "v", WV, False, lambda n: ot_taken.item(pe, q, b, n), v_ready)
                joint_part(q, b, 9, 1)
                xn_ready[1].item(pe, q, b, 1)
                transposes(xn, h2_ready, (lambda n: v_taken.item(pe, q, nxt, n)) if more
                           else (lambda n: ot_taken.item(pe, q, b, n)))
                joint_part(q, b, 10, 2)
                if more:
                    mixed(q, nxt, "r", WR, True, lambda n: h2_taken.item(pe, q, b, n), r_ready)
                joint_part(q, b, 12, 4)
                mixed(q, b, "rc", WRC, True, (lambda n: r_taken.item(pe, q, nxt, n)) if more
                      else (lambda n: h2_taken.item(pe, q, b, n)), rc_ready)

            with pe.Fori(0, Q - 1) as q:
                for b in range(B):
                    period(q, b, True)
            for b in range(B):
                period(Q - 1, b, b + 1 < B)

        @block.scalar
        def _(act):
            def wt_high(q, b, first, count, more):
                for o in range(first, first + count if more else min(first + count, O)):
                    wt_in[o % SLOTS].item(act, q, b, o // SLOTS + 1)
                    nc.scalar.copy(wt_hi[:, o % SLOTS], wt[:, o % SLOTS]).then_inc(wt_hi_ready.sem, 1)

            def pre(q, b, name, free):
                which, _, pair = MIX[name]
                for hf in range(2):
                    free(hf)
                    for i in range(HB):
                        m = hf * HB + i
                        ins = nc.scalar.mul(mixf[:, pair, m], h[:, which, m, 0:N], rest[:, REST[name], m:m + 1])
                    ins.then_inc(pre_ready[name].sem, 1)

            def high(q, b, name, hf, free):
                full_ready[name].item(act, q, b, hf + 1)
                free(hf)
                pair = MIX[name][2]
                nc.scalar.copy(mix_hi[:, hf], mixf[:, pair, hf * HB:(hf + 1) * HB]).then_inc(hi_ready[name].sem, 1)

            def to_h(q, b, ready, taken, which, g, beta):
                nc.scalar.copy(h[:, which, :, 0], h_last[:, which, b % B]).then_inc(halo_step[which].sem, 1)
                for m in range(M):
                    ready.item(act, q, b, m + 1)
                    nc.scalar.activation(h[:, which, m, 1:], ring[m][:], ACT.Identity, scale=col(g, m),
                                         bias=col(beta, m)).then_inc(taken.sem, 1)
                taken.item(act, q, b, M)
                halo_step[which].item(act, q, b, 1)
                nc.scalar.copy(h_last[:, which, b % B], h[:, which, :, N]).then_inc(halo_step[which].sem, 1)

            def take(q, b, ready, taken, to, free=lambda m: None):
                for m in range(M):
                    free(m)
                    ready.item(act, q, b, m + 1)
                    nc.scalar.copy(to[:, m], ring[m][:]).then_inc(taken.sem, 1)

            def take_r(q, b):
                for t in range(T):
                    r_ready.item(act, q, b, t + 1)
                    nc.scalar.activation(gate[:, t], ring[t][:], ACT.Sigmoid).then_inc(r_taken.sem, 1)

            def exp_under_max(q, b, hf):
                ex_ready.item(act, q, b, hf + 1)
                nc.scalar.activation(ee[:], ee[:], ACT.Exp).then_inc(ex_done.sem, 1)

            def log_of_sum(q, b, hf):
                s_ready.item(act, q, b, hf + 1)
                nc.scalar.activation(pp[:, :, 1:], ee[:, 1], ACT.Ln).then_inc(ln_done.sem, 1)

            def exp_and_share(q, b, hf):
                z_ready.item(act, q, b, hf + 1)
                nc.scalar.activation(ee[:], ee[:], ACT.Exp).then_inc(z_done.sem, 1)
                for i in range(HB):
                    ins = nc.scalar.activation(dl[:, i], dl[:, i], ACT.Sigmoid, scale=-1.0,
                                               bias=col("first", hf * HB + i))
                ins.then_inc(share_done.sem, 1)

            act.wait_ge(consts_in.sem, 32)
            for i, raw in enumerate((k[:, 0], k[:, 1], v[:], gate[:])):
                act.wait_ge(raw_in[i].sem, 16)
                nc.scalar.copy(w_hi[:, i], raw).then_inc(w_hi_ready.sem, 1)
            for s in (joint_taken, rc_taken, *wc_stored, *rc_stored, *xs_stored, *kc_stored):
                s.give_places(act)
            act.wait_ge(state_ready.sem, 6)
            wt_high(0, 0, 0, LEAD, True)
            to_h(0, 0, xt_ready, xt_taken, 0, "ln1_g", "ln1_b")
            act.wait_ge(w_lo_ready.sem, 4)
            pre(0, 0, "k", lambda hf: None)
            pre(0, 0, "v", lambda hf: None)
            high(0, 0, "k", 0, lambda hf: None)
            high(0, 0, "k", 1, lambda hf: None)
            take(0, 0, k_ready, k_taken, k[:, 0])
            high(0, 0, "v", 0, lambda hf: used["k"].item(act, 0, 0, hf + 1))
            high(0, 0, "v", 1, lambda hf: used["k"].item(act, 0, 0, hf + 1))
            pre(0, 0, "r", lambda hf: used["k"].item(act, 0, 0, hf + 1))
            exp_under_max(0, 0, 0)
            take(0, 0, v_ready, v_taken, v)
            high(0, 0, "r", 0, lambda hf: used["v"].item(act, 0, 0, hf + 1))
            log_of_sum(0, 0, 0)
            high(0, 0, "r", 1, lambda hf: used["v"].item(act, 0, 0, hf + 1))
            exp_and_share(0, 0, 0)
            take_r(0, 0)

            def period(q, b, more):
                nxt = b + 1

                def rc_used(hf):
                    used["rc"].place(act, q, b, hf + 1)

                def kc_out(hf):
                    kc_stored[hf].place(act, q, b, 1)

                def product_done(name, c):
                    return lambda hf: used[name].item(act, q, c, hf + 1)

                wt_high(q, b, 3, 1, more)
                exp_under_max(q, b, 1)
                wt_high(q, b, 4, 1, more)
                if more:
                    to_h(q, nxt, xt_ready, xt_taken, 0, "ln1_g", "ln1_b")
                    pre(q, nxt, "k", rc_used)
                log_of_sum(q, b, 1)
                wt_high(q, b, 5, 1, more)
                if more:
                    high(q, nxt, "k", 0, rc_used)
                    high(q, nxt, "k", 1, rc_used)
                wt_high(q, b, 6, 1, more)
                exp_and_share(q, b, 1)
                if more:
                    pre(q, nxt, "v", kc_out)
                wt_high(q, b, 7, 2, more)
                if more:
                    take(q, nxt, k_ready, k_taken, k[:, nxt % B],
                         lambda m: wc_stored[m].place(act, q, b, 1))
                wt_high(q, b, 9, 1, more)
                if more:
                    high(q, nxt, "v", 0, product_done("k", nxt))
                    high(q, nxt, "v", 1, product_done("k", nxt))
                    pre(q, nxt, "r", product_done("k", nxt))
                wt_high(q, b, 10, 2, more)
                if more:
                    exp_under_max(q, nxt, 0)
                    log_of_sum(q, nxt, 0)
                wt_high(q, b, 12, 1, more)
                if more:
                    take(q, nxt, v_ready, v_taken, v)
                    high(q, nxt, "r", 0, product_done("v", nxt))
                    high(q, nxt, "r", 1, product_done("v", nxt))
                to_h(q, b, h2_ready, h2_taken, 1, "ln2_g", "ln2_b")
                if more:
                    exp_and_share(q, nxt, 0)
                xs_ready.item(act, q, b, 1)
                act.dma_start(scratch["xs"][b * Q + q], x[:, b]).then_inc(xs_stored[b].sem, 16)
                pre(q, b, "kc", product_done("v", nxt if more else b))
                wt_high(q, b, 13, 3, more)
                if more:
                    take_r(q, nxt)
                pre(q, b, "rc", product_done("r", nxt if more else b))
                for hf in range(2):
                    high(q, b, "rc", hf, product_done("r", nxt if more else b))
                for hf in range(2):
                    full_ready["kc"].item(act, q, b, hf + 1)
                    act.dma_start(scratch["kc"][b * Q + q, hf], mixf[:, 1, hf * HB:(hf + 1) * HB]
                                  ).then_inc(kc_stored[hf].sem, 16)
                for m in range(M):
                    joint_ready.item(act, q, b, m + 1)
                    nc.scalar.copy(k[:, b, m], joint[m][:]).then_inc(joint_taken.sem, 1)
                    joint_taken.item(act, q, b, m + 1)
                    act.dma_start(scratch["wc"][b * Q + q, m], k[:, b, m]).then_inc(wc_stored[m].sem, 16)
                wt_high(q, b, O, LEAD, more)
                for t in range(T):
                    rc_ready.item(act, q, b, t + 1)
                    rc_stored[t % 2].place(act, q, b, t // 2 + 1)
                    nc.scalar.activation(going[:, t % 2], ring[t][:], ACT.Sigmoid).then_inc(rc_taken.sem, 1)
                    rc_taken.item(act, q, b, t + 1)
                    act.dma_start(scratch["rc"][b * Q + q, t], going[:, t % 2]).then_inc(rc_stored[t % 2].sem, 16)

            with act.Fori(0, Q - 1) as q:
                for b in range(B):
                    period(q, b, True)
            for b in range(B):
                period(Q - 1, b, b + 1 < B)
            for s in rc_stored:
                act.wait_ge(s.sem, 16 * (1 + B * Q * T // 2))
            for s in wc_stored:
                act.wait_ge(s.sem, 16 * (1 + B * Q))
            for s in xs_stored:
                act.wait_ge(s.sem, 16 * (1 + Q))
            for s in kc_stored:
                act.wait_ge(s.sem, 16 * (1 + B * Q))

        @block.gpsimd
        def _(pool):
            nc.gpsimd.memset(half_neg[:], -0.5).then_inc(half_ready.sem, 1)
            pool.wait_ge(half_ready.sem, 1)

            def root(q, b, which):
                var_ready[which].item(pool, q, b, 1)
                nc.gpsimd.tensor_tensor(rstd[:], veps[:], half_neg[:], ALU.pow).then_inc(rstd_ready[which].sem, 1)

            def wt_low(q, b, first, count):
                for o in range(first, first + count):
                    wt_hi_ready.item(pool, q, b, o + 1)
                    nc.gpsimd.tensor_tensor(wt_lo[:, o % SLOTS], wt[:, o % SLOTS], wt_hi[:, o % SLOTS].bitcast(F32),
                                            ALU.subtract).then_inc(wt_lo_ready.sem, 1)

            def period(q, b, more):
                if more:
                    root(q, b + 1, 0)
                wt_low(q, b, 0, 12)
                root(q, b, 1)
                nc.gpsimd.tensor_tensor(x[:, b], x[:, b], gate[:], ALU.add).then_inc(xs_ready.sem, 1)
                wt_low(q, b, 12, 4)

            root(0, 0, 0)
            with pool.Fori(0, Q - 1) as q:
                for b in range(B):
                    period(q, b, True)
            for b in range(B):
                period(Q - 1, b, b + 1 < B)

        @block.vector
        def _(dve):
            def chain(sig, q, b, from_=0):
                done = [from_]

                def then(ins):
                    ins.then_inc(sig.sem, 1)
                    done[0] += 1
                    sig.item(dve, q, b, done[0])
                then.done = done
                return then

            def norm_front(q, b, which, source):
                then = chain(ln_step[which], q, b)
                for t in range(T):
                    ins = nc.vector.bn_stats(stats[:, t], source[:, t])
                then(ins)
                nc.vector.memset(veps[:], LN_EPS)
                for t in range(T):
                    ins = nc.vector.bn_aggr(mv[:, t], stats[:, t])
                then(ins)
                nc.vector.tensor_tensor(veps[:], mv[:, :, 1], veps[:], ALU.add).then_inc(var_ready[which].sem, 1)

            def norm_back(q, b, which, source):
                rstd_ready[which].item(dve, q, b, 1)
                for t in range(T):
                    ins = nc.vector.tensor_scalar(xn[:, t], source[:, t], mv[:, t, 0:1], rstd[:, t:t + 1],
                                                  ALU.subtract, ALU.mult)
                ins.then_inc(xn_ready[which].sem, 1)

            def mix(q, b, name, hf):
                which, ratio, pair = MIX[name]
                pre_ready[name].item(dve, q, b, hf + 1)
                for i in range(HB):
                    m = hf * HB + i
                    place = mixf[:, pair, m]
                    ins = nc.vector.scalar_tensor_tensor(place, h[:, which, m, 1:], col(ratio, m), place,
                                                         ALU.mult, ALU.add)
                ins.then_inc(full_ready[name].sem, 1)

            def low(q, b, name, hf):
                pair = MIX[name][2]
                hi_ready[name].item(dve, q, b, hf + 1)
                mine = slice(hf * HB, (hf + 1) * HB)
                nc.vector.tensor_tensor(mix_lo[:, pair, mine], mixf[:, pair, mine],
                                        mix_hi[:, hf].bitcast(F32), ALU.subtract).then_inc(lo_ready[name].sem, 1)

            def mix_and_low(q, b, name):
                mix(q, b, name, 0)
                mix(q, b, name, 1)
                low(q, b, name, 0)
                low(q, b, name, 1)

            for tile, value in ((h_last, 0.0), (m_last, LEAST), (s_last, 0.0), (p_last, LEAST), (a_last, 0.0)):
                nc.vector.memset(tile[:], value).then_inc(state_ready.sem, 1)
            x_in[0].item(dve, 0, 0, 1)
            norm_front(0, 0, 0, x[:, 0])
            norm_back(0, 0, 0, x[:, 0])
            dve.wait_ge(consts_in.sem, 32)
            for name, (_, ratio, _) in MIX.items():
                first = COLS.index(ratio) * M
                ins = nc.vector.tensor_scalar(rest[:, REST[name]], cols[:, first:first + M], -1.0, 1.0,
                                              ALU.mult, ALU.add)
            ins.then_inc(state_ready.sem, 1)
            for i, raw in enumerate((k[:, 0], k[:, 1], v[:], gate[:])):
                dve.wait_ge(raw_in[i].sem, 16)
                dve.wait_ge(w_hi_ready.sem, i + 1)
                nc.vector.tensor_tensor(w_lo[:, i], raw, w_hi[:, i].bitcast(F32), ALU.subtract
                                        ).then_inc(w_lo_ready.sem, 1)
            dve.wait_ge(state_ready.sem, 6)
            mix_and_low(0, 0, "k")
            mix_and_low(0, 0, "v")

            def recurrence_of(q, b, from_):
                then = chain(step, q, b, from_)
                bb = b % B
                kb = k[:, bb]

                def under_max(hf):
                    mine = slice(hf * HB, (hf + 1) * HB)
                    k_taken.item(dve, q, b, (hf + 1) * HB)
                    nc.vector.tensor_copy(mx[:, :, 0], m_last[:, bb, mine])
                    for i in range(HB):
                        ins = nc.vector.tensor_tensor_scan(mx[:, i, 1:], kb[:, hf * HB + i], kb[:, hf * HB + i],
                                                           m_last[:, bb, hf * HB + i:hf * HB + i + 1],
                                                           ALU.max, ALU.max)
                    then(ins)
                    nc.vector.tensor_tensor(ee[:, 0], mx[:, :, 0:N], mx[:, :, 1:], ALU.subtract)
                    nc.vector.tensor_tensor(ee[:, 1], kb[:, mine], mx[:, :, 1:], ALU.subtract
                                            ).then_inc(ex_ready.sem, 1)
                    nc.vector.tensor_copy(m_last[:, bb, mine], mx[:, :, N])

                def running_sum(hf):
                    mine = slice(hf * HB, (hf + 1) * HB)
                    ex_done.item(dve, q, b, hf + 1)
                    for i in range(HB):
                        ins = nc.vector.tensor_tensor_scan(ee[:, 1, i], ee[:, 0, i], ee[:, 1, i],
                                                           s_last[:, bb, hf * HB + i:hf * HB + i + 1],
                                                           ALU.mult, ALU.add)
                    ins.then_inc(s_ready.sem, 1)
                    s_ready.item(dve, q, b, hf + 1)
                    nc.vector.tensor_copy(s_last[:, bb, mine], ee[:, 1, :, N - 1])
                    then(nc.vector.tensor_copy(pp[:, :, 0], p_last[:, bb, mine]))

                def exponents(hf):
                    mine = slice(hf * HB, (hf + 1) * HB)
                    ln_done.item(dve, q, b, hf + 1)
                    then(nc.vector.tensor_tensor(pp[:, :, 1:], pp[:, :, 1:], mx[:, :, 1:], ALU.add))
                    nc.vector.tensor_copy(p_last[:, bb, mine], pp[:, :, N])
                    nc.vector.tensor_tensor(dl[:], pp[:, :, 0:N], kb[:, mine], ALU.subtract
                                            ).then_inc(dl_ready.sem, 1)
                    dl_ready.item(dve, q, b, hf + 1)
                    nc.vector.tensor_scalar(ee[:, 0], dl[:], 0.0, None, ALU.min)
                    nc.vector.tensor_scalar(ee[:, 1], dl[:], -1.0, 0.0, ALU.mult, ALU.min
                                            ).then_inc(z_ready.sem, 1)
                    nc.vector.tensor_copy(aa[:, :, 0], a_last[:, bb, mine])

                def recurrence(hf):
                    mine = slice(hf * HB, (hf + 1) * HB)
                    z_done.item(dve, q, b, hf + 1)
                    v_taken.item(dve, q, b, (hf + 1) * HB)
                    then(nc.vector.tensor_tensor(ee[:, 1], ee[:, 1], v[:, mine], ALU.mult))
                    for i in range(HB):
                        ins = nc.vector.tensor_tensor_scan(aa[:, i, 1:], ee[:, 0, i], ee[:, 1, i],
                                                           a_last[:, bb, hf * HB + i:hf * HB + i + 1],
                                                           ALU.mult, ALU.add)
                    then(ins)
                    nc.vector.tensor_copy(a_last[:, bb, mine], aa[:, :, N])
                    then(nc.vector.tensor_tensor(v[:, mine], v[:, mine], aa[:, :, 0:N], ALU.subtract))
                    share_done.item(dve, q, b, hf + 1)
                    then(nc.vector.tensor_tensor(v[:, mine], v[:, mine], dl[:], ALU.mult))
                    nc.vector.tensor_tensor(v[:, mine], v[:, mine], aa[:, :, 0:N], ALU.add
                                            ).then_inc(wkv_ready.sem, 1)
                    wkv_ready.item(dve, q, b, hf + 1)

                return under_max, running_sum, exponents, recurrence, then

            def opening(q, b):
                under_max, running_sum, exponents, _, then = recurrence_of(q, b, 0)
                return lambda: under_max(0), lambda: running_sum(0), lambda: exponents(0)

            first_under_max, first_running_sum, first_exponents = opening(0, 0)
            first_under_max()
            mix(0, 0, "r", 0)
            mix(0, 0, "r", 1)
            first_running_sum()
            low(0, 0, "r", 0)
            low(0, 0, "r", 1)
            first_exponents()

            def period(q, b, more):
                nxt = b + 1
                under_max, running_sum, exponents, recurrence, then = recurrence_of(q, b, OPENING_LINKS)
                if more:
                    x_in[nxt % B].item(dve, q, 0, 1 + nxt // B)
                    norm_front(q, nxt, 0, x[:, nxt % B])
                recurrence(0)
                if more:
                    h2_ready.place(dve, q, b, M)
                    norm_back(q, nxt, 0, x[:, nxt % B])
                under_max(1)
                running_sum(1)
                if more:
                    mix(q, nxt, "k", 0)
                    mix(q, nxt, "k", 1)
                exponents(1)
                if more:
                    low(q, nxt, "k", 0)
                    low(q, nxt, "k", 1)
                recurrence(1)
                if more:
                    mix(q, nxt, "v", 0)
                    mix(q, nxt, "v", 1)
                for t in range(T):
                    ot_ready.item(dve, q, b, t + 1)
                    r_taken.item(dve, q, b, t + 1)
                    nc.vector.tensor_tensor(gate[:, t], gate[:, t], ring[t][:], ALU.mult
                                            ).then_inc(ot_taken.sem, 1)
                if more:
                    next_under_max, next_running_sum, next_exponents = opening(q, nxt)
                    low(q, nxt, "v", 0)
                    low(q, nxt, "v", 1)
                    next_under_max()
                ot_taken.item(dve, q, b, T)
                nc.vector.tensor_tensor(gate[:], gate[:], x[:, b], ALU.add).then_inc(x1_ready.sem, 1)
                x1_ready.item(dve, q, b, 1)
                norm_front(q, b, 1, gate)
                if more:
                    next_running_sum()
                xt_ready.item(dve, q, nxt if more else b, M)
                norm_back(q, b, 1, gate)
                if more:
                    mix(q, nxt, "r", 0)
                    mix(q, nxt, "r", 1)
                    low(q, nxt, "r", 0)
                    low(q, nxt, "r", 1)
                    next_exponents()
                mix(q, b, "kc", 0)
                mix(q, b, "kc", 1)
                mix_and_low(q, b, "rc")
                assert then.done[0] == A_STEPS, then.done[0]

            with dve.Fori(0, Q - 1) as q:
                for b in range(B):
                    period(q, b, True)
            for b in range(B):
                period(Q - 1, b, b + 1 < B)
    clear(nc, semaphores)


def phase_b(nc, io, scratch):
    semaphores = []
    with ExitStack() as ctx:
        def sb(name, shape, dt=F32):
            return ctx.enter_context(nc.sbuf_tensor("b_" + name, shape, dt))

        def sig(name, *args, **kw):
            semaphores.append(nc.alloc_semaphore(name="b_" + name))
            return Signal(semaphores[-1], *args, **kw)

        wk_hi = sb("wk_hi", [P, O // M, M, C], F32R)
        wk_lo = sb("wk_lo", [P, O // M, M, C], F32R)
        wv_hi = sb("wv_hi", [P, O, C], F32R)
        wv_lo = sb("wv_lo", [P, O, C], F32R)
        ones = sb("ones", [P, P])
        half_neg = sb("half_neg", [P, T])
        raw = sb("raw", [P, M, N])
        in_hi = sb("in_hi", [P, M, N], F32R)
        in_lo = sb("in_lo", [P, M, N], F32R)
        relu = sb("relu", [P, 2, N])
        sq = sb("sq", [P, 2, N])
        sq_hi = sb("sq_hi", [P, 4, N], F32R)
        sq_lo = sb("sq_lo", [P, 4, N], F32R)
        rc = sb("rc", [P, 2, C])
        xs = sb("xs", [P, 2, C])
        y = sb("y", [P, T, C])
        stats = sb("stats", [P, T, 6])
        mv = sb("mv", [P, T, 2])
        veps = sb("veps", [P, T])
        rstd = sb("rstd", [P, T])
        w2 = sb("w2", [P, 2, C])
        b1 = sb("b1", [P, B, O])
        b2 = sb("b2", [1, B, C])
        acc = sb("acc", [P, C])
        bias_row = sb("bias_row", [1, C])

        wide = [ctx.enter_context(nc.psum_tensor(f"b_wide{i}", [P, 512], F32)) for i in range(2)]
        back = [ctx.enter_context(nc.psum_tensor(f"b_back{i}", [P, 512], F32)) for i in range(T)]
        bias_sum = ctx.enter_context(nc.psum_tensor("b_bias_sum", [P, 512], F32))

        PIECES = 2 * O // M
        piece_in = [sig(f"piece_in{i}") for i in range(2)]
        piece_hi = sig("piece_hi")
        piece_lo = sig("piece_lo")
        ones_ready = sig("ones_ready")
        half_ready = sig("half_ready")

        raw_in = [sig(f"raw_in{i}", 1, unit=16) for i in range(2)]
        in_hi_ready = sig("in_hi_ready", 2)
        in_lo_ready = sig("in_lo_ready", 2, places=2)
        wide_ready = sig("wide_ready", O, places=O)
        relu_done = sig("relu_done", O, places=2)
        sq_done = sig("sq_done", O, places=2)
        sq_hi_ready = sig("sq_hi_ready", O)
        sq_lo_ready = sig("sq_lo_ready", O)
        sq_used = sig("sq_used", O, places=4)
        back_ready = sig("back_ready", T)
        back_taken = sig("back_taken", T, places=T)
        rc_in = [sig(f"rc_in{i}", T // 2, unit=16) for i in range(2)]
        xs_in = [sig(f"xs_in{i}", T // 2, unit=16) for i in range(2)]
        tile_done = sig("tile_done", T, places=2)
        step = sig("step", 2)
        var_ready = sig("var_ready", 1)
        rstd_ready = sig("rstd_ready", 1)
        x2_ready = sig("x2_ready", 1)
        x2_stored = sig("x2_stored", 1, places=1, unit=16)
        b_in = [sig(f"b_in{b}", 2, unit=16, batches=1) for b in range(B)]
        w2_in = [sig(f"w2_in{i}", O // 2, unit=16) for i in range(2)]
        acc_step = sig("acc_step", O, places=2)
        bias_summed = sig("bias_summed", 1, places=1)
        bias_out = sig("bias_out", 1, places=1)
        bias_stored = sig("bias_stored", 1, places=1, unit=16)

        def w2_at(o):
            return 4 + o // 2

        block = ctx.enter_context(nc.Block())

        @block.sync
        def _(sp):
            for i in range(PIECES):
                stage = (raw, y)[i % 2]
                if i >= 2:
                    sp.wait_ge(piece_lo.sem, i - 1)
                j = i // 2
                if i % 2 == 0:
                    src = io["wkc"][:, j * C:(j + 1) * C].rearrange("(m p) n -> p m n", p=P)
                else:
                    src = io["wvc"][j * M * P:(j + 1) * M * P].rearrange("(m p) n -> p m n", p=P)
                sp.dma_start(stage[:], src).then_inc(piece_in[i % 2].sem, 16)
            sp.wait_ge(piece_lo.sem, PIECES)
            for hf in range(2):
                sp.dma_start(raw[:, hf * HB:(hf + 1) * HB], scratch["kc"][0, hf]).then_inc(raw_in[hf].sem, 16)
            with sp.Fori(0, Q) as q:
                for b in range(B):
                    g = q + b * Q
                    acc_step.place(sp, q, b, 2)
                    sp.dma_start(b1[:, b], io["b1"][b, q]).then_inc(b_in[b].sem, 16)
                    bias_summed.place(sp, q, b, 1)
                    sp.dma_start(b2[:, b], io["b2"][b, q]).then_inc(b_in[b].sem, 16)
                    for hf in range(2):
                        in_lo_ready.item(sp, q, b, hf + 1)
                        nxt = q + Q if b == 0 else q + 1
                        sp.dma_start(raw[:, hf * HB:(hf + 1) * HB], scratch["kc"][nxt, hf]
                                     ).then_inc(raw_in[hf].sem, 16)
                    for o in range(O):
                        acc_step.place(sp, q, b, o + 1)
                        sp.dma_start(w2[:, o % 2], io["w12"][b, q, o, 1]).then_inc(w2_in[o % 2].sem, 16)
                    for t in range(T):
                        tile_done.place(sp, q, b, t + 1)
                        sp.dma_start(rc[:, t % 2], scratch["rc"][g, t]).then_inc(rc_in[t % 2].sem, 16)
                        sp.dma_start(xs[:, t % 2], scratch["xs"][g, :, t]).then_inc(xs_in[t % 2].sem, 16)
                    x2_ready.item(sp, q, b, 1)
                    sp.dma_start(scratch["x2"][g], y[:]).then_inc(x2_stored.sem, 16)
            sp.wait_ge(x2_stored.sem, 16 * (1 + B * Q))
            for hf in range(2):
                sp.wait_ge(raw_in[hf].sem, 16 * (1 + B * Q))

        @block.tensor
        def _(pe):
            for s in (wide_ready, sq_used, bias_summed):
                s.give_places(pe)
            pe.wait_ge(piece_lo.sem, PIECES)
            pe.wait_ge(ones_ready.sem, 1)
            with pe.Fori(0, Q) as q:
                for b in range(B):
                    def widen(o):
                        relu_done.place(pe, q, b, o + 1)
                        for m in range(M):
                            if o == 0 and m % HB == 0:
                                in_lo_ready.item(pe, q, b, m // HB + 1)
                            part = slice((o % M) * P, (o % M + 1) * P)
                            last = split_product(nc, wide[o % 2][:],
                                                 (wk_hi[:, o // M, m, part], wk_lo[:, o // M, m, part]),
                                                 (in_hi[:, m], in_lo[:, m]), m == 0, m == M - 1)
                        last.then_inc(wide_ready.sem, 1)

                    def narrow(o):
                        sq_lo_ready.item(pe, q, b, o + 1)
                        for t in range(T):
                            if o == 0:
                                back_taken.place(pe, q, b, t + 1)
                            part = slice(t * P, (t + 1) * P)
                            last = split_product(nc, back[t][:],
                                                 (sq_hi[:, o % 4, part], sq_lo[:, o % 4, part]),
                                                 (wv_hi[:, o], wv_lo[:, o]), o == 0, o == O - 1)
                            if o == O - 1:
                                last.then_inc(back_ready.sem, 1)
                        if o == O - 1:
                            pe.drain().then_inc(sq_used.sem, 1)
                        else:
                            last.then_inc(sq_used.sem, 1)

                    for o in range(O):
                        widen(o)
                        if o >= 2:
                            narrow(o - 2)
                        if o == 14:
                            acc_step.item(pe, q, b, O)
                            b_in[b].item(pe, q, 0, 2)
                            bias_out.place(pe, q, b, 1)
                            nc.tensor.matmul(bias_sum[:], ones[:], acc[:], start=True, stop=False)
                            nc.tensor.matmul(bias_sum[:], ones[0:1, :], b2[:, b], start=False, stop=True
                                             ).then_inc(bias_summed.sem, 1)
                    narrow(O - 2)
                    narrow(O - 1)

        @block.scalar
        def _(act):
            for i in range(PIECES):
                act.wait_ge(piece_in[i % 2].sem, 16 * (i // 2 + 1))
                stage, to = ((raw, wk_hi[:, i // 2]), (y, wv_hi[:, i // 2 * M:(i // 2 + 1) * M]))[i % 2]
                nc.scalar.copy(to, stage[:]).then_inc(piece_hi.sem, 1)
            for s in (relu_done, bias_out, bias_stored):
                s.give_places(act)
            with act.Fori(0, Q) as q:
                for b in range(B):
                    for hf in range(2):
                        mine = slice(hf * HB, (hf + 1) * HB)
                        raw_in[hf].item(act, q, b, 1)
                        if hf == 0:
                            wide_ready.place(act, q, b, O)
                        nc.scalar.copy(in_hi[:, mine], raw[:, mine]).then_inc(in_hi_ready.sem, 1)
                    for o in range(O):
                        wide_ready.item(act, q, b, o + 1)
                        sq_done.place(act, q, b, o + 1)
                        nc.scalar.activation(relu[:, o % 2], wide[o % 2][:], ACT.Relu).then_inc(relu_done.sem, 1)
                        relu_done.item(act, q, b, o + 1)
                        sq_used.place(act, q, b, o + 1)
                        nc.scalar.activation(sq_hi[:, o % 4], relu[:, o % 2], ACT.Square
                                             ).then_inc(sq_hi_ready.sem, 1)
                    bias_summed.item(act, q, b, 1)
                    bias_stored.place(act, q, b, 1)
                    nc.scalar.copy(bias_row[:], bias_sum[0:1, :]).then_inc(bias_out.sem, 1)
                    bias_out.item(act, q, b, 1)
                    act.dma_start(scratch["bias"][q + b * Q], bias_row[:]).then_inc(bias_stored.sem, 16)
            act.wait_ge(bias_stored.sem, 16 * (1 + B * Q))

        @block.gpsimd
        def _(pool):
            in_lo_ready.give_places(pool)
            nc.gpsimd.memset(half_neg[:], -0.5).then_inc(half_ready.sem, 1)
            pool.wait_ge(half_ready.sem, 1)
            with pool.Fori(0, Q) as q:
                for b in range(B):
                    for hf in range(2):
                        mine = slice(hf * HB, (hf + 1) * HB)
                        in_hi_ready.item(pool, q, b, hf + 1)
                        nc.gpsimd.tensor_tensor(in_lo[:, mine], raw[:, mine], in_hi[:, mine].bitcast(F32),
                                                ALU.subtract).then_inc(in_lo_ready.sem, 1)
                    var_ready.item(pool, q, b, 1)
                    nc.gpsimd.tensor_tensor(rstd[:], veps[:], half_neg[:], ALU.pow).then_inc(rstd_ready.sem, 1)

        @block.vector
        def _(dve):
            for i in range(PIECES):
                stage, hi, lo = ((raw, wk_hi[:, i // 2], wk_lo[:, i // 2]),
                                 (y, wv_hi[:, i // 2 * M:(i // 2 + 1) * M],
                                  wv_lo[:, i // 2 * M:(i // 2 + 1) * M]))[i % 2]
                dve.wait_ge(piece_hi.sem, i + 1)
                dve.wait_ge(piece_in[i % 2].sem, 16 * (i // 2 + 1))
                nc.vector.tensor_tensor(lo, stage[:], hi.bitcast(F32), ALU.subtract).then_inc(piece_lo.sem, 1)
            nc.vector.memset(ones[:], 1.0).then_inc(ones_ready.sem, 1)
            for s in (sq_done, back_taken, tile_done, acc_step):
                s.give_places(dve)
            dve.wait_ge(piece_lo.sem, PIECES)
            x2_stored.give_places(dve)
            with dve.Fori(0, Q) as q:
                for b in range(B):
                    for o in range(O):
                        relu_done.item(dve, q, b, o + 1)
                        if o >= 2:
                            sq_lo_ready.item(dve, q, b, o - 1)
                        nc.vector.tensor_tensor(sq[:, o % 2], relu[:, o % 2], relu[:, o % 2], ALU.mult
                                                ).then_inc(sq_done.sem, 1)
                        for w in range(O):
                            if w2_at(w) != o:
                                continue
                            w2_in[w % 2].item(dve, q, b, w // 2 + 1)
                            column = b1[:, b, w:w + 1]
                            if w == 0:
                                b_in[b].item(dve, q, 0, 2)
                                bias_summed.place(dve, q, b, 1)
                                nc.vector.tensor_scalar(acc[:], w2[:, 0], column, None, ALU.mult
                                                        ).then_inc(acc_step.sem, 1)
                            else:
                                acc_step.item(dve, q, b, w)
                                nc.vector.scalar_tensor_tensor(acc[:], w2[:, w % 2], column, acc[:],
                                                               ALU.mult, ALU.add).then_inc(acc_step.sem, 1)
                        sq_done.item(dve, q, b, o + 1)
                        sq_hi_ready.item(dve, q, b, o + 1)
                        nc.vector.tensor_tensor(sq_lo[:, o % 4], sq[:, o % 2], sq_hi[:, o % 4].bitcast(F32),
                                                ALU.subtract).then_inc(sq_lo_ready.sem, 1)
                    x2_stored.place(dve, q, b, 1)
                    for t in range(T + 1):
                        if t < T:
                            back_ready.item(dve, q, b, t + 1)
                            rc_in[t % 2].item(dve, q, b, t // 2 + 1)
                            nc.vector.tensor_tensor(y[:, t], rc[:, t % 2], back[t][:], ALU.mult
                                                    ).then_inc(back_taken.sem, 1)
                        if t >= 1:
                            back_taken.item(dve, q, b, t)
                            xs_in[(t - 1) % 2].item(dve, q, b, (t - 1) // 2 + 1)
                            nc.vector.tensor_tensor(y[:, t - 1], y[:, t - 1], xs[:, (t - 1) % 2], ALU.add
                                                    ).then_inc(tile_done.sem, 1)
                    for t in range(T):
                        tile_done.item(dve, q, b, t + 1)
                        ins = nc.vector.bn_stats(stats[:, t], y[:, t])
                    ins.then_inc(step.sem, 1)
                    step.item(dve, q, b, 1)
                    nc.vector.memset(veps[:], LN_EPS)
                    for t in range(T):
                        ins = nc.vector.bn_aggr(mv[:, t], stats[:, t])
                    ins.then_inc(step.sem, 1)
                    step.item(dve, q, b, 2)
                    nc.vector.tensor_tensor(veps[:], mv[:, :, 1], veps[:], ALU.add).then_inc(var_ready.sem, 1)
                    rstd_ready.item(dve, q, b, 1)
                    for t in range(T):
                        ins = nc.vector.tensor_scalar(y[:, t], y[:, t], mv[:, t, 0:1], rstd[:, t:t + 1],
                                                      ALU.subtract, ALU.mult)
                    ins.then_inc(x2_ready.sem, 1)
    clear(nc, semaphores)


def phase_c(nc, io, scratch, out):
    semaphores = []
    with ExitStack() as ctx:
        def sb(name, shape, dt=F32):
            return ctx.enter_context(nc.sbuf_tensor("c_" + name, shape, dt))

        def sig(name, *args, **kw):
            semaphores.append(nc.alloc_semaphore(name="c_" + name))
            return Signal(semaphores[-1], *args, **kw)

        G = M
        PG = 2
        STEPS = T * G // PG
        PH = PG * HG
        ROWS = [min(P, GK - j * P) for j in range(KC)]

        wq_hi, wq_lo = sb("wq_hi", [P, M, C], F32R), sb("wq_lo", [P, M, C], F32R)
        wo_hi, wo_lo = sb("wo_hi", [P, M, C], F32R), sb("wo_lo", [P, M, C], F32R)
        kd_hi, kd_lo = sb("kd_hi", [P, B, G, GK], F32R), sb("kd_lo", [P, B, G, GK], F32R)
        vd_hi, vd_lo = sb("vd_hi", [P, B, G, KC, P], F32R), sb("vd_lo", [P, B, G, KC, P], F32R)
        cols = sb("cols", [P, len(COLS) * M])
        ident = sb("ident", [P, P])
        half_neg = sb("half_neg", [P, T])
        bo = sb("bo", [P, C])
        bv = sb("bv", [P, C])
        values = sb("values", [KEYS, B, C])
        context = sb("context", [P, M, B * KEYS])

        def col(name, m):
            i = COLS.index(name) * M + m
            return cols[:, i:i + 1]

        x2 = sb("x2", [P, B, T, C])
        xt_hi, xt_lo = sb("xt_hi", [P, M, N], F32R), sb("xt_lo", [P, M, N], F32R)
        qt_hi, qt_lo = sb("qt_hi", [P, M, N], F32R), sb("qt_lo", [P, M, N], F32R)
        pr = sb("pr", [P, T, HEADS * KEYS])
        pt_hi, pt_lo = sb("pt_hi", [P, 3, N], F32R), sb("pt_lo", [P, 3, N], F32R)
        most = sb("most", [P, 2, PG, HG])
        total = sb("total", [P, 2, PH])
        share = sb("share", [P, 2, PH])
        x3 = sb("x3", [P, T, C])
        wc = sb("wc", [P, 2, C])
        wc_hi, wc_lo = sb("wc_hi", [P, M, C], F32R), sb("wc_lo", [P, M, C], F32R)
        bias = sb("bias", [P, C])
        stats = sb("stats", [P, T, 6])
        mv = sb("mv", [P, T, 2])
        veps = sb("veps", [P, T])
        rstd = sb("rstd", [P, T])

        ring = [ctx.enter_context(nc.psum_tensor(f"c_ring{i}", [P, 512], F32)) for i in range(4)]
        sc = [ctx.enter_context(nc.psum_tensor(f"c_sc{i}", [P, PG, 512], F32)) for i in range(2)]

        pr_flat = pr[:].rearrange("p t k -> p (t k)")
        x2_flat = x2[:].rearrange("p b t c -> p (b t c)")
        wk_raw, wv_raw = x2[:, 0], x2[:, 1]
        wq_raw = x3[:]
        wo_raw = pr_flat[:, 0:M * C].rearrange("p (m c) -> p m c", m=M)
        kd_raw = pr_flat[:, M * C:M * C + B * G * GK].rearrange("p (b g k) -> p b g k", b=B, g=G)
        vd_raw = x2_flat[:, 0:B * G * KC * P].rearrange("p (b g j e) -> p b g j e", b=B, g=G, j=KC)

        s_consts = sig("s_consts")
        s_kv_raw = sig("s_kv_raw")
        s_q_raw = sig("s_q_raw")
        s_o_raw = sig("s_o_raw")
        s_kd_zero = sig("s_kd_zero")
        s_vd_zero = sig("s_vd_zero")
        s_keys = sig("s_keys")
        s_keys_taken = sig("s_keys_taken")
        s_values = sig("s_values")
        s_values_taken = sig("s_values_taken")
        s_values_out = sig("s_values_out")
        s_vd_in = sig("s_vd_in")
        s_hi = sig("s_hi")
        s_lo = sig("s_lo")
        s_half = sig("s_half")

        x2_in = [sig(f"x2_in{b}", 1, unit=16, batches=1) for b in range(B)]
        wc_in = [sig(f"wc_in{i}", M // 2, unit=16) for i in range(2)]
        bias_in = sig("bias_in", 1, unit=16)
        wc_hi_ready = sig("wc_hi_ready", M)
        wc_lo_ready = sig("wc_lo_ready", M, places=2)
        xt_ready = sig("xt_ready", M)
        xt_hi_ready = sig("xt_hi_ready", M)
        xt_taken = sig("xt_taken", M)
        q_ready = sig("q_ready", M)
        q_hi_ready = sig("q_hi_ready", M)
        q_taken = sig("q_taken", M)
        sc_ready = sig("sc_ready", STEPS)
        sc_taken = sig("sc_taken", STEPS, places=2)
        most_ready = sig("most_ready", STEPS)
        exp_done = sig("exp_done", STEPS)
        total_ready = sig("total_ready", STEPS)
        share_ready = sig("share_ready", STEPS)
        pr_ready = sig("pr_ready", STEPS)
        pt_ready = sig("pt_ready", G * KC)
        pt_hi_ready = sig("pt_hi_ready", G * KC)
        pt_taken = sig("pt_taken", G * KC)
        pt_used = sig("pt_used", G * KC, places=3)
        o_ready = sig("o_ready", G)
        o_hi_ready = sig("o_hi_ready", G)
        o_taken = sig("o_taken", G)
        x2_read = sig("x2_read", 1, places=1)
        bo_added = sig("bo_added", 1)
        proj_ready = sig("proj_ready", T)
        proj_taken = sig("proj_taken", T)
        step = sig("step", 4)
        var_ready = sig("var_ready", 2)
        rstd_ready = sig("rstd_ready", 2)
        x3_ready = sig("x3_ready", 1)
        x3t_ready = sig("x3t_ready", M)
        x3t_hi_ready = sig("x3t_hi_ready", M)
        x3t_taken = sig("x3t_taken", M)
        bias_added = sig("bias_added", 1, places=1)
        ffn_ready = sig("ffn_ready", T, places=T)
        ffn_taken = sig("ffn_taken", T, places=T)
        y_ready = sig("y_ready", 1)
        y_stored = sig("y_stored", 1, places=1, unit=16)

        def segments():
            for head in range(HG):
                key = 0
                while key < KEYS:
                    chunk, row = divmod(head * KEYS + key, P)
                    count = min(KEYS - key, P - row)
                    yield head, key, chunk, row, count
                    key += count

        block = ctx.enter_context(nc.Block())

        @block.sync
        def _(sp):
            for to, src in ((cols[:], io["cols"]), (ident[:], io["ident"]),
                            (context[:], io["ctx"].rearrange("(m p) k -> p m k", p=P)),
                            (bv[:], io["bv"].to_broadcast([P, C])), (bo[:], io["bo"].to_broadcast([P, C]))):
                sp.dma_start(to, src).then_inc(s_consts.sem, 16)
            for to, name in ((wk_raw, "xwk"), (wv_raw, "xwv")):
                sp.dma_start(to, io[name].rearrange("(m p) n -> p m n", p=P)).then_inc(s_kv_raw.sem, 16)
            sp.dma_start(wq_raw, io["xwq"].rearrange("(m p) n -> p m n", p=P)).then_inc(s_q_raw.sem, 16)
            sp.dma_start(wo_raw, io["xwo"].rearrange("(m p) n -> p m n", p=P)).then_inc(s_o_raw.sem, 16)
            sp.wait_ge(s_values_taken.sem, B)
            sp.dma_start(scratch["v"].rearrange("b k c -> k b c"), values[:]).then_inc(s_values_out.sem, 16)
            sp.wait_ge(s_values_out.sem, 16)
            sp.wait_ge(s_vd_zero.sem, 1)
            for b in range(B):
                src = scratch["v"][b].rearrange("k (g h d) -> h k g d", g=G, h=HG)
                for head, key, chunk, row, count in segments():
                    sp.dma_start(vd_raw[row:row + count, b, :, chunk, head * HD:(head + 1) * HD],
                                 src[head, key:key + count]).then_inc(s_vd_in.sem, 16)
            sp.wait_ge(s_lo.sem, 4)
            sp.dma_start(x2[:, 0], scratch["x2"][0]).then_inc(x2_in[0].sem, 16)
            with sp.Fori(0, Q) as q:
                for b in range(B):
                    x2_read.place(sp, q, b, 1)
                    nxt = q + Q if b == 0 else q + 1
                    sp.dma_start(x2[:, 1 - b], scratch["x2"][nxt]).then_inc(x2_in[1 - b].sem, 16)
                    for m in range(M):
                        wc_lo_ready.place(sp, q, b, m + 1)
                        sp.dma_start(wc[:, m % 2], scratch["wc"][q + b * Q, m]).then_inc(wc_in[m % 2].sem, 16)
                    bias_added.place(sp, q, b, 1)
                    sp.dma_start(bias[:], scratch["bias"][q + b * Q].to_broadcast([P, C])
                                 ).then_inc(bias_in.sem, 16)
                    y_ready.item(sp, q, b, 1)
                    sp.dma_start(out[b, q].rearrange("(t p) c -> p t c", p=P), x3[:]).then_inc(y_stored.sem, 16)
            sp.wait_ge(y_stored.sem, 16 * (1 + B * Q))
            sp.wait_ge(x2_in[0].sem, 16 * (1 + Q))

        @block.tensor
        def _(pe):
            pe.wait_ge(s_consts.sem, 16 * 5)
            pe.wait_ge(s_kv_raw.sem, 32)
            for g in range(G):
                for m in range(M):
                    last = nc.tensor.matmul(ring[g][:, 0:B * KEYS], wk_raw[:, m, g * P:(g + 1) * P],
                                            context[:, m], start=m == 0, stop=m == M - 1)
                last.then_inc(s_keys.sem, 1)
            for b in range(B):
                for m in range(M):
                    last = nc.tensor.matmul(sc[0][0:KEYS, b], context[:, m, b * KEYS:(b + 1) * KEYS],
                                            wv_raw[:, m], start=m == 0, stop=m == M - 1)
                last.then_inc(s_values.sem, 1)
            for s in (pt_used, ffn_ready):
                s.give_places(pe)
            pe.wait_ge(s_lo.sem, 4)
            with pe.Fori(0, Q) as q:
                for b in range(B):
                    def transposes(source, ready, free):
                        for m in range(M):
                            free(m)
                            for t in range(T):
                                last = nc.tensor.transpose(ring[m][:, t * P:(t + 1) * P],
                                                           source[:, t, m * P:(m + 1) * P], ident[:])
                            last.then_inc(ready.sem, 1)

                    def by_tokens(source, weight, ready, free):
                        (s_hi, s_lo), (w_hi, w_lo) = source, weight
                        for t in range(T):
                            free(t)
                            part = slice(t * P, (t + 1) * P)
                            for m in range(M):
                                last = split_product(nc, ring[t][:], (s_hi[:, m, part], s_lo[:, m, part]),
                                                     (w_hi[:, m], w_lo[:, m]), m == 0, m == M - 1)
                            last.then_inc(ready.sem, 1)

                    def attend(i):
                        g, j = divmod(i, KC)
                        pt_taken.item(pe, q, b, i + 1)
                        if j == 0:
                            if g == 0:
                                q_taken.item(pe, q, b, M)
                            else:
                                o_taken.item(pe, q, b, g)
                        rows, s = ROWS[j], i % 3
                        last = split_product(nc, ring[3][:], (vd_hi[0:rows, b, g, j], vd_lo[0:rows, b, g, j]),
                                             (pt_hi[0:rows, s], pt_lo[0:rows, s]), j == 0, j == KC - 1)
                        if j == KC - 1:
                            last.then_inc(o_ready.sem, 1)
                            pe.drain().then_inc(pt_used.sem, 1)
                        else:
                            last.then_inc(pt_used.sem, 1)

                    x2_in[b].item(pe, q, 0, 1)
                    transposes(x2[:, b], xt_ready, lambda m: ffn_taken.place(pe, q, b, m + 1))
                    for g in range(M):
                        xt_taken.item(pe, q, b, M if g == 0 else g + 1)
                        part = slice(g * P, (g + 1) * P)
                        for m in range(M):
                            last = split_product(nc, ring[g][:], (wq_hi[:, m, part], wq_lo[:, m, part]),
                                                 (xt_hi[:, m], xt_lo[:, m]), m == 0, m == M - 1)
                        last.then_inc(q_ready.sem, 1)
                    for i in range(STEPS):
                        t, pair = divmod(i, G // PG)
                        sc_taken.place(pe, q, b, i + 1)
                        for gg in range(PG):
                            g = pair * PG + gg
                            if t == 0:
                                q_taken.item(pe, q, b, g + 1)
                            part = slice(t * P, (t + 1) * P)
                            last = split_product(nc, sc[i % 2][:, gg, 0:GK], (qt_hi[:, g, part], qt_lo[:, g, part]),
                                                 (kd_hi[:, b, g], kd_lo[:, b, g]), True, True)
                        last.then_inc(sc_ready.sem, 1)
                    pr_ready.item(pe, q, b, STEPS)
                    for i in range(G * KC + 2):
                        if i < G * KC:
                            g, j = divmod(i, KC)
                            if g == 0:
                                q_taken.item(pe, q, b, j + 1)
                            else:
                                pt_taken.item(pe, q, b, i - KC + 1)
                        if i >= 2:
                            attend(i - 2)
                        if i < G * KC:
                            for t in range(T):
                                last = nc.tensor.transpose(
                                    ring[j][0:ROWS[j], t * P:(t + 1) * P],
                                    pr[:, t, g * GK + j * P:g * GK + j * P + ROWS[j]], ident[:])
                            last.then_inc(pt_ready.sem, 1)
                    o_taken.item(pe, q, b, G)
                    by_tokens((qt_hi, qt_lo), (wo_hi, wo_lo), proj_ready, lambda t: None)
                    x3_ready.item(pe, q, b, 1)
                    transposes(x3, x3t_ready, lambda m: proj_taken.item(pe, q, b, m + 1))
                    x3t_taken.item(pe, q, b, M)
                    wc_lo_ready.item(pe, q, b, M)
                    by_tokens((xt_hi, xt_lo), (wc_hi, wc_lo), ffn_ready, lambda t: None)

        @block.scalar
        def _(act):
            act.wait_ge(s_consts.sem, 16 * 5)
            act.wait_ge(s_kd_zero.sem, 1)
            for g in range(G):
                act.wait_ge(s_keys.sem, g + 1)
                for head in range(HG):
                    mine = slice(head * HD, (head + 1) * HD)
                    ins = nc.scalar.activation(
                        kd_raw[mine, :, g, head * KEYS:(head + 1) * KEYS],
                        ring[g][mine, 0:B * KEYS].rearrange("p (b k) -> p b k", b=B), ACT.Identity,
                        bias=col("bk", g)[mine])
            ins.then_inc(s_keys_taken.sem, 1)
            act.wait_ge(s_q_raw.sem, 16)
            nc.scalar.copy(wq_hi[:], wq_raw).then_inc(s_hi.sem, 1)
            act.wait_ge(s_o_raw.sem, 16)
            nc.scalar.copy(wo_hi[:], wo_raw).then_inc(s_hi.sem, 1)
            act.wait_ge(s_keys_taken.sem, 1)
            nc.scalar.copy(kd_hi[:], kd_raw).then_inc(s_hi.sem, 1)
            act.wait_ge(s_vd_in.sem, 16 * B * len(list(segments())))
            nc.scalar.copy(vd_hi[:], vd_raw).then_inc(s_hi.sem, 1)
            with act.Fori(0, Q) as q:
                for b in range(B):
                    def high(ready, done, to, count=M):
                        for m in range(count):
                            ready.item(act, q, b, m + 1)
                            nc.scalar.copy(to[:, m], ring[m][:]).then_inc(done.sem, 1)

                    ffn_ready.place(act, q, b, T)
                    high(xt_ready, xt_hi_ready, xt_hi)
                    for g in range(M):
                        q_ready.item(act, q, b, g + 1)
                        nc.scalar.activation(qt_hi[:, g], ring[g][:], ACT.Identity, bias=col("bq", g)
                                             ).then_inc(q_hi_ready.sem, 1)
                    for i in range(STEPS):
                        t, pair = divmod(i, G // PG)
                        sc_taken.item(act, q, b, i + 1)
                        span = pr[:, t, pair * PH * KEYS:(pair + 1) * PH * KEYS]
                        nc.scalar.activation(span, span, ACT.Exp).then_inc(exp_done.sem, 1)
                    for m in range(M):
                        wc_in[m % 2].item(act, q, b, m // 2 + 1)
                        nc.scalar.copy(wc_hi[:, m], wc[:, m % 2]).then_inc(wc_hi_ready.sem, 1)
                    for i in range(G * KC):
                        g, j = divmod(i, KC)
                        pt_ready.item(act, q, b, i + 1)
                        pt_used.place(act, q, b, i + 1)
                        rows = slice(0, ROWS[j])
                        nc.scalar.copy(pt_hi[rows, i % 3], ring[j][rows, :]).then_inc(pt_hi_ready.sem, 1)
                        if j == KC - 2 and g >= 1:
                            o_ready.item(act, q, b, g)
                            nc.scalar.copy(qt_hi[:, g - 1], ring[3][:]).then_inc(o_hi_ready.sem, 1)
                    o_ready.item(act, q, b, G)
                    nc.scalar.copy(qt_hi[:, G - 1], ring[3][:]).then_inc(o_hi_ready.sem, 1)
                    high(x3t_ready, x3t_hi_ready, xt_hi)

        @block.gpsimd
        def _(pool):
            nc.gpsimd.memset(kd_raw, 0.0).then_inc(s_kd_zero.sem, 1)
            nc.gpsimd.memset(half_neg[:], -0.5).then_inc(s_half.sem, 1)
            pool.wait_ge(s_values.sem, B)
            nc.gpsimd.memset(vd_raw, 0.0).then_inc(s_vd_zero.sem, 1)
            wc_lo_ready.give_places(pool)
            bias_added.give_places(pool)
            pool.wait_ge(s_half.sem, 1)
            pool.wait_ge(s_consts.sem, 16 * 5)
            with pool.Fori(0, Q) as q:
                for b in range(B):
                    xt_ready.item(pool, q, b, M)
                    nc.gpsimd.tensor_tensor(x2[:, b], x2[:, b], bo[:].unsqueeze(1).to_broadcast([P, T, C]),
                                            ALU.add).then_inc(bo_added.sem, 1)
                    for m in range(M):
                        wc_hi_ready.item(pool, q, b, m + 1)
                        nc.gpsimd.tensor_tensor(wc_lo[:, m], wc[:, m % 2], wc_hi[:, m].bitcast(F32), ALU.subtract
                                                ).then_inc(wc_lo_ready.sem, 1)
                    var_ready.item(pool, q, b, 1)
                    nc.gpsimd.tensor_tensor(rstd[:], veps[:], half_neg[:], ALU.pow).then_inc(rstd_ready.sem, 1)
                    bias_in.item(pool, q, b, 1)
                    x3t_ready.item(pool, q, b, M)
                    nc.gpsimd.tensor_tensor(x3[:], x3[:], bias[:].unsqueeze(1).to_broadcast([P, T, C]),
                                            ALU.add).then_inc(bias_added.sem, 1)
                    var_ready.item(pool, q, b, 2)
                    nc.gpsimd.tensor_tensor(rstd[:], veps[:], half_neg[:], ALU.pow).then_inc(rstd_ready.sem, 1)

        @block.vector
        def _(dve):
            dve.wait_ge(s_consts.sem, 16 * 5)
            for b in range(B):
                dve.wait_ge(s_values.sem, b + 1)
                nc.vector.tensor_tensor(values[:, b], sc[0][0:KEYS, b], bv[0:KEYS, :], ALU.add
                                        ).then_inc(s_values_taken.sem, 1)
            for i, (raw, hi, lo) in enumerate(((wq_raw, wq_hi, wq_lo), (wo_raw, wo_hi, wo_lo),
                                               (kd_raw, kd_hi, kd_lo), (vd_raw, vd_hi, vd_lo))):
                dve.wait_ge(s_hi.sem, i + 1)
                nc.vector.tensor_tensor(lo[:], raw, hi[:].bitcast(F32), ALU.subtract).then_inc(s_lo.sem, 1)
            for s in (sc_taken, ffn_taken, x2_read, y_stored):
                s.give_places(dve)
            dve.wait_ge(s_lo.sem, 4)
            dve.wait_ge(s_values_taken.sem, B)
            with dve.Fori(0, Q) as q:
                for b in range(B):
                    def low(hi_ready, taken, hi, lo):
                        for m in range(M):
                            hi_ready.item(dve, q, b, m + 1)
                            nc.vector.tensor_tensor(lo[:, m], ring[m][:], hi[:, m].bitcast(F32), ALU.subtract
                                                    ).then_inc(taken.sem, 1)

                    def layer_norm(tile, taken, which, ready):
                        for t in range(T):
                            taken.item(dve, q, b, t + 1)
                            ins = nc.vector.bn_stats(stats[:, t], tile[:, t])
                        ins.then_inc(step.sem, 1)
                        step.item(dve, q, b, 2 * which + 1)
                        nc.vector.memset(veps[:], LN_EPS)
                        for t in range(T):
                            ins = nc.vector.bn_aggr(mv[:, t], stats[:, t])
                        ins.then_inc(step.sem, 1)
                        step.item(dve, q, b, 2 * which + 2)
                        nc.vector.tensor_tensor(veps[:], mv[:, :, 1], veps[:], ALU.add).then_inc(var_ready.sem, 1)
                        rstd_ready.item(dve, q, b, which + 1)
                        for t in range(T):
                            ins = nc.vector.tensor_scalar(tile[:, t], tile[:, t], mv[:, t, 0:1], rstd[:, t:t + 1],
                                                          ALU.subtract, ALU.mult)
                        ins.then_inc(ready.sem, 1)

                    def heads(ap):
                        return ap.rearrange("p g (h k) -> p g h k", k=KEYS)

                    def softmax_front(i):
                        t, pair = divmod(i, G // PG)
                        s = i % 2
                        sc_ready.item(dve, q, b, i + 1)
                        scores = heads(sc[s][:, :, 0:GK])
                        nc.vector.tensor_reduce(most[:, s], scores, AX_X, ALU.max).then_inc(most_ready.sem, 1)
                        most_ready.item(dve, q, b, i + 1)
                        span = pr[:, t, pair * PH * KEYS:(pair + 1) * PH * KEYS]
                        nc.vector.tensor_tensor(span.rearrange("p (g h k) -> p g h k", g=PG, k=KEYS), scores,
                                                most[:, s].unsqueeze(3).to_broadcast([P, PG, HG, KEYS]),
                                                ALU.subtract).then_inc(sc_taken.sem, 1)

                    def softmax_back(i):
                        t, pair = divmod(i, G // PG)
                        s = i % 2
                        span = pr[:, t, pair * PH * KEYS:(pair + 1) * PH * KEYS].rearrange("p (h k) -> p h k", k=KEYS)
                        exp_done.item(dve, q, b, i + 1)
                        nc.vector.tensor_reduce(total[:, s], span, AX_X, ALU.add).then_inc(total_ready.sem, 1)
                        total_ready.item(dve, q, b, i + 1)
                        nc.vector.reciprocal(share[:, s], total[:, s]).then_inc(share_ready.sem, 1)
                        share_ready.item(dve, q, b, i + 1)
                        nc.vector.tensor_tensor(span, span, share[:, s].unsqueeze(2).to_broadcast([P, PH, KEYS]),
                                                ALU.mult).then_inc(pr_ready.sem, 1)

                    low(xt_hi_ready, xt_taken, xt_hi, xt_lo)
                    for g in range(M):
                        q_hi_ready.item(dve, q, b, g + 1)
                        nc.vector.scalar_tensor_tensor(qt_lo[:, g], ring[g][:], col("bq", g),
                                                       qt_hi[:, g].bitcast(F32), ALU.add, ALU.subtract
                                                       ).then_inc(q_taken.sem, 1)
                    for i in range(STEPS + 1):
                        if i < STEPS:
                            softmax_front(i)
                        if i >= 1:
                            softmax_back(i - 1)

                    def o_low(g):
                        o_hi_ready.item(dve, q, b, g + 1)
                        nc.vector.tensor_tensor(qt_lo[:, g], ring[3][:], qt_hi[:, g].bitcast(F32), ALU.subtract
                                                ).then_inc(o_taken.sem, 1)

                    for i in range(G * KC):
                        g, j = divmod(i, KC)
                        rows = slice(0, ROWS[j])
                        pt_hi_ready.item(dve, q, b, i + 1)
                        nc.vector.tensor_tensor(pt_lo[rows, i % 3], ring[j][rows, :],
                                                pt_hi[rows, i % 3].bitcast(F32), ALU.subtract
                                                ).then_inc(pt_taken.sem, 1)
                        if j == KC - 2 and g >= 1:
                            o_low(g - 1)
                    o_low(G - 1)
                    y_stored.place(dve, q, b, 1)
                    bo_added.item(dve, q, b, 1)
                    for t in range(T):
                        proj_ready.item(dve, q, b, t + 1)
                        nc.vector.tensor_tensor(x3[:, t], x2[:, b, t], ring[t][:], ALU.add
                                                ).then_inc(proj_taken.sem, 1)
                    layer_norm(x3, proj_taken, 0, x3_ready)
                    dve.sem_inc(x2_read.sem, 1)
                    low(x3t_hi_ready, x3t_taken, xt_hi, xt_lo)
                    bias_added.item(dve, q, b, 1)
                    for t in range(T):
                        ffn_ready.item(dve, q, b, t + 1)
                        nc.vector.tensor_tensor(x3[:, t], x3[:, t], ring[t][:], ALU.add
                                                ).then_inc(ffn_taken.sem, 1)
                    layer_norm(x3, ffn_taken, 1, y_ready)
    clear(nc, semaphores)


def build(nc, io, out):
    scratch = {
        "xs": nc.dram_tensor("xs_scratch", (B * Q, P, T, C), F32).ap(),
        "kc": nc.dram_tensor("kc_scratch", (B * Q, 2, P, HB, N), F32).ap(),
        "rc": nc.dram_tensor("rc_scratch", (B * Q, T, P, C), F32).ap(),
        "wc": nc.dram_tensor("wc_scratch", (B * Q, M, P, C), F32).ap(),
        "bias": nc.dram_tensor("bias_scratch", (B * Q, 1, C), F32).ap(),
        "x2": nc.dram_tensor("x2_scratch", (B * Q, P, T, C), F32).ap(),
        "v": nc.dram_tensor("v_scratch", (B, KEYS, C), F32).ap(),
    }
    phase_a(nc, io, scratch)
    phase_b(nc, io, scratch)
    phase_c(nc, io, scratch, out)


def kernel(**inputs):
    import numpy as np
    import concourse.bacc as bacc
    from concourse.bass_utils import run_bass_kernel_spmd

    a = {n: np.asarray(v) for n, v in inputs.items()}

    def turned(w):
        return np.ascontiguousarray(np.swapaxes(w, -1, -2))

    w1 = a["L0_ffn_W1"].reshape(B, Q, O, 1, P, C)
    w2t = turned(a["L0_ffn_W2"]).reshape(B, Q, O, 1, P, C)
    per_channel = [a["L0_attn_" + n] for n in ("ln1_g", "ln1_b", "ln2_g", "ln2_b", "mix_k", "mix_v", "mix_r",
                                               "cmix_k", "cmix_r", "time_first")]
    per_channel += [a["L0_xattn_bq"], a["L0_xattn_bk"]]
    arrays = {
        "x": a["x"].reshape(B, Q, N, C),
        "ctx": turned(a["ctx_1024"].reshape(B * KEYS, C)),
        "cols": np.concatenate([v.reshape(M, P).T for v in per_channel], axis=1),
        "ident": np.eye(P, dtype=np.float32),
        "wk": turned(a["L0_attn_Wk_t"]), "wv": turned(a["L0_attn_Wv_t"]), "wr": turned(a["L0_attn_Wr_t"]),
        "wrc": turned(a["L0_attn_Wr_c"]), "wkc": turned(a["L0_attn_Wk_c"]), "wvc": turned(a["L0_attn_Wv_c"]),
        "xwq": turned(a["L0_xattn_Wq"]), "xwk": turned(a["L0_xattn_Wk"]), "xwv": turned(a["L0_xattn_Wv"]),
        "xwo": turned(a["L0_xattn_Wo"]), "bv": a["L0_xattn_bv"].reshape(1, C), "bo": a["L0_xattn_bo"].reshape(1, C),
        "w12": np.concatenate([w1, w2t], axis=3),
        "b1": turned(a["L0_ffn_b1"].reshape(B, Q, O, P)), "b2": a["L0_ffn_b2"].reshape(B, Q, 1, C),
    }
    arrays = {n: np.ascontiguousarray(v) for n, v in arrays.items()}
    nc = bacc.Bacc("TRN2", target_bir_lowering=False, num_devices=1, dynamic_dma_scratch_size=1024)
    io = {n: nc.dram_tensor(n + "_dram", v.shape, F32, kind="ExternalInput").ap() for n, v in arrays.items()}
    out = nc.dram_tensor("out_dram", (B, Q, N, C), F32, kind="ExternalOutput").ap()
    build(nc, io, out)
    got = run_bass_kernel_spmd(nc, [{n + "_dram": v for n, v in arrays.items()}], core_ids=[0])
    return got.results[0]["out_dram"].reshape(B, Q * N, C)
```

```python
import math
from contextlib import ExitStack

import concourse.bass as bass
from concourse import mybir

F32 = mybir.dt.float32
F32R = mybir.dt.float32r
ALU = mybir.AluOpType
ACT = mybir.ActivationFunctionType
AX_X = mybir.AxisListType.X

P = 128
B = 2
C = 512
M = C // P
N = 512
T = N // P
Q = 4
HID = 2048
O = HID // P
HB = M // 2
HEADS, KEYS = 16, 77
HD = C // HEADS
HG = P // HD
GK = HG * KEYS
KC = -(-GK // P)
LN_EPS = 1e-5
LEAST = -1e30

COLS = ("ln1_g", "ln1_b", "ln2_g", "ln2_b", "mix_k", "mix_v", "mix_r", "cmix_k", "cmix_r", "first", "bq", "bk")


class Signal:

    def __init__(self, sem, per=0, places=0, unit=1, batches=B):
        self.sem, self.per, self.places, self.unit, self.batches = sem, per, places, unit, batches

    def _until(self, eng, q, b, n):
        eng.wait_ge(self.sem, q * (self.batches * self.per * self.unit) + self.unit * (b * self.per + n))

    def item(self, eng, q, b, n):
        self._until(eng, q, b, self.places + n)

    def place(self, eng, q, b, n):
        self._until(eng, q, b, n)

    def give_places(self, eng):
        eng.sem_inc(self.sem, self.places * self.unit)


def split_product(nc, out, stationary, moving, start, stop):
    (s_hi, s_lo), (m_hi, m_lo) = stationary, moving
    nc.tensor.matmul(out, s_hi, m_hi, start=start, stop=False)
    nc.tensor.matmul(out, s_hi, m_lo, start=False, stop=False)
    return nc.tensor.matmul(out, s_lo, m_hi, start=False, stop=stop)


def clear(nc, semaphores):
    nc.clear_and_free_semaphores(semaphores)
    nc.all_engine_barrier()

A_STEPS = 14
OPENING_LINKS = 3


def phase_a(nc, io, scratch):
    semaphores = []
    with ExitStack() as ctx:
        def sb(name, shape, dt=F32):
            return ctx.enter_context(nc.sbuf_tensor("a_" + name, shape, dt))

        def sig(name, *args, **kw):
            semaphores.append(nc.alloc_semaphore(name="a_" + name))
            return Signal(semaphores[-1], *args, **kw)

        def in_place(name, shape):
            low = sb(name + "_lo", shape, F32R)
            size = 4 * math.prod(shape[1:])
            return low, nc.alloc_sbuf_tensor_at("a_" + name, shape, F32, offset=nc.sbuf_base - size)

        WK, WV, WR, WRC = range(4)
        w_hi = sb("w_hi", [P, 4, M, C], F32R)
        w_lo = sb("w_lo", [P, 4, M, C], F32R)
        cols = sb("cols", [P, len(COLS) * M])
        rest = sb("rest", [P, 5, M])
        ident = sb("ident", [P, P])
        half_neg = sb("half_neg", [P, T])

        def col(name, m):
            i = COLS.index(name) * M + m
            return cols[:, i:i + 1]

        x = sb("x", [P, B, T, C])
        xn = sb("xn", [P, T, C])
        gate = sb("gate", [P, T, C])
        stats = sb("stats", [P, T, 6])
        mv = sb("mv", [P, T, 2])
        rstd = sb("rstd", [P, T])
        veps = sb("veps", [P, T])
        h = sb("h", [P, 2, M, N + 1])
        mix_lo, mixf = in_place("mixf", [P, 2, M, N])
        mix_hi = sb("mix_hi", [P, 2, HB, N], F32R)
        k = sb("k", [P, B, M, N])
        v = sb("v", [P, M, N])
        mx = sb("mx", [P, HB, N + 1])
        ee = sb("ee", [P, 2, HB, N])
        pp = sb("pp", [P, HB, N + 1])
        dl = sb("dl", [P, HB, N])
        aa = sb("aa", [P, HB, N + 1])
        h_last = sb("h_last", [P, 2, B, M])
        m_last = sb("m_last", [P, B, M])
        s_last = sb("s_last", [P, B, M])
        p_last = sb("p_last", [P, B, M])
        a_last = sb("a_last", [P, B, M])
        SLOTS = 4
        wt_lo, wt = in_place("wt", [P, SLOTS, 2, C])
        wt_hi = sb("wt_hi", [P, SLOTS, 2, C], F32R)
        going = sb("going", [P, 2, C])

        ring = [ctx.enter_context(nc.psum_tensor(f"a_ring{i}", [P, 512], F32)) for i in range(4)]
        joint = [ctx.enter_context(nc.psum_tensor(f"a_joint{i}", [P, 512], F32)) for i in range(4)]

        RAW = (k[:, 0], k[:, 1], v[:], gate[:])

        MIX = {"k": (0, "mix_k", 0), "v": (0, "mix_v", 1), "r": (0, "mix_r", 0),
               "kc": (1, "cmix_k", 1), "rc": (1, "cmix_r", 0)}
        REST = {n: i for i, n in enumerate(MIX)}

        consts_in = sig("consts_in")
        raw_in = [sig(f"raw_in{i}") for i in range(4)]
        w_hi_ready = sig("w_hi_ready")
        w_lo_ready = sig("w_lo_ready")
        state_ready = sig("state_ready")
        half_ready = sig("half_ready")

        x_in = [sig(f"x_in{b}", 1, unit=16, batches=1) for b in range(B)]
        wt_in = [sig(f"wt_in{s}", O // SLOTS, unit=16) for s in range(SLOTS)]
        wt_hi_ready = sig("wt_hi_ready", O)
        wt_lo_ready = sig("wt_lo_ready", O)
        wt_used = sig("wt_used", O, places=SLOTS)
        joint_ready = sig("joint_ready", M)
        joint_taken = sig("joint_taken", M, places=M)
        wc_stored = [sig(f"wc_stored{m}", 1, places=1, unit=16) for m in range(M)]
        rc_stored = [sig(f"rc_stored{s}", T // 2, places=1, unit=16) for s in range(2)]
        ln_step = [sig(f"ln_step{w}", 2) for w in range(2)]
        var_ready = [sig(f"var_ready{w}", 1) for w in range(2)]
        rstd_ready = [sig(f"rstd_ready{w}", 1) for w in range(2)]
        xn_ready = [sig(f"xn_ready{w}", 1) for w in range(2)]
        halo_step = [sig(f"halo_step{w}", 2) for w in range(2)]
        xt_ready = sig("xt_ready", M)
        xt_taken = sig("xt_taken", M)
        pre_ready = {n: sig(f"pre_{n}", 2) for n in MIX}
        full_ready = {n: sig(f"full_{n}", 2) for n in MIX}
        hi_ready = {n: sig(f"hi_{n}", 2) for n in MIX if n != "kc"}
        lo_ready = {n: sig(f"lo_{n}", 2) for n in MIX if n != "kc"}
        used = {n: sig(f"used_{n}", 2, places=2 if n == "rc" else 0) for n in MIX if n != "kc"}
        k_ready = sig("k_ready", M)
        k_taken = sig("k_taken", M)
        v_ready = sig("v_ready", M)
        v_taken = sig("v_taken", M)
        r_ready = sig("r_ready", T)
        r_taken = sig("r_taken", T)
        step = sig("step", A_STEPS)
        ex_ready = sig("ex_ready", 2)
        ex_done = sig("ex_done", 2)
        s_ready = sig("s_ready", 2)
        ln_done = sig("ln_done", 2)
        dl_ready = sig("dl_ready", 2)
        z_ready = sig("z_ready", 2)
        z_done = sig("z_done", 2)
        share_done = sig("share_done", 2)
        wkv_ready = sig("wkv_ready", 2)
        ot_ready = sig("ot_ready", T)
        ot_taken = sig("ot_taken", T)
        x1_ready = sig("x1_ready", 1)
        xs_ready = sig("xs_ready", 1)
        xs_stored = [sig(f"xs_stored{b}", 1, places=1, unit=16, batches=1) for b in range(B)]
        h2_ready = sig("h2_ready", M, places=M)
        h2_taken = sig("h2_taken", M)
        rc_ready = sig("rc_ready", T)
        rc_taken = sig("rc_taken", T, places=T)
        kc_stored = [sig(f"kc_stored{s}", 1, places=1, unit=16) for s in range(2)]

        block = ctx.enter_context(nc.Block())

        LEAD = 4

        @block.sync
        def _(sp):
            def load_x(q, b):
                if not (isinstance(q, int) and q == 0 and b == 0):
                    xs_stored[b % B].place(sp, q, 0, 1 + b // B)
                sp.dma_start(x[:, b % B], io["x"][b % B, q + b // B].rearrange("(t p) c -> p t c", p=P)
                             ).then_inc(x_in[b % B].sem, 16)

            load_x(0, 0)
            sp.dma_start(ident[:], io["ident"]).then_inc(consts_in.sem, 16)
            sp.dma_start(cols[:], io["cols"]).then_inc(consts_in.sem, 16)
            for i, name in enumerate(("wk", "wv", "wr", "wrc")):
                sp.dma_start(RAW[i], io[name].rearrange("(m p) n -> p m n", p=P)).then_inc(raw_in[i].sem, 16)

            def period(q, b, more):
                if more:
                    load_x(q, b + 1)
                for o in range(O):
                    wt_used.place(sp, q, b, o + 1)
                    sp.dma_start(wt[:, o % SLOTS], io["w12"][b, q, o].rearrange("w p c -> p w c")
                                 ).then_inc(wt_in[o % SLOTS].sem, 16)

            with sp.Fori(0, Q - 1) as q:
                for b in range(B):
                    period(q, b, True)
            for b in range(B):
                period(Q - 1, b, b + 1 < B)

        @block.tensor
        def _(pe):
            def transposes(source, ready, free):
                for m in range(4):
                    free(m + 1)
                    for t in range(4):
                        last = nc.tensor.transpose(ring[m][:, t * P:(t + 1) * P],
                                                   source[:, t, m * P:(m + 1) * P], ident[:])
                    last.then_inc(ready.sem, 1)

            def joint_part(q, b, first, count):
                for o in range(first, first + count):
                    s = o % SLOTS
                    wt_lo_ready.item(pe, q, b, o + 1)
                    for m in range(M):
                        if o == 0:
                            joint_taken.place(pe, q, b, m + 1)
                        last = split_product(
                            nc, joint[m][:],
                            (wt_hi[:, s, 0, m * P:(m + 1) * P], wt_lo[:, s, 0, m * P:(m + 1) * P]),
                            (wt_hi[:, s, 1], wt_lo[:, s, 1]), o == 0, o == O - 1)
                        if o == O - 1:
                            last.then_inc(joint_ready.sem, 1)
                    if o == O - 1:
                        pe.drain().then_inc(wt_used.sem, 1)
                    else:
                        last.then_inc(wt_used.sem, 1)

            def mixed(q, b, name, w, rows, free, ready):
                for hf in range(2):
                    lo_ready[name].item(pe, q, b, hf + 1)
                    for n in range(4):
                        if hf == 0:
                            free(n + 1)
                        for i in range(HB):
                            kb = hf * HB + i
                            part = slice(n * P, (n + 1) * P)
                            act_parts = (mix_hi[:, hf, i], mix_lo[:, MIX[name][2], kb])
                            w_parts = (w_hi[:, w, kb], w_lo[:, w, kb])
                            if rows:
                                st, mvg = tuple(a[:, part] for a in act_parts), w_parts
                            else:
                                st, mvg = tuple(a[:, part] for a in w_parts), act_parts
                            last = split_product(nc, ring[n][:], st, mvg, kb == 0, kb == M - 1)
                        if hf == 1:
                            last.then_inc(ready.sem, 1)
                    if hf == 0:
                        last.then_inc(used[name].sem, 1)
                    else:
                        pe.drain().then_inc(used[name].sem, 1)

            for s in (used["rc"], wt_used, h2_ready):
                s.give_places(pe)
            pe.wait_ge(consts_in.sem, 32)
            xn_ready[0].item(pe, 0, 0, 1)
            transposes(xn, xt_ready, lambda n: None)
            pe.wait_ge(w_lo_ready.sem, 1)
            mixed(0, 0, "k", WK, False, lambda n: xt_taken.item(pe, 0, 0, n), k_ready)
            pe.wait_ge(w_lo_ready.sem, 2)
            mixed(0, 0, "v", WV, False, lambda n: k_taken.item(pe, 0, 0, n), v_ready)
            pe.wait_ge(w_lo_ready.sem, 3)
            mixed(0, 0, "r", WR, True, lambda n: v_taken.item(pe, 0, 0, n), r_ready)
            pe.wait_ge(w_lo_ready.sem, 4)

            def period(q, b, more):
                nxt = b + 1

                def behind_products(n):
                    rc_taken.place(pe, q, b, n)
                    r_taken.item(pe, q, b, n)

                if more:
                    xn_ready[0].item(pe, q, nxt, 1)
                    transposes(xn, xt_ready, behind_products)
                joint_part(q, b, 0, 5)
                if more:
                    mixed(q, nxt, "k", WK, False, lambda n: xt_taken.item(pe, q, nxt, n), k_ready)
                joint_part(q, b, 5, 2)
                wkv_ready.item(pe, q, b, 2)
                transposes(v, ot_ready, (lambda n: k_taken.item(pe, q, nxt, n)) if more else behind_products)
                joint_part(q, b, 7, 2)
                if more:
                    mixed(q, nxt, "v", WV, False, lambda n: ot_taken.item(pe, q, b, n), v_ready)
                joint_part(q, b, 9, 1)
                xn_ready[1].item(pe, q, b, 1)
                transposes(xn, h2_ready, (lambda n: v_taken.item(pe, q, nxt, n)) if more
                           else (lambda n: ot_taken.item(pe, q, b, n)))
                joint_part(q, b, 10, 2)
                if more:
                    mixed(q, nxt, "r", WR, True, lambda n: h2_taken.item(pe, q, b, n), r_ready)
                joint_part(q, b, 12, 4)
                mixed(q, b, "rc", WRC, True, (lambda n: r_taken.item(pe, q, nxt, n)) if more
                      else (lambda n: h2_taken.item(pe, q, b, n)), rc_ready)

            with pe.Fori(0, Q - 1) as q:
                for b in range(B):
                    period(q, b, True)
            for b in range(B):
                period(Q - 1, b, b + 1 < B)

        @block.scalar
        def _(act):
            def wt_high(q, b, first, count, more):
                for o in range(first, first + count if more else min(first + count, O)):
                    wt_in[o % SLOTS].item(act, q, b, o // SLOTS + 1)
                    nc.scalar.copy(wt_hi[:, o % SLOTS], wt[:, o % SLOTS]).then_inc(wt_hi_ready.sem, 1)

            def pre(q, b, name, free):
                which, _, pair = MIX[name]
                for hf in range(2):
                    free(hf)
                    for i in range(HB):
                        m = hf * HB + i
                        ins = nc.scalar.mul(mixf[:, pair, m], h[:, which, m, 0:N], rest[:, REST[name], m:m + 1])
                    ins.then_inc(pre_ready[name].sem, 1)

            def high(q, b, name, hf, free):
                full_ready[name].item(act, q, b, hf + 1)
                free(hf)
                pair = MIX[name][2]
                nc.scalar.copy(mix_hi[:, hf], mixf[:, pair, hf * HB:(hf + 1) * HB]).then_inc(hi_ready[name].sem, 1)

            def to_h(q, b, ready, taken, which, g, beta):
                nc.scalar.copy(h[:, which, :, 0], h_last[:, which, b % B]).then_inc(halo_step[which].sem, 1)
                for m in range(M):
                    ready.item(act, q, b, m + 1)
                    nc.scalar.activation(h[:, which, m, 1:], ring[m][:], ACT.Identity, scale=col(g, m),
                                         bias=col(beta, m)).then_inc(taken.sem, 1)
                taken.item(act, q, b, M)
                halo_step[which].item(act, q, b, 1)
                nc.scalar.copy(h_last[:, which, b % B], h[:, which, :, N]).then_inc(halo_step[which].sem, 1)

            def take(q, b, ready, taken, to, free=lambda m: None):
                for m in range(M):
                    free(m)
                    ready.item(act, q, b, m + 1)
                    nc.scalar.copy(to[:, m], ring[m][:]).then_inc(taken.sem, 1)

            def take_r(q, b):
                for t in range(T):
                    r_ready.item(act, q, b, t + 1)
                    nc.scalar.activation(gate[:, t], ring[t][:], ACT.Sigmoid).then_inc(r_taken.sem, 1)

            def exp_under_max(q, b, hf):
                ex_ready.item(act, q, b, hf + 1)
                nc.scalar.activation(ee[:], ee[:], ACT.Exp).then_inc(ex_done.sem, 1)

            def log_of_sum(q, b, hf):
                s_ready.item(act, q, b, hf + 1)
                nc.scalar.activation(pp[:, :, 1:], ee[:, 1], ACT.Ln).then_inc(ln_done.sem, 1)

            def exp_and_share(q, b, hf):
                z_ready.item(act, q, b, hf + 1)
                nc.scalar.activation(ee[:], ee[:], ACT.Exp).then_inc(z_done.sem, 1)
                for i in range(HB):
                    ins = nc.scalar.activation(dl[:, i], dl[:, i], ACT.Sigmoid, scale=-1.0,
                                               bias=col("first", hf * HB + i))
                ins.then_inc(share_done.sem, 1)

            def weight_high(i):
                act.wait_ge(raw_in[i].sem, 16)
                nc.scalar.copy(w_hi[:, i], RAW[i]).then_inc(w_hi_ready.sem, 1)

            act.wait_ge(consts_in.sem, 32)
            for s in (joint_taken, rc_taken, *wc_stored, *rc_stored, *xs_stored, *kc_stored):
                s.give_places(act)
            weight_high(0)
            act.wait_ge(state_ready.sem, 6)
            to_h(0, 0, xt_ready, xt_taken, 0, "ln1_g", "ln1_b")
            pre(0, 0, "k", lambda hf: None)
            weight_high(1)
            high(0, 0, "k", 0, lambda hf: None)
            high(0, 0, "k", 1, lambda hf: None)
            pre(0, 0, "v", lambda hf: None)
            weight_high(2)
            weight_high(3)
            wt_high(0, 0, 0, LEAD, True)
            act.wait_ge(w_lo_ready.sem, 1)
            take(0, 0, k_ready, k_taken, k[:, 0])
            high(0, 0, "v", 0, lambda hf: used["k"].item(act, 0, 0, hf + 1))
            high(0, 0, "v", 1, lambda hf: used["k"].item(act, 0, 0, hf + 1))
            pre(0, 0, "r", lambda hf: used["k"].item(act, 0, 0, hf + 1))
            exp_under_max(0, 0, 0)
            act.wait_ge(w_lo_ready.sem, 4)
            take(0, 0, v_ready, v_taken, v)
            high(0, 0, "r", 0, lambda hf: used["v"].item(act, 0, 0, hf + 1))
            log_of_sum(0, 0, 0)
            high(0, 0, "r", 1, lambda hf: used["v"].item(act, 0, 0, hf + 1))
            exp_and_share(0, 0, 0)
            take_r(0, 0)

            def period(q, b, more):
                nxt = b + 1

                def rc_used(hf):
                    used["rc"].place(act, q, b, hf + 1)

                def kc_out(hf):
                    kc_stored[hf].place(act, q, b, 1)

                def product_done(name, c):
                    return lambda hf: used[name].item(act, q, c, hf + 1)

                if more:
                    to_h(q, nxt, xt_ready, xt_taken, 0, "ln1_g", "ln1_b")
                exp_under_max(q, b, 1)
                wt_high(q, b, 4, 1, more)
                if more:
                    pre(q, nxt, "k", rc_used)
                log_of_sum(q, b, 1)
                if more:
                    high(q, nxt, "k", 0, rc_used)
                    high(q, nxt, "k", 1, rc_used)
                wt_high(q, b, 5, 2, more)
                wt_high(q, b, 7, 1, more)
                exp_and_share(q, b, 1)
                if more:
                    pre(q, nxt, "v", kc_out)
                wt_high(q, b, 8, 1, more)
                if more:
                    take(q, nxt, k_ready, k_taken, k[:, nxt % B],
                         lambda m: wc_stored[m].place(act, q, b, 1))
                wt_high(q, b, 9, 1, more)
                if more:
                    high(q, nxt, "v", 0, product_done("k", nxt))
                    high(q, nxt, "v", 1, product_done("k", nxt))
                    pre(q, nxt, "r", product_done("k", nxt))
                wt_high(q, b, 10, 2, more)
                if more:
                    exp_under_max(q, nxt, 0)
                    log_of_sum(q, nxt, 0)
                wt_high(q, b, 12, 1, more)
                if more:
                    take(q, nxt, v_ready, v_taken, v)
                    high(q, nxt, "r", 0, product_done("v", nxt))
                    high(q, nxt, "r", 1, product_done("v", nxt))
                to_h(q, b, h2_ready, h2_taken, 1, "ln2_g", "ln2_b")
                if more:
                    exp_and_share(q, nxt, 0)
                xs_ready.item(act, q, b, 1)
                act.dma_start(scratch["xs"][b * Q + q], x[:, b]).then_inc(xs_stored[b].sem, 16)
                pre(q, b, "kc", product_done("v", nxt if more else b))
                wt_high(q, b, 13, 3, more)
                if more:
                    take_r(q, nxt)
                pre(q, b, "rc", product_done("r", nxt if more else b))
                for hf in range(2):
                    high(q, b, "rc", hf, product_done("r", nxt if more else b))
                for hf in range(2):
                    full_ready["kc"].item(act, q, b, hf + 1)
                    act.dma_start(scratch["kc"][b * Q + q, hf], mixf[:, 1, hf * HB:(hf + 1) * HB]
                                  ).then_inc(kc_stored[hf].sem, 16)
                for m in range(M):
                    joint_ready.item(act, q, b, m + 1)
                    nc.scalar.copy(k[:, b, m], joint[m][:]).then_inc(joint_taken.sem, 1)
                    joint_taken.item(act, q, b, m + 1)
                    act.dma_start(scratch["wc"][b * Q + q, m], k[:, b, m]).then_inc(wc_stored[m].sem, 16)
                wt_high(q, b, O, LEAD, more)
                for t in range(T):
                    rc_ready.item(act, q, b, t + 1)
                    rc_stored[t % 2].place(act, q, b, t // 2 + 1)
                    nc.scalar.activation(going[:, t % 2], ring[t][:], ACT.Sigmoid).then_inc(rc_taken.sem, 1)
                    rc_taken.item(act, q, b, t + 1)
                    act.dma_start(scratch["rc"][b * Q + q, t], going[:, t % 2]).then_inc(rc_stored[t % 2].sem, 16)

            with act.Fori(0, Q - 1) as q:
                for b in range(B):
                    period(q, b, True)
            for b in range(B):
                period(Q - 1, b, b + 1 < B)
            for s in rc_stored:
                act.wait_ge(s.sem, 16 * (1 + B * Q * T // 2))
            for s in wc_stored:
                act.wait_ge(s.sem, 16 * (1 + B * Q))
            for s in xs_stored:
                act.wait_ge(s.sem, 16 * (1 + Q))
            for s in kc_stored:
                act.wait_ge(s.sem, 16 * (1 + B * Q))

        @block.gpsimd
        def _(pool):
            nc.gpsimd.memset(half_neg[:], -0.5).then_inc(half_ready.sem, 1)
            pool.wait_ge(half_ready.sem, 1)

            def root(q, b, which):
                var_ready[which].item(pool, q, b, 1)
                nc.gpsimd.tensor_tensor(rstd[:], veps[:], half_neg[:], ALU.pow).then_inc(rstd_ready[which].sem, 1)

            def wt_low(q, b, first, count):
                for o in range(first, first + count):
                    wt_hi_ready.item(pool, q, b, o + 1)
                    nc.gpsimd.tensor_tensor(wt_lo[:, o % SLOTS], wt[:, o % SLOTS], wt_hi[:, o % SLOTS].bitcast(F32),
                                            ALU.subtract).then_inc(wt_lo_ready.sem, 1)

            def period(q, b, more):
                if more:
                    root(q, b + 1, 0)
                wt_low(q, b, 0, 12)
                root(q, b, 1)
                nc.gpsimd.tensor_tensor(x[:, b], x[:, b], gate[:], ALU.add).then_inc(xs_ready.sem, 1)
                wt_low(q, b, 12, 4)

            root(0, 0, 0)
            with pool.Fori(0, Q - 1) as q:
                for b in range(B):
                    period(q, b, True)
            for b in range(B):
                period(Q - 1, b, b + 1 < B)

        @block.vector
        def _(dve):
            def chain(sig, q, b, from_=0):
                done = [from_]

                def then(ins):
                    ins.then_inc(sig.sem, 1)
                    done[0] += 1
                    sig.item(dve, q, b, done[0])
                then.done = done
                return then

            def norm_front(q, b, which, source):
                then = chain(ln_step[which], q, b)
                for t in range(T):
                    ins = nc.vector.bn_stats(stats[:, t], source[:, t])
                then(ins)
                nc.vector.memset(veps[:], LN_EPS)
                for t in range(T):
                    ins = nc.vector.bn_aggr(mv[:, t], stats[:, t])
                then(ins)
                nc.vector.tensor_tensor(veps[:], mv[:, :, 1], veps[:], ALU.add).then_inc(var_ready[which].sem, 1)

            def norm_back(q, b, which, source):
                rstd_ready[which].item(dve, q, b, 1)
                for t in range(T):
                    ins = nc.vector.tensor_scalar(xn[:, t], source[:, t], mv[:, t, 0:1], rstd[:, t:t + 1],
                                                  ALU.subtract, ALU.mult)
                ins.then_inc(xn_ready[which].sem, 1)

            def mix(q, b, name, hf):
                which, ratio, pair = MIX[name]
                pre_ready[name].item(dve, q, b, hf + 1)
                for i in range(HB):
                    m = hf * HB + i
                    place = mixf[:, pair, m]
                    ins = nc.vector.scalar_tensor_tensor(place, h[:, which, m, 1:], col(ratio, m), place,
                                                         ALU.mult, ALU.add)
                ins.then_inc(full_ready[name].sem, 1)

            def low(q, b, name, hf):
                pair = MIX[name][2]
                hi_ready[name].item(dve, q, b, hf + 1)
                mine = slice(hf * HB, (hf + 1) * HB)
                nc.vector.tensor_tensor(mix_lo[:, pair, mine], mixf[:, pair, mine],
                                        mix_hi[:, hf].bitcast(F32), ALU.subtract).then_inc(lo_ready[name].sem, 1)

            def mix_and_low(q, b, name):
                mix(q, b, name, 0)
                mix(q, b, name, 1)
                low(q, b, name, 0)
                low(q, b, name, 1)

            for tile, value in ((h_last, 0.0), (m_last, LEAST), (s_last, 0.0), (p_last, LEAST), (a_last, 0.0)):
                nc.vector.memset(tile[:], value).then_inc(state_ready.sem, 1)
            x_in[0].item(dve, 0, 0, 1)
            norm_front(0, 0, 0, x[:, 0])
            norm_back(0, 0, 0, x[:, 0])
            dve.wait_ge(consts_in.sem, 32)
            for name, (_, ratio, _) in MIX.items():
                first = COLS.index(ratio) * M
                ins = nc.vector.tensor_scalar(rest[:, REST[name]], cols[:, first:first + M], -1.0, 1.0,
                                              ALU.mult, ALU.add)
            ins.then_inc(state_ready.sem, 1)
            def recurrence_of(q, b, from_):
                then = chain(step, q, b, from_)
                bb = b % B
                kb = k[:, bb]

                def under_max(hf):
                    mine = slice(hf * HB, (hf + 1) * HB)
                    k_taken.item(dve, q, b, (hf + 1) * HB)
                    nc.vector.tensor_copy(mx[:, :, 0], m_last[:, bb, mine])
                    for i in range(HB):
                        ins = nc.vector.tensor_tensor_scan(mx[:, i, 1:], kb[:, hf * HB + i], kb[:, hf * HB + i],
                                                           m_last[:, bb, hf * HB + i:hf * HB + i + 1],
                                                           ALU.max, ALU.max)
                    then(ins)
                    nc.vector.tensor_tensor(ee[:, 0], mx[:, :, 0:N], mx[:, :, 1:], ALU.subtract)
                    nc.vector.tensor_tensor(ee[:, 1], kb[:, mine], mx[:, :, 1:], ALU.subtract
                                            ).then_inc(ex_ready.sem, 1)
                    nc.vector.tensor_copy(m_last[:, bb, mine], mx[:, :, N])

                def running_sum(hf):
                    mine = slice(hf * HB, (hf + 1) * HB)
                    ex_done.item(dve, q, b, hf + 1)
                    for i in range(HB):
                        ins = nc.vector.tensor_tensor_scan(ee[:, 1, i], ee[:, 0, i], ee[:, 1, i],
                                                           s_last[:, bb, hf * HB + i:hf * HB + i + 1],
                                                           ALU.mult, ALU.add)
                    ins.then_inc(s_ready.sem, 1)
                    s_ready.item(dve, q, b, hf + 1)
                    nc.vector.tensor_copy(s_last[:, bb, mine], ee[:, 1, :, N - 1])
                    then(nc.vector.tensor_copy(pp[:, :, 0], p_last[:, bb, mine]))

                def exponents(hf):
                    mine = slice(hf * HB, (hf + 1) * HB)
                    ln_done.item(dve, q, b, hf + 1)
                    then(nc.vector.tensor_tensor(pp[:, :, 1:], pp[:, :, 1:], mx[:, :, 1:], ALU.add))
                    nc.vector.tensor_copy(p_last[:, bb, mine], pp[:, :, N])
                    nc.vector.tensor_tensor(dl[:], pp[:, :, 0:N], kb[:, mine], ALU.subtract
                                            ).then_inc(dl_ready.sem, 1)
                    dl_ready.item(dve, q, b, hf + 1)
                    nc.vector.tensor_scalar(ee[:, 0], dl[:], 0.0, None, ALU.min)
                    nc.vector.tensor_scalar(ee[:, 1], dl[:], -1.0, 0.0, ALU.mult, ALU.min
                                            ).then_inc(z_ready.sem, 1)
                    nc.vector.tensor_copy(aa[:, :, 0], a_last[:, bb, mine])

                def recurrence(hf):
                    mine = slice(hf * HB, (hf + 1) * HB)
                    z_done.item(dve, q, b, hf + 1)
                    v_taken.item(dve, q, b, (hf + 1) * HB)
                    then(nc.vector.tensor_tensor(ee[:, 1], ee[:, 1], v[:, mine], ALU.mult))
                    for i in range(HB):
                        ins = nc.vector.tensor_tensor_scan(aa[:, i, 1:], ee[:, 0, i], ee[:, 1, i],
                                                           a_last[:, bb, hf * HB + i:hf * HB + i + 1],
                                                           ALU.mult, ALU.add)
                    then(ins)
                    nc.vector.tensor_copy(a_last[:, bb, mine], aa[:, :, N])
                    then(nc.vector.tensor_tensor(v[:, mine], v[:, mine], aa[:, :, 0:N], ALU.subtract))
                    share_done.item(dve, q, b, hf + 1)
                    then(nc.vector.tensor_tensor(v[:, mine], v[:, mine], dl[:], ALU.mult))
                    nc.vector.tensor_tensor(v[:, mine], v[:, mine], aa[:, :, 0:N], ALU.add
                                            ).then_inc(wkv_ready.sem, 1)
                    wkv_ready.item(dve, q, b, hf + 1)

                return under_max, running_sum, exponents, recurrence, then

            def opening(q, b):
                under_max, running_sum, exponents, _, then = recurrence_of(q, b, 0)
                return lambda: under_max(0), lambda: running_sum(0), lambda: exponents(0)

            def weight_low(i):
                dve.wait_ge(raw_in[i].sem, 16)
                dve.wait_ge(w_hi_ready.sem, i + 1)
                nc.vector.tensor_tensor(w_lo[:, i], RAW[i], w_hi[:, i].bitcast(F32), ALU.subtract
                                        ).then_inc(w_lo_ready.sem, 1)

            weight_low(0)
            dve.wait_ge(state_ready.sem, 6)
            mix_and_low(0, 0, "k")
            weight_low(1)
            mix(0, 0, "v", 0)
            mix(0, 0, "v", 1)
            weight_low(2)
            weight_low(3)
            low(0, 0, "v", 0)
            low(0, 0, "v", 1)
            first_under_max, first_running_sum, first_exponents = opening(0, 0)
            first_under_max()
            mix(0, 0, "r", 0)
            mix(0, 0, "r", 1)
            first_running_sum()
            low(0, 0, "r", 0)
            low(0, 0, "r", 1)
            first_exponents()

            def period(q, b, more):
                nxt = b + 1
                under_max, running_sum, exponents, recurrence, then = recurrence_of(q, b, OPENING_LINKS)
                if more:
                    x_in[nxt % B].item(dve, q, 0, 1 + nxt // B)
                    norm_front(q, nxt, 0, x[:, nxt % B])
                recurrence(0)
                if more:
                    h2_ready.place(dve, q, b, M)
                    norm_back(q, nxt, 0, x[:, nxt % B])
                under_max(1)
                running_sum(1)
                if more:
                    mix(q, nxt, "k", 0)
                    mix(q, nxt, "k", 1)
                if more:
                    low(q, nxt, "k", 0)
                    low(q, nxt, "k", 1)
                exponents(1)
                recurrence(1)
                if more:
                    mix(q, nxt, "v", 0)
                    mix(q, nxt, "v", 1)
                for t in range(T):
                    ot_ready.item(dve, q, b, t + 1)
                    r_taken.item(dve, q, b, t + 1)
                    nc.vector.tensor_tensor(gate[:, t], gate[:, t], ring[t][:], ALU.mult
                                            ).then_inc(ot_taken.sem, 1)
                if more:
                    next_under_max, next_running_sum, next_exponents = opening(q, nxt)
                    low(q, nxt, "v", 0)
                    low(q, nxt, "v", 1)
                    next_under_max()
                ot_taken.item(dve, q, b, T)
                nc.vector.tensor_tensor(gate[:], gate[:], x[:, b], ALU.add).then_inc(x1_ready.sem, 1)
                x1_ready.item(dve, q, b, 1)
                norm_front(q, b, 1, gate)
                if more:
                    next_running_sum()
                xt_ready.item(dve, q, nxt if more else b, M)
                norm_back(q, b, 1, gate)
                if more:
                    mix(q, nxt, "r", 0)
                    mix(q, nxt, "r", 1)
                    low(q, nxt, "r", 0)
                    low(q, nxt, "r", 1)
                    next_exponents()
                mix(q, b, "kc", 0)
                mix(q, b, "kc", 1)
                mix_and_low(q, b, "rc")
                assert then.done[0] == A_STEPS, then.done[0]

            with dve.Fori(0, Q - 1) as q:
                for b in range(B):
                    period(q, b, True)
            for b in range(B):
                period(Q - 1, b, b + 1 < B)
    clear(nc, semaphores)


def phase_b(nc, io, scratch):
    semaphores = []
    with ExitStack() as ctx:
        def sb(name, shape, dt=F32):
            return ctx.enter_context(nc.sbuf_tensor("b_" + name, shape, dt))

        def sig(name, *args, **kw):
            semaphores.append(nc.alloc_semaphore(name="b_" + name))
            return Signal(semaphores[-1], *args, **kw)

        wk_hi = sb("wk_hi", [P, O // M, M, C], F32R)
        wk_lo = sb("wk_lo", [P, O // M, M, C], F32R)
        wv_hi = sb("wv_hi", [P, O, C], F32R)
        wv_lo = sb("wv_lo", [P, O, C], F32R)
        ones = sb("ones", [P, P])
        half_neg = sb("half_neg", [P, T])
        raw = sb("raw", [P, M, N])
        in_hi = sb("in_hi", [P, M, N], F32R)
        in_lo = sb("in_lo", [P, M, N], F32R)
        relu = sb("relu", [P, 2, N])
        sq = sb("sq", [P, 2, N])
        sq_hi = sb("sq_hi", [P, 4, N], F32R)
        sq_lo = sb("sq_lo", [P, 4, N], F32R)
        rc = sb("rc", [P, T, C])
        xs = sb("xs", [P, T, C])
        y = sb("y", [P, T, C])
        stats = sb("stats", [P, T, 6])
        mv = sb("mv", [P, T, 2])
        veps = sb("veps", [P, T])
        rstd = sb("rstd", [P, T])
        w2 = sb("w2", [P, 2, C])
        b1 = sb("b1", [P, B, O])
        b2 = sb("b2", [1, B, C])
        acc = sb("acc", [P, C])
        bias_row = sb("bias_row", [1, C])

        wide = [ctx.enter_context(nc.psum_tensor(f"b_wide{i}", [P, 512], F32)) for i in range(2)]
        back = [ctx.enter_context(nc.psum_tensor(f"b_back{i}", [P, 512], F32)) for i in range(T)]
        bias_sum = ctx.enter_context(nc.psum_tensor("b_bias_sum", [P, 512], F32))

        PIECES = 2 * O // M
        STAGES = (y, rc, xs)
        piece_in = [sig(f"piece_in{i}") for i in range(len(STAGES))]
        piece_hi = sig("piece_hi")
        piece_lo = sig("piece_lo")
        ones_ready = sig("ones_ready")
        half_ready = sig("half_ready")

        raw_in = [sig(f"raw_in{i}", 1, unit=16) for i in range(2)]
        in_hi_ready = sig("in_hi_ready", 2)
        in_lo_ready = sig("in_lo_ready", 2, places=2)
        wide_ready = sig("wide_ready", O)
        relu_done = sig("relu_done", O, places=2)
        sq_done = sig("sq_done", O, places=2)
        sq_hi_ready = sig("sq_hi_ready", O)
        sq_lo_ready = sig("sq_lo_ready", O)
        sq_used = sig("sq_used", O, places=4)
        back_ready = sig("back_ready", T)
        back_taken = sig("back_taken", T, places=T)
        rc_in = [sig(f"rc_in{t}", 1, unit=16) for t in range(T)]
        xs_in = [sig(f"xs_in{t}", 1, unit=16) for t in range(T)]
        tile_done = sig("tile_done", T, places=T)
        step = sig("step", 2)
        var_ready = sig("var_ready", 1)
        rstd_ready = sig("rstd_ready", 1)
        x2_ready = sig("x2_ready", 1)
        x2_stored = sig("x2_stored", 1, places=1, unit=16)
        b_in = [sig(f"b_in{b}", 2, unit=16, batches=1) for b in range(B)]
        w2_in = [sig(f"w2_in{i}", O // 2, unit=16) for i in range(2)]
        acc_step = sig("acc_step", O, places=2)
        bias_summed = sig("bias_summed", 1, places=1)
        bias_out = sig("bias_out", 1, places=1)
        bias_stored = sig("bias_stored", 1, places=1, unit=16)

        def w2_at(o):
            return 4 + o // 2

        AHEAD = 3

        def staged(i):
            j = i // 2
            if i % 2 == 0:
                hi, lo = wk_hi[:, j], wk_lo[:, j]
            else:
                hi, lo = wv_hi[:, j * M:(j + 1) * M], wv_lo[:, j * M:(j + 1) * M]
            return i % len(STAGES), hi, lo

        def periods(eng, period):
            with eng.Fori(0, Q - 1) as q:
                for b in range(B):
                    period(q, b, True)
            for b in range(B):
                period(Q - 1, b, b + 1 < B)

        block = ctx.enter_context(nc.Block())

        @block.sync
        def _(sp):
            def piece(i):
                stage, j = i % len(STAGES), i // 2
                if i >= len(STAGES):
                    sp.wait_ge(piece_lo.sem, i - len(STAGES) + 1)
                if i % 2 == 0:
                    src = io["wkc"][:, j * C:(j + 1) * C].rearrange("(m p) n -> p m n", p=P)
                else:
                    src = io["wvc"][j * M * P:(j + 1) * M * P].rearrange("(m p) n -> p m n", p=P)
                sp.dma_start(STAGES[stage][:], src).then_inc(piece_in[stage].sem, 16)

            piece(0)
            for hf in range(2):
                sp.dma_start(raw[:, hf * HB:(hf + 1) * HB], scratch["kc"][0, hf]).then_inc(raw_in[hf].sem, 16)
            for i in range(1, PIECES):
                piece(i)
            sp.wait_ge(piece_lo.sem, PIECES)
            with sp.Fori(0, Q) as q:
                for b in range(B):
                    g = q + b * Q
                    acc_step.place(sp, q, b, 2)
                    sp.dma_start(b1[:, b], io["b1"][b, q]).then_inc(b_in[b].sem, 16)
                    bias_summed.place(sp, q, b, 1)
                    sp.dma_start(b2[:, b], io["b2"][b, q]).then_inc(b_in[b].sem, 16)
                    for hf in range(2):
                        in_lo_ready.item(sp, q, b, hf + 1)
                        nxt = q + Q if b == 0 else q + 1
                        sp.dma_start(raw[:, hf * HB:(hf + 1) * HB], scratch["kc"][nxt, hf]
                                     ).then_inc(raw_in[hf].sem, 16)
                    for t in range(T):
                        tile_done.place(sp, q, b, t + 1)
                        sp.dma_start(rc[:, t], scratch["rc"][g, t]).then_inc(rc_in[t].sem, 16)
                        sp.dma_start(xs[:, t], scratch["xs"][g, :, t]).then_inc(xs_in[t].sem, 16)
                    for o in range(O):
                        acc_step.place(sp, q, b, o + 1)
                        sp.dma_start(w2[:, o % 2], io["w12"][b, q, o, 1]).then_inc(w2_in[o % 2].sem, 16)
                    x2_ready.item(sp, q, b, 1)
                    sp.dma_start(scratch["x2"][g], y[:]).then_inc(x2_stored.sem, 16)
            sp.wait_ge(x2_stored.sem, 16 * (1 + B * Q))
            for hf in range(2):
                sp.wait_ge(raw_in[hf].sem, 16 * (1 + B * Q))

        @block.tensor
        def _(pe):
            for s in (sq_used, bias_summed):
                s.give_places(pe)
            pe.wait_ge(ones_ready.sem, 1)
            with pe.Fori(0, Q) as q:
                for b in range(B):
                    def widen(o):
                        if o % M == 0:
                            pe.wait_ge(piece_lo.sem, 2 * (o // M) + 1)
                        relu_done.place(pe, q, b, o + 1)
                        for m in range(M):
                            if o == 0 and m % HB == 0:
                                in_lo_ready.item(pe, q, b, m // HB + 1)
                            part = slice((o % M) * P, (o % M + 1) * P)
                            last = split_product(nc, wide[o % 2][:],
                                                 (wk_hi[:, o // M, m, part], wk_lo[:, o // M, m, part]),
                                                 (in_hi[:, m], in_lo[:, m]), m == 0, m == M - 1)
                        last.then_inc(wide_ready.sem, 1)

                    def narrow(o):
                        if o % M == 0:
                            pe.wait_ge(piece_lo.sem, 2 * (o // M) + 2)
                        sq_lo_ready.item(pe, q, b, o + 1)
                        for t in range(T):
                            if o == 0:
                                back_taken.place(pe, q, b, t + 1)
                            part = slice(t * P, (t + 1) * P)
                            last = split_product(nc, back[t][:],
                                                 (sq_hi[:, o % 4, part], sq_lo[:, o % 4, part]),
                                                 (wv_hi[:, o], wv_lo[:, o]), o == 0, o == O - 1)
                            if o == O - 1:
                                last.then_inc(back_ready.sem, 1)
                        if o == O - 1:
                            pe.drain().then_inc(sq_used.sem, 1)
                        else:
                            last.then_inc(sq_used.sem, 1)

                    for o in range(O):
                        widen(o)
                        if o >= 2:
                            narrow(o - 2)
                        if o == 14:
                            acc_step.item(pe, q, b, O)
                            b_in[b].item(pe, q, 0, 2)
                            bias_out.place(pe, q, b, 1)
                            nc.tensor.matmul(bias_sum[:], ones[:], acc[:], start=True, stop=False)
                            nc.tensor.matmul(bias_sum[:], ones[0:1, :], b2[:, b], start=False, stop=True
                                             ).then_inc(bias_summed.sem, 1)
                    narrow(O - 2)
                    narrow(O - 1)

        @block.scalar
        def _(act):
            for s in (relu_done, bias_out, bias_stored):
                s.give_places(act)

            def split_input(q, b):
                for hf in range(2):
                    mine = slice(hf * HB, (hf + 1) * HB)
                    raw_in[hf].item(act, q, b, 1)
                    nc.scalar.copy(in_hi[:, mine], raw[:, mine]).then_inc(in_hi_ready.sem, 1)

            for i in range(PIECES):
                stage, to, _ = staged(i)
                act.wait_ge(piece_in[stage].sem, 16 * (i // len(STAGES) + 1))
                nc.scalar.copy(to, STAGES[stage][:]).then_inc(piece_hi.sem, 1)
                if i == 1:
                    split_input(0, 0)

            def period(q, b, more):
                for o in range(O):
                    wide_ready.item(act, q, b, o + 1)
                    sq_done.place(act, q, b, o + 1)
                    nc.scalar.activation(relu[:, o % 2], wide[o % 2][:], ACT.Relu).then_inc(relu_done.sem, 1)
                    relu_done.item(act, q, b, o + 1)
                    sq_used.place(act, q, b, o + 1)
                    nc.scalar.activation(sq_hi[:, o % 4], relu[:, o % 2], ACT.Square
                                         ).then_inc(sq_hi_ready.sem, 1)
                if more:
                    split_input(q, b + 1)
                bias_summed.item(act, q, b, 1)
                bias_stored.place(act, q, b, 1)
                nc.scalar.copy(bias_row[:], bias_sum[0:1, :]).then_inc(bias_out.sem, 1)
                bias_out.item(act, q, b, 1)
                act.dma_start(scratch["bias"][q + b * Q], bias_row[:]).then_inc(bias_stored.sem, 16)

            periods(act, period)
            act.wait_ge(bias_stored.sem, 16 * (1 + B * Q))

        @block.gpsimd
        def _(pool):
            in_lo_ready.give_places(pool)
            nc.gpsimd.memset(half_neg[:], -0.5).then_inc(half_ready.sem, 1)
            pool.wait_ge(half_ready.sem, 1)

            def split_input(q, b):
                for hf in range(2):
                    mine = slice(hf * HB, (hf + 1) * HB)
                    in_hi_ready.item(pool, q, b, hf + 1)
                    nc.gpsimd.tensor_tensor(in_lo[:, mine], raw[:, mine], in_hi[:, mine].bitcast(F32),
                                            ALU.subtract).then_inc(in_lo_ready.sem, 1)

            def period(q, b, more):
                if more:
                    split_input(q, b + 1)
                var_ready.item(pool, q, b, 1)
                nc.gpsimd.tensor_tensor(rstd[:], veps[:], half_neg[:], ALU.pow).then_inc(rstd_ready.sem, 1)

            split_input(0, 0)
            periods(pool, period)

        @block.vector
        def _(dve):
            nc.vector.memset(ones[:], 1.0).then_inc(ones_ready.sem, 1)
            for i in range(PIECES):
                stage, hi, lo = staged(i)
                dve.wait_ge(piece_hi.sem, i + 1)
                dve.wait_ge(piece_in[stage].sem, 16 * (i // len(STAGES) + 1))
                nc.vector.tensor_tensor(lo, STAGES[stage][:], hi.bitcast(F32), ALU.subtract
                                        ).then_inc(piece_lo.sem, 1)
            for s in (sq_done, back_taken, tile_done, acc_step):
                s.give_places(dve)
            dve.wait_ge(piece_lo.sem, PIECES)
            x2_stored.give_places(dve)

            def square(q, b, o):
                relu_done.item(dve, q, b, o + 1)
                if o >= 2:
                    sq_lo_ready.item(dve, q, b, o - 1)
                nc.vector.tensor_tensor(sq[:, o % 2], relu[:, o % 2], relu[:, o % 2], ALU.mult
                                        ).then_inc(sq_done.sem, 1)
                for w in range(O):
                    if w2_at(w) != o:
                        continue
                    w2_in[w % 2].item(dve, q, b, w // 2 + 1)
                    column = b1[:, b, w:w + 1]
                    if w == 0:
                        b_in[b].item(dve, q, 0, 2)
                        bias_summed.place(dve, q, b, 1)
                        nc.vector.tensor_scalar(acc[:], w2[:, 0], column, None, ALU.mult
                                                ).then_inc(acc_step.sem, 1)
                    else:
                        acc_step.item(dve, q, b, w)
                        nc.vector.scalar_tensor_tensor(acc[:], w2[:, w % 2], column, acc[:],
                                                       ALU.mult, ALU.add).then_inc(acc_step.sem, 1)
                sq_done.item(dve, q, b, o + 1)
                sq_hi_ready.item(dve, q, b, o + 1)
                nc.vector.tensor_tensor(sq_lo[:, o % 4], sq[:, o % 2], sq_hi[:, o % 4].bitcast(F32),
                                        ALU.subtract).then_inc(sq_lo_ready.sem, 1)

            for o in range(AHEAD):
                square(0, 0, o)

            def period(q, b, more):
                for o in range(AHEAD, O):
                    square(q, b, o)
                x2_stored.place(dve, q, b, 1)
                for t in range(T + 1):
                    if t < T:
                        back_ready.item(dve, q, b, t + 1)
                        rc_in[t].item(dve, q, b, 1)
                        nc.vector.tensor_tensor(y[:, t], rc[:, t], back[t][:], ALU.mult
                                                ).then_inc(back_taken.sem, 1)
                    if t >= 1:
                        back_taken.item(dve, q, b, t)
                        xs_in[t - 1].item(dve, q, b, 1)
                        nc.vector.tensor_tensor(y[:, t - 1], y[:, t - 1], xs[:, t - 1], ALU.add
                                                ).then_inc(tile_done.sem, 1)
                if more:
                    square(q, b + 1, 0)
                    square(q, b + 1, 1)
                for t in range(T):
                    tile_done.item(dve, q, b, t + 1)
                    ins = nc.vector.bn_stats(stats[:, t], y[:, t])
                ins.then_inc(step.sem, 1)
                step.item(dve, q, b, 1)
                nc.vector.memset(veps[:], LN_EPS)
                for t in range(T):
                    ins = nc.vector.bn_aggr(mv[:, t], stats[:, t])
                ins.then_inc(step.sem, 1)
                step.item(dve, q, b, 2)
                nc.vector.tensor_tensor(veps[:], mv[:, :, 1], veps[:], ALU.add).then_inc(var_ready.sem, 1)
                for o in range(2, AHEAD):
                    if more:
                        square(q, b + 1, o)
                rstd_ready.item(dve, q, b, 1)
                for t in range(T):
                    ins = nc.vector.tensor_scalar(y[:, t], y[:, t], mv[:, t, 0:1], rstd[:, t:t + 1],
                                                  ALU.subtract, ALU.mult)
                ins.then_inc(x2_ready.sem, 1)

            periods(dve, period)
    clear(nc, semaphores)


def phase_c(nc, io, scratch, out):
    semaphores = []
    with ExitStack() as ctx:
        def sb(name, shape, dt=F32):
            return ctx.enter_context(nc.sbuf_tensor("c_" + name, shape, dt))

        def sig(name, *args, **kw):
            semaphores.append(nc.alloc_semaphore(name="c_" + name))
            return Signal(semaphores[-1], *args, **kw)

        G = M
        PG = 2
        STEPS = T * G // PG
        PH = PG * HG
        ROWS = [min(P, GK - j * P) for j in range(KC)]

        wq_hi, wq_lo = sb("wq_hi", [P, M, C], F32R), sb("wq_lo", [P, M, C], F32R)
        wo_hi, wo_lo = sb("wo_hi", [P, M, C], F32R), sb("wo_lo", [P, M, C], F32R)
        kd_hi, kd_lo = sb("kd_hi", [P, B, G, GK], F32R), sb("kd_lo", [P, B, G, GK], F32R)
        vd_hi, vd_lo = sb("vd_hi", [P, B, G, KC, P], F32R), sb("vd_lo", [P, B, G, KC, P], F32R)
        cols = sb("cols", [P, len(COLS) * M])
        ident = sb("ident", [P, P])
        half_neg = sb("half_neg", [P, T])
        bo = sb("bo", [P, C])

        def col(name, m):
            i = COLS.index(name) * M + m
            return cols[:, i:i + 1]

        x2 = sb("x2", [P, B, T, C])
        xt_hi, xt_lo = sb("xt_hi", [P, M, N], F32R), sb("xt_lo", [P, M, N], F32R)
        qt_hi, qt_lo = sb("qt_hi", [P, M, N], F32R), sb("qt_lo", [P, M, N], F32R)
        ot_hi, ot_lo = sb("ot_hi", [P, M, N], F32R), sb("ot_lo", [P, M, N], F32R)
        vd_raw = nc.alloc_sbuf_tensor_at("c_vd_raw", [P, B, G, KC, P], F32, offset=nc.sbuf_base - 2 * 4 * M * N)
        pr = sb("pr", [P, B, T, HEADS * KEYS])
        SLOTS = 3
        pt_hi, pt_lo = sb("pt_hi", [P, SLOTS, N], F32R), sb("pt_lo", [P, SLOTS, N], F32R)
        most = sb("most", [P, 2, PG, HG])
        total = sb("total", [P, 2, PH])
        share = sb("share", [P, 2, PH])
        x3 = sb("x3", [P, T, C])
        wc = sb("wc", [P, 2, C])
        wc_hi, wc_lo = sb("wc_hi", [P, M, C], F32R), sb("wc_lo", [P, M, C], F32R)
        bias = sb("bias", [P, C])
        stats = sb("stats", [P, T, 6])
        mv = sb("mv", [P, T, 2])
        veps = sb("veps", [P, T])
        rstd = sb("rstd", [P, T])

        ring = [ctx.enter_context(nc.psum_tensor(f"c_ring{i}", [P, 512], F32)) for i in range(4)]
        sc = [ctx.enter_context(nc.psum_tensor(f"c_sc{i}", [P, PG, 512], F32)) for i in range(2)]

        spare = pr[:].rearrange("p b t k -> p (b t k)")
        KD = B * G * GK
        W = M * C
        wq_raw = x3[:]
        wk_raw = spare[:, 0:W].rearrange("p (m c) -> p m c", m=M)
        wv_raw = spare[:, W:2 * W].rearrange("p (m c) -> p m c", m=M)
        wo_raw = spare[:, 2 * W:3 * W].rearrange("p (m c) -> p m c", m=M)
        kd_raw = spare[:, 3 * W:3 * W + KD].rearrange("p (b g k) -> p b g k", b=B, g=G)
        context = spare[:, 3 * W + KD:3 * W + KD + M * B * KEYS].rearrange("p (m k) -> p m k", m=M)
        bv = bias
        values = wc[0:KEYS]

        s_consts = sig("s_consts")
        s_context = sig("s_context")
        s_kv_raw = sig("s_kv_raw")
        s_q_raw = sig("s_q_raw")
        s_o_raw = sig("s_o_raw")
        s_kd_zero = sig("s_kd_zero")
        s_vd_zero = sig("s_vd_zero")
        s_keys = sig("s_keys")
        s_keys_taken = sig("s_keys_taken")
        s_values = sig("s_values")
        s_values_taken = sig("s_values_taken")
        s_values_out = sig("s_values_out")
        s_vd_in = sig("s_vd_in")
        s_hi = sig("s_hi")
        s_lo = sig("s_lo")
        s_half = sig("s_half")

        x2_in = [sig(f"x2_in{b}", 1, unit=16, batches=1) for b in range(B)]
        wc_in = [sig(f"wc_in{i}", M // 2, unit=16) for i in range(2)]
        bias_in = sig("bias_in", 1, unit=16)
        wc_hi_ready = sig("wc_hi_ready", M)
        wc_lo_ready = sig("wc_lo_ready", M, places=2)
        xt_ready = sig("xt_ready", M)
        xt_hi_ready = sig("xt_hi_ready", M)
        xt_taken = sig("xt_taken", M)
        q_ready = sig("q_ready", M)
        q_hi_ready = sig("q_hi_ready", M)
        q_taken = sig("q_taken", M)
        sc_ready = sig("sc_ready", STEPS)
        sc_taken = sig("sc_taken", STEPS, places=2)
        most_ready = sig("most_ready", STEPS)
        exp_done = sig("exp_done", STEPS)
        total_ready = sig("total_ready", STEPS)
        share_ready = sig("share_ready", STEPS)
        pr_ready = sig("pr_ready", STEPS, places=2)
        pt_ready = sig("pt_ready", G * KC)
        pt_hi_ready = sig("pt_hi_ready", G * KC)
        pt_taken = sig("pt_taken", G * KC)
        pt_used = sig("pt_used", G * KC, places=SLOTS)
        o_ready = sig("o_ready", G)
        o_hi_ready = sig("o_hi_ready", G)
        o_taken = sig("o_taken", G)
        x2_read = sig("x2_read", 1)
        bo_added = sig("bo_added", 1)
        proj_ready = sig("proj_ready", T, places=T)
        proj_taken = sig("proj_taken", T)
        step = sig("step", 4)
        var_ready = sig("var_ready", 2)
        rstd_ready = sig("rstd_ready", 2)
        x3_ready = sig("x3_ready", 1)
        x3t_ready = sig("x3t_ready", M)
        x3t_hi_ready = sig("x3t_hi_ready", M)
        x3t_taken = sig("x3t_taken", M)
        bias_added = sig("bias_added", 1, places=1)
        ffn_ready = sig("ffn_ready", T, places=T)
        ffn_taken = sig("ffn_taken", T, places=T)
        y_ready = sig("y_ready", 1)
        y_stored = sig("y_stored", 1, places=1, unit=16)

        def segments():
            for head in range(HG):
                key = 0
                while key < KEYS:
                    chunk, row = divmod(head * KEYS + key, P)
                    count = min(KEYS - key, P - row)
                    yield head, key, chunk, row, count
                    key += count

        BESIDE_ATTENTION = {2: 0, 5: 1, 8: 2, 11: 3}
        AHEAD = 4
        LAG = 3

        block = ctx.enter_context(nc.Block())


        def periods(eng, period):
            with eng.Fori(0, Q - 1) as q:
                for b in range(B):
                    period(q, b, 2)
            for b in range(B):
                period(Q - 1, b, B - 1 - b)

        @block.sync
        def _(sp):
            def weight(to, name, signal):
                sp.dma_start(to, io[name].rearrange("(m p) n -> p m n", p=P)).then_inc(signal.sem, 16)

            sp.dma_start(x2[:, 0], scratch["x2"][0]).then_inc(x2_in[0].sem, 16)
            weight(wq_raw, "xwq", s_q_raw)
            for to, src in ((cols[:], io["cols"]), (ident[:], io["ident"])):
                sp.dma_start(to, src).then_inc(s_consts.sem, 16)
            sp.dma_start(context, io["ctx"].rearrange("(m p) k -> p m k", p=P)).then_inc(s_context.sem, 16)
            weight(wk_raw, "xwk", s_kv_raw)
            weight(wv_raw, "xwv", s_kv_raw)
            sp.dma_start(bv[:], io["bv"].to_broadcast([P, C])).then_inc(s_context.sem, 16)
            sp.dma_start(bo[:], io["bo"].to_broadcast([P, C])).then_inc(s_context.sem, 16)
            sp.dma_start(x2[:, 1], scratch["x2"][Q]).then_inc(x2_in[1].sem, 16)
            weight(wo_raw, "xwo", s_o_raw)
            sp.wait_ge(s_values_taken.sem, B)
            sp.dma_start(scratch["v"].rearrange("b k c -> k b c"), values).then_inc(s_values_out.sem, 16)
            sp.wait_ge(s_values_out.sem, 16)
            sp.wait_ge(s_vd_zero.sem, 1)
            for b in range(B):
                src = scratch["v"][b].rearrange("k (g h d) -> h k g d", g=G, h=HG)
                for head, key, chunk, row, count in segments():
                    sp.dma_start(vd_raw[row:row + count, b, :, chunk, head * HD:(head + 1) * HD],
                                 src[head, key:key + count]).then_inc(s_vd_in.sem, 16)

            def period(q, b, more):
                for m in range(M):
                    wc_lo_ready.place(sp, q, b, m + 1)
                    sp.dma_start(wc[:, m % 2], scratch["wc"][q + b * Q, m]).then_inc(wc_in[m % 2].sem, 16)
                bias_added.place(sp, q, b, 1)
                sp.dma_start(bias[:], scratch["bias"][q + b * Q].to_broadcast([P, C])).then_inc(bias_in.sem, 16)
                if more > 1:
                    x2_read.item(sp, q, b, 1)
                    sp.dma_start(x2[:, b], scratch["x2"][q + (b * Q + 1)]).then_inc(x2_in[b].sem, 16)
                y_ready.item(sp, q, b, 1)
                sp.dma_start(out[b, q].rearrange("(t p) c -> p t c", p=P), x3[:]).then_inc(y_stored.sem, 16)

            periods(sp, period)
            sp.wait_ge(y_stored.sem, 16 * (1 + B * Q))

        @block.tensor
        def _(pe):
            def transposes(source, ready, free):
                for m in range(M):
                    free(m)
                    for t in range(T):
                        last = nc.tensor.transpose(ring[m][:, t * P:(t + 1) * P],
                                                   source[:, t, m * P:(m + 1) * P], ident[:])
                    last.then_inc(ready.sem, 1)

            def by_tokens(t, source, weight, ready, block_ready):
                (s_hi, s_lo), (w_hi, w_lo) = source, weight
                part = slice(t * P, (t + 1) * P)
                for m in range(M):
                    if t == 0:
                        block_ready(m)
                    last = split_product(nc, ring[t][:], (s_hi[:, m, part], s_lo[:, m, part]),
                                         (w_hi[:, m], w_lo[:, m]), m == 0, m == M - 1)
                last.then_inc(ready.sem, 1)

            def queries(q, b):
                for g in range(M):
                    part = slice(g * P, (g + 1) * P)
                    for m in range(M):
                        xt_taken.item(pe, q, b, max(g, m) + 1)
                        last = split_product(nc, ring[g][:], (wq_hi[:, m, part], wq_lo[:, m, part]),
                                             (xt_hi[:, m], xt_lo[:, m]), m == 0, m == M - 1)
                    last.then_inc(q_ready.sem, 1)

            def scores(q, b, i):
                t, pair = divmod(i, G // PG)
                sc_taken.place(pe, q, b, i + 1)
                for gg in range(PG):
                    g = pair * PG + gg
                    if t == 0:
                        q_taken.item(pe, q, b, g + 1)
                    part = slice(t * P, (t + 1) * P)
                    last = split_product(nc, sc[i % 2][:, gg, 0:GK], (qt_hi[:, g, part], qt_lo[:, g, part]),
                                         (kd_hi[:, b % B, g], kd_lo[:, b % B, g]), True, True)
                last.then_inc(sc_ready.sem, 1)

            pe.wait_ge(s_consts.sem, 16 * 2)
            x2_in[0].item(pe, 0, 0, 1)
            transposes(x2[:, 0], xt_ready, lambda m: None)
            pe.wait_ge(s_lo.sem, 1)
            queries(0, 0)
            pe.wait_ge(s_context.sem, 16)
            pe.wait_ge(s_kv_raw.sem, 32)
            for g in range(G):
                q_taken.item(pe, 0, 0, g + 1)
                for m in range(M):
                    last = nc.tensor.matmul(ring[g][:, 0:B * KEYS], wk_raw[:, m, g * P:(g + 1) * P],
                                            context[:, m], start=m == 0, stop=m == M - 1)
                last.then_inc(s_keys.sem, 1)
            for b in range(B):
                for m in range(M):
                    last = nc.tensor.matmul(sc[0][0:KEYS, b], context[:, m, b * KEYS:(b + 1) * KEYS],
                                            wv_raw[:, m], start=m == 0, stop=m == M - 1)
                last.then_inc(s_values.sem, 1)
            for s in (pt_used, ffn_ready, proj_ready):
                s.give_places(pe)
            x2_in[1].item(pe, 0, 0, 1)
            pe.wait_ge(s_keys_taken.sem, 1)
            transposes(x2[:, 1], xt_ready, lambda m: None)
            pe.wait_ge(s_values_taken.sem, B)
            pe.wait_ge(s_lo.sem, 2)
            for i in range(STEPS):
                scores(0, 0, i)
            queries(0, 1)
            pe.wait_ge(s_lo.sem, 4)

            def period(q, b, more):
                def attend(i):
                    g, j = divmod(i, KC)
                    pt_taken.item(pe, q, b, i + 1)
                    if j == 0:
                        if g == 0:
                            ffn_taken.place(pe, q, b, T)
                        else:
                            o_taken.item(pe, q, b, g)
                    rows, s = ROWS[j], i % SLOTS
                    last = split_product(nc, ring[3][:], (vd_hi[0:rows, b, g, j], vd_lo[0:rows, b, g, j]),
                                         (pt_hi[0:rows, s], pt_lo[0:rows, s]), j == 0, j == KC - 1)
                    if j == KC - 1:
                        last.then_inc(o_ready.sem, 1)
                        pe.drain().then_inc(pt_used.sem, 1)
                    else:
                        last.then_inc(pt_used.sem, 1)

                pr_ready.item(pe, q, b, STEPS)
                for i in range(G * KC + LAG):
                    if i < G * KC:
                        g, j = divmod(i, KC)
                        if i == 0:
                            ffn_taken.place(pe, q, b, 1)
                            if more < 2:
                                q_taken.item(pe, q, b + more, M)
                        elif i == 1:
                            ffn_taken.place(pe, q, b, KC)
                        elif g > 0:
                            pt_taken.item(pe, q, b, i - KC + 1)
                    if i >= LAG:
                        attend(i - LAG)
                    if i < G * KC:
                        for t in range(T):
                            last = nc.tensor.transpose(
                                ring[j][0:ROWS[j], t * P:(t + 1) * P],
                                pr[:, b, t, g * GK + j * P:g * GK + j * P + ROWS[j]], ident[:])
                        last.then_inc(pt_ready.sem, 1)
                    if more and i in BESIDE_ATTENTION:
                        scores(q, b + 1, BESIDE_ATTENTION[i])
                for t in range(T):
                    if more:
                        scores(q, b + 1, STEPS - T + t)
                    if t == T - 1:
                        o_taken.item(pe, q, b, G)
                    by_tokens(t, (ot_hi, ot_lo), (wo_hi, wo_lo), proj_ready,
                              lambda g: o_taken.item(pe, q, b, g + 1))
                if more > 1:
                    x2_in[b].item(pe, q, 0, 2)
                    transposes(x2[:, b], xt_ready, lambda m: proj_taken.item(pe, q, b, m + 1))
                    queries(q, b + 2)
                x3_ready.item(pe, q, b, 1)
                transposes(x3, x3t_ready, (lambda m: q_taken.item(pe, q, b + 2, m + 1)) if more > 1
                           else (lambda m: proj_taken.item(pe, q, b, m + 1)))
                wc_lo_ready.item(pe, q, b, M)
                for t in range(T):
                    x3t_taken.item(pe, q, b, t + 1)
                    by_tokens(t, (xt_hi, xt_lo), (wc_hi, wc_lo), ffn_ready,
                              lambda m: x3t_taken.item(pe, q, b, m + 1))

            periods(pe, period)

        @block.scalar
        def _(act):
            def high(q, b, ready, done):
                for m in range(M):
                    ready.item(act, q, b, m + 1)
                    nc.scalar.copy(xt_hi[:, m], ring[m][:]).then_inc(done.sem, 1)

            def high_queries(q, b):
                for g in range(M):
                    q_ready.item(act, q, b, g + 1)
                    nc.scalar.activation(qt_hi[:, g], ring[g][:], ACT.Identity, bias=col("bq", g)
                                         ).then_inc(q_hi_ready.sem, 1)

            def exponential(q, b, i):
                t, pair = divmod(i, G // PG)
                sc_taken.item(act, q, b, i + 1)
                span = pr[:, b % B, t, pair * PH * KEYS:(pair + 1) * PH * KEYS]
                nc.scalar.activation(span, span, ACT.Exp).then_inc(exp_done.sem, 1)

            act.wait_ge(s_q_raw.sem, 16)
            nc.scalar.copy(wq_hi[:], wq_raw).then_inc(s_hi.sem, 1)
            act.wait_ge(s_consts.sem, 16 * 2)
            high(0, 0, xt_ready, xt_hi_ready)
            high_queries(0, 0)
            act.wait_ge(s_kd_zero.sem, 1)
            for g in range(G):
                act.wait_ge(s_keys.sem, g + 1)
                for head in range(HG):
                    mine = slice(head * HD, (head + 1) * HD)
                    ins = nc.scalar.activation(
                        kd_raw[mine, :, g, head * KEYS:(head + 1) * KEYS],
                        ring[g][mine, 0:B * KEYS].rearrange("p (b k) -> p b k", b=B), ACT.Identity,
                        bias=col("bk", g)[mine])
            ins.then_inc(s_keys_taken.sem, 1)
            act.wait_ge(s_keys_taken.sem, 1)
            nc.scalar.copy(kd_hi[:], kd_raw).then_inc(s_hi.sem, 1)
            act.wait_ge(s_o_raw.sem, 16)
            nc.scalar.copy(wo_hi[:], wo_raw).then_inc(s_hi.sem, 1)
            high(0, 1, xt_ready, xt_hi_ready)
            act.wait_ge(s_lo.sem, 3)
            for i in range(STEPS):
                exponential(0, 0, i)
            act.wait_ge(s_vd_in.sem, 16 * B * len(list(segments())))
            nc.scalar.copy(vd_hi[:], vd_raw[:]).then_inc(s_hi.sem, 1)
            high_queries(0, 1)

            def period(q, b, more):
                def high_output(g):
                    o_ready.item(act, q, b, g + 1)
                    if g == 0:
                        proj_ready.place(act, q, b, T)
                    nc.scalar.copy(ot_hi[:, g], ring[3][:]).then_inc(o_hi_ready.sem, 1)

                def high_weights(m):
                    if m == 0:
                        ffn_ready.place(act, q, b, T)
                    wc_in[m % 2].item(act, q, b, m // 2 + 1)
                    nc.scalar.copy(wc_hi[:, m], wc[:, m % 2]).then_inc(wc_hi_ready.sem, 1)

                for i in range(G * KC + LAG):
                    if i < G * KC:
                        g, j = divmod(i, KC)
                        pt_ready.item(act, q, b, i + 1)
                        pt_used.place(act, q, b, i + 1)
                        rows = slice(0, ROWS[j])
                        nc.scalar.copy(pt_hi[rows, i % SLOTS], ring[j][rows, :]).then_inc(pt_hi_ready.sem, 1)
                        if j == KC - 1 and g >= 1:
                            high_output(g - 1)
                    if more and i - 1 in BESIDE_ATTENTION:
                        exponential(q, b + 1, BESIDE_ATTENTION[i - 1])
                    if i in (9, 10):
                        high_weights(i - 9)
                high_output(G - 1)
                for i in range(T - 1):
                    if more:
                        exponential(q, b + 1, STEPS - T + i)
                    if i in (1, 2):
                        high_weights(i + 1)
                if more > 1:
                    high(q, b + 2, xt_ready, xt_hi_ready)
                if more:
                    exponential(q, b + 1, STEPS - 1)
                if more > 1:
                    sc_ready.item(act, q, b + 1, STEPS)
                    high_queries(q, b + 2)
                high(q, b, x3t_ready, x3t_hi_ready)

            periods(act, period)

        @block.gpsimd
        def _(pool):
            nc.gpsimd.memset(kd_raw, 0.0).then_inc(s_kd_zero.sem, 1)
            nc.gpsimd.memset(vd_raw[:], 0.0).then_inc(s_vd_zero.sem, 1)
            nc.gpsimd.memset(half_neg[:], -0.5).then_inc(s_half.sem, 1)
            pool.wait_ge(s_values_out.sem, 16)
            pr_ready.give_places(pool)
            wc_lo_ready.give_places(pool)
            bias_added.give_places(pool)
            pool.wait_ge(s_half.sem, 1)
            pool.wait_ge(s_context.sem, 16 * 3)
            pool.wait_ge(s_lo.sem, 1)

            def normalize(q, b, i):
                t, pair = divmod(i, G // PG)
                span = pr[:, b % B, t, pair * PH * KEYS:(pair + 1) * PH * KEYS].rearrange("p (h k) -> p h k", k=KEYS)
                share_ready.item(pool, q, b, i + 1)
                nc.gpsimd.tensor_tensor(span, span, share[:, i % 2].unsqueeze(2).to_broadcast([P, PH, KEYS]),
                                        ALU.mult).then_inc(pr_ready.sem, 1)

            for i in range(STEPS):
                normalize(0, 0, i)

            def period(q, b, more):
                def normalize_next(*steps):
                    for i in steps:
                        if more:
                            normalize(q, b + 1, i)

                def weights_low(m):
                    wc_hi_ready.item(pool, q, b, m + 1)
                    nc.gpsimd.tensor_tensor(wc_lo[:, m], wc[:, m % 2], wc_hi[:, m].bitcast(F32), ALU.subtract
                                            ).then_inc(wc_lo_ready.sem, 1)

                y_stored.place(pool, q, b, 1)
                xt_ready.item(pool, q, b, M)
                nc.gpsimd.tensor_tensor(x3[:], x2[:, b], bo[:].unsqueeze(1).to_broadcast([P, T, C]),
                                        ALU.add).then_inc(bo_added.sem, 1)
                pool.drain().then_inc(x2_read.sem, 1)
                normalize_next(0, 1, 2)
                weights_low(0)
                weights_low(1)
                normalize_next(3, 4)
                weights_low(2)
                normalize_next(5)
                weights_low(3)
                normalize_next(6)
                var_ready.item(pool, q, b, 1)
                nc.gpsimd.tensor_tensor(rstd[:], veps[:], half_neg[:], ALU.pow).then_inc(rstd_ready.sem, 1)
                normalize_next(7)
                bias_in.item(pool, q, b, 1)
                x3t_ready.item(pool, q, b, M)
                nc.gpsimd.tensor_tensor(x3[:], x3[:], bias[:].unsqueeze(1).to_broadcast([P, T, C]),
                                        ALU.add).then_inc(bias_added.sem, 1)
                var_ready.item(pool, q, b, 2)
                nc.gpsimd.tensor_tensor(rstd[:], veps[:], half_neg[:], ALU.pow).then_inc(rstd_ready.sem, 1)

            periods(pool, period)

        @block.vector
        def _(dve):
            def low(q, b, hi_ready, taken):
                for m in range(M):
                    hi_ready.item(dve, q, b, m + 1)
                    nc.vector.tensor_tensor(xt_lo[:, m], ring[m][:], xt_hi[:, m].bitcast(F32), ALU.subtract
                                            ).then_inc(taken.sem, 1)

            def low_queries(q, b):
                for g in range(M):
                    q_hi_ready.item(dve, q, b, g + 1)
                    nc.vector.scalar_tensor_tensor(qt_lo[:, g], ring[g][:], col("bq", g),
                                                   qt_hi[:, g].bitcast(F32), ALU.add, ALU.subtract
                                                   ).then_inc(q_taken.sem, 1)

            def split_low(i):
                raw, hi, lo = ((wq_raw, wq_hi, wq_lo), (kd_raw, kd_hi, kd_lo), (wo_raw, wo_hi, wo_lo),
                               (vd_raw[:], vd_hi, vd_lo))[i]
                dve.wait_ge(s_hi.sem, i + 1)
                nc.vector.tensor_tensor(lo[:], raw, hi[:].bitcast(F32), ALU.subtract).then_inc(s_lo.sem, 1)

            def heads(ap):
                return ap.rearrange("p g (h k) -> p g h k", k=KEYS)

            def softmax_front(q, b, i):
                t, pair = divmod(i, G // PG)
                s = i % 2
                sc_ready.item(dve, q, b, i + 1)
                scores = heads(sc[s][:, :, 0:GK])
                nc.vector.tensor_reduce(most[:, s], scores, AX_X, ALU.max).then_inc(most_ready.sem, 1)
                most_ready.item(dve, q, b, i + 1)
                span = pr[:, b % B, t, pair * PH * KEYS:(pair + 1) * PH * KEYS]
                nc.vector.tensor_tensor(span.rearrange("p (g h k) -> p g h k", g=PG, k=KEYS), scores,
                                        most[:, s].unsqueeze(3).to_broadcast([P, PG, HG, KEYS]),
                                        ALU.subtract).then_inc(sc_taken.sem, 1)

            def softmax_back(q, b, i):
                t, pair = divmod(i, G // PG)
                s = i % 2
                span = pr[:, b % B, t, pair * PH * KEYS:(pair + 1) * PH * KEYS].rearrange("p (h k) -> p h k", k=KEYS)
                exp_done.item(dve, q, b, i + 1)
                pr_ready.place(dve, q, b, i + 1)
                nc.vector.tensor_reduce(total[:, s], span, AX_X, ALU.add).then_inc(total_ready.sem, 1)
                total_ready.item(dve, q, b, i + 1)
                nc.vector.reciprocal(share[:, s], total[:, s]).then_inc(share_ready.sem, 1)

            def softmax_step(q, b, i):
                if i < STEPS:
                    softmax_front(q, b, i)
                if i >= 1:
                    softmax_back(q, b, i - 1)

            dve.wait_ge(s_q_raw.sem, 16)
            dve.wait_ge(s_consts.sem, 16 * 2)
            split_low(0)
            low(0, 0, xt_hi_ready, xt_taken)
            low_queries(0, 0)
            dve.wait_ge(s_context.sem, 16 * 3)
            for b in range(B):
                dve.wait_ge(s_values.sem, b + 1)
                nc.vector.tensor_tensor(values[:, b], sc[0][0:KEYS, b], bv[0:KEYS, :], ALU.add
                                        ).then_inc(s_values_taken.sem, 1)
            split_low(1)
            split_low(2)
            for s in (sc_taken, ffn_taken, y_stored):
                s.give_places(dve)
            low(0, 1, xt_hi_ready, xt_taken)
            dve.wait_ge(s_lo.sem, 3)
            for i in range(STEPS + 1):
                softmax_step(0, 0, i)
            low_queries(0, 1)
            split_low(3)

            def norm_front(q, b, taken, which):
                for t in range(T):
                    taken.item(dve, q, b, t + 1)
                    ins = nc.vector.bn_stats(stats[:, t], x3[:, t])
                ins.then_inc(step.sem, 1)
                step.item(dve, q, b, 2 * which + 1)
                nc.vector.memset(veps[:], LN_EPS)
                for t in range(T):
                    ins = nc.vector.bn_aggr(mv[:, t], stats[:, t])
                ins.then_inc(step.sem, 1)
                step.item(dve, q, b, 2 * which + 2)
                nc.vector.tensor_tensor(veps[:], mv[:, :, 1], veps[:], ALU.add).then_inc(var_ready.sem, 1)

            def norm_back(q, b, which, ready):
                rstd_ready.item(dve, q, b, which + 1)
                for t in range(T):
                    ins = nc.vector.tensor_scalar(x3[:, t], x3[:, t], mv[:, t, 0:1], rstd[:, t:t + 1],
                                                  ALU.subtract, ALU.mult)
                ins.then_inc(ready.sem, 1)

            def low_output(q, b, g):
                o_hi_ready.item(dve, q, b, g + 1)
                nc.vector.tensor_tensor(ot_lo[:, g], ring[3][:], ot_hi[:, g].bitcast(F32), ALU.subtract
                                        ).then_inc(o_taken.sem, 1)

            def attention(q, b, first, count, more):
                for i in range(first, first + count):
                    if i < G * KC:
                        g, j = divmod(i, KC)
                        rows = slice(0, ROWS[j])
                        pt_hi_ready.item(dve, q, b, i + 1)
                        nc.vector.tensor_tensor(pt_lo[rows, i % SLOTS], ring[j][rows, :],
                                                pt_hi[rows, i % SLOTS].bitcast(F32), ALU.subtract
                                                ).then_inc(pt_taken.sem, 1)
                        if j == KC - 1 and g >= 1:
                            low_output(q, b, g - 1)
                    if more and i in BESIDE_ATTENTION:
                        softmax_step(q, b + 1, BESIDE_ATTENTION[i])

            attention(0, 0, 0, AHEAD, True)

            def period(q, b, more):
                attention(q, b, AHEAD, G * KC + LAG - AHEAD, more)
                low_output(q, b, G - 1)
                bo_added.item(dve, q, b, 1)
                for t in range(T):
                    if more and t < T - 1:
                        softmax_step(q, b + 1, STEPS - T + t)
                    proj_ready.item(dve, q, b, t + 1)
                    nc.vector.tensor_tensor(x3[:, t], x3[:, t], ring[t][:], ALU.add).then_inc(proj_taken.sem, 1)
                if more > 1:
                    low(q, b + 2, xt_hi_ready, xt_taken)
                if more:
                    softmax_step(q, b + 1, STEPS - 1)
                norm_front(q, b, proj_taken, 0)
                if more:
                    softmax_step(q, b + 1, STEPS)
                norm_back(q, b, 0, x3_ready)
                if more > 1:
                    low_queries(q, b + 2)
                low(q, b, x3t_hi_ready, x3t_taken)
                bias_added.item(dve, q, b, 1)
                for t in range(T):
                    ffn_ready.item(dve, q, b, t + 1)
                    nc.vector.tensor_tensor(x3[:, t], x3[:, t], ring[t][:], ALU.add
                                            ).then_inc(ffn_taken.sem, 1)
                if more:
                    attention(q, b + 1, 0, 2, more > 1)
                norm_front(q, b, ffn_taken, 1)
                if more:
                    attention(q, b + 1, 2, AHEAD - 2, more > 1)
                norm_back(q, b, 1, y_ready)

            periods(dve, period)
    clear(nc, semaphores)


def build(nc, io, out):
    scratch = {
        "xs": nc.dram_tensor("xs_scratch", (B * Q, P, T, C), F32).ap(),
        "kc": nc.dram_tensor("kc_scratch", (B * Q, 2, P, HB, N), F32).ap(),
        "rc": nc.dram_tensor("rc_scratch", (B * Q, T, P, C), F32).ap(),
        "wc": nc.dram_tensor("wc_scratch", (B * Q, M, P, C), F32).ap(),
        "bias": nc.dram_tensor("bias_scratch", (B * Q, 1, C), F32).ap(),
        "x2": nc.dram_tensor("x2_scratch", (B * Q, P, T, C), F32).ap(),
        "v": nc.dram_tensor("v_scratch", (B, KEYS, C), F32).ap(),
    }
    phase_a(nc, io, scratch)
    phase_b(nc, io, scratch)
    phase_c(nc, io, scratch, out)


def kernel(**inputs):
    import numpy as np
    import concourse.bacc as bacc
    from concourse.bass_utils import run_bass_kernel_spmd

    a = {n: np.asarray(v) for n, v in inputs.items()}

    def turned(w):
        return np.ascontiguousarray(np.swapaxes(w, -1, -2))

    w1 = a["L0_ffn_W1"].reshape(B, Q, O, 1, P, C)
    w2t = turned(a["L0_ffn_W2"]).reshape(B, Q, O, 1, P, C)
    per_channel = [a["L0_attn_" + n] for n in ("ln1_g", "ln1_b", "ln2_g", "ln2_b", "mix_k", "mix_v", "mix_r",
                                               "cmix_k", "cmix_r", "time_first")]
    per_channel += [a["L0_xattn_bq"], a["L0_xattn_bk"]]
    arrays = {
        "x": a["x"].reshape(B, Q, N, C),
        "ctx": turned(a["ctx_1024"].reshape(B * KEYS, C)),
        "cols": np.concatenate([v.reshape(M, P).T for v in per_channel], axis=1),
        "ident": np.eye(P, dtype=np.float32),
        "wk": turned(a["L0_attn_Wk_t"]), "wv": turned(a["L0_attn_Wv_t"]), "wr": turned(a["L0_attn_Wr_t"]),
        "wrc": turned(a["L0_attn_Wr_c"]), "wkc": turned(a["L0_attn_Wk_c"]), "wvc": turned(a["L0_attn_Wv_c"]),
        "xwq": turned(a["L0_xattn_Wq"]), "xwk": turned(a["L0_xattn_Wk"]), "xwv": turned(a["L0_xattn_Wv"]),
        "xwo": turned(a["L0_xattn_Wo"]), "bv": a["L0_xattn_bv"].reshape(1, C), "bo": a["L0_xattn_bo"].reshape(1, C),
        "w12": np.concatenate([w1, w2t], axis=3),
        "b1": turned(a["L0_ffn_b1"].reshape(B, Q, O, P)), "b2": a["L0_ffn_b2"].reshape(B, Q, 1, C),
    }
    arrays = {n: np.ascontiguousarray(v) for n, v in arrays.items()}
    nc = bacc.Bacc("TRN2", target_bir_lowering=False, num_devices=1, dynamic_dma_scratch_size=1024)
    io = {n: nc.dram_tensor(n + "_dram", v.shape, F32, kind="ExternalInput").ap() for n, v in arrays.items()}
    out = nc.dram_tensor("out_dram", (B, Q, N, C), F32, kind="ExternalOutput").ap()
    build(nc, io, out)
    got = run_bass_kernel_spmd(nc, [{n + "_dram": v for n, v in arrays.items()}], core_ids=[0])
    return got.results[0]["out_dram"].reshape(B, Q * N, C)
```
